# Optimizing a Trainium2 kernel written in Bass

```python
import numpy as np
import jax
import jax.numpy as jnp

def _softmax(x, axis=-1):
    return jax.nn.softmax(x, axis=axis)
def _gelu(x):
    return jax.nn.gelu(x, approximate=True)
def _silu(x):
    return jax.nn.silu(x)
def _sigmoid(x):
    return jax.nn.sigmoid(x)
def _layernorm(x, axis=-1, eps=1e-5):
    m = jnp.mean(x, axis=axis, keepdims=True)
    v = jnp.var(x, axis=axis, keepdims=True)
    return (x - m) / jnp.sqrt(v + eps)
def _scatter_add(tgt, idx, src, axis=0):
    return tgt.at[idx].add(src)
def _segment_sum(src, seg, n):
    return jax.ops.segment_sum(src, seg, n)

kernel_name = 'mk_conv_preact_d2_conv_nchw768_9aa759'

def setup_inputs(seed: int = 0):
    np.random.seed(seed)
    _w = jnp.asarray
    def _rec_inputs():
        import jax
        import jax.numpy as jnp
        _gk = jax.random.key(seed)
        x = -0.0001538 + 1 * jax.random.normal(jax.random.fold_in(_gk, 1), (2, 768, 64, 64), jnp.float32)
        return x
    x = _rec_inputs()
    def _L0_conv_setup():
        import jax, jax.numpy as jnp
        import numpy as np
        B, DM, H, W = (2, 768, 64, 64)
        EXPAND, DSTATE, DCONV = (2, 4, 3)
        DI = DM * EXPAND
        R = DM // 16
        key = jax.random.key(seed)
        ks = jax.random.split(key, 8)
        s = 0.02
        dt = jnp.exp(jax.random.uniform(ks[5], (1, DI)) * (np.log(0.1) - np.log(0.001)) + np.log(0.001))
        dt = jnp.clip(dt, 0.0001)
        inv_dt = dt + jnp.log(-jnp.expm1(-dt))
        A_log = jnp.log(jnp.arange(1, DSTATE + 1, dtype=jnp.float32))
        A_log = jnp.broadcast_to(A_log[None, None, :], (1, DI, DSTATE))
        return {'hidden_states': jax.random.normal(ks[0], (B, DM, H, W), jnp.float32), 'in_proj_w': jax.random.normal(ks[1], (DI, DM), jnp.float32) * s, 'conv_w': jax.random.normal(ks[2], (DI, 1, DCONV, DCONV), jnp.float32) * s, 'conv_b': jnp.zeros((DI,), jnp.float32), 'x_proj_w': jax.random.normal(ks[3], (R + 2 * DSTATE, DI), jnp.float32) * s, 'dt_w': jax.random.uniform(ks[4], (1, DI, R), jnp.float32, -R ** (-0.5), R ** (-0.5)), 'dt_b': inv_dt, 'A_log': A_log, 'D_param': jnp.ones((1, DI), jnp.float32), 'ln_g': jnp.ones((DI,), jnp.float32), 'ln_b': jnp.zeros((DI,), jnp.float32), 'out_proj_w': jax.random.normal(ks[6], (DM, DI), jnp.float32) * s}
    _L0_conv_all = _L0_conv_setup()
    _L0_conv_in = {k: v for k, v in _L0_conv_all.items() if k in ('in_proj_w', 'conv_w', 'conv_b', 'x_proj_w', 'dt_w', 'dt_b', 'A_log', 'D_param', 'ln_g', 'ln_b', 'out_proj_w', )}
    del _L0_conv_all

    def _L1_conv_setup():
        import jax, jax.numpy as jnp
        import numpy as np
        NH = 32
        R = 4
        LMBD = 0.01
        SCALE = 0.02

        def softshrink(v, l):
            return jnp.where(v > l, v - l, jnp.where(v < -l, v + l, jnp.zeros((), v.dtype)))
        key = jax.random.key(seed)
        k0, k1, k2, k3, k4 = jax.random.split(key, 5)
        B, C, H, W = (4, 768, 128, 128)
        SH = C // NH
        x = jax.random.normal(k0, (B, C, H, W), jnp.float32)
        w1 = SCALE * jax.random.normal(k1, (2, NH, SH, R * SH), jnp.float32)
        b1 = SCALE * jax.random.normal(k2, (2, NH, R * SH), jnp.float32)
        w2 = SCALE * jax.random.normal(k3, (2, NH, R * SH, SH), jnp.float32)
        b2 = SCALE * jax.random.normal(k4, (2, NH, SH), jnp.float32)
        return {'x': x, 'w1': w1, 'b1': b1, 'w2': w2, 'b2': b2}
    _L1_conv_all = _L1_conv_setup()
    _L1_conv_in = {k: v for k, v in _L1_conv_all.items() if k in ('w1', 'b1', 'w2', 'b2', )}
    del _L1_conv_all

    return {
        "x": x,
        "L0_conv_in_proj_w": _L0_conv_in["in_proj_w"],
        "L0_conv_conv_w": _L0_conv_in["conv_w"],
        "L0_conv_conv_b": _L0_conv_in["conv_b"],
        "L0_conv_x_proj_w": _L0_conv_in["x_proj_w"],
        "L0_conv_dt_w": _L0_conv_in["dt_w"],
        "L0_conv_dt_b": _L0_conv_in["dt_b"],
        "L0_conv_A_log": _L0_conv_in["A_log"],
        "L0_conv_D_param": _L0_conv_in["D_param"],
        "L0_conv_ln_g": _L0_conv_in["ln_g"],
        "L0_conv_ln_b": _L0_conv_in["ln_b"],
        "L0_conv_out_proj_w": _L0_conv_in["out_proj_w"],
        "L1_conv_w1": _L1_conv_in["w1"],
        "L1_conv_b1": _L1_conv_in["b1"],
        "L1_conv_w2": _L1_conv_in["w2"],
        "L1_conv_b2": _L1_conv_in["b2"],
    }

def reference(x, L0_conv_in_proj_w, L0_conv_conv_w, L0_conv_conv_b, L0_conv_x_proj_w, L0_conv_dt_w, L0_conv_dt_b, L0_conv_A_log, L0_conv_D_param, L0_conv_ln_g, L0_conv_ln_b, L0_conv_out_proj_w, L1_conv_w1, L1_conv_b1, L1_conv_w2, L1_conv_b2):
    import jax
    import jax.numpy as jnp
    def _L0_conv_ref(hidden_states, in_proj_w, conv_w, conv_b, x_proj_w, dt_w, dt_b, A_log, D_param, ln_g, ln_b, out_proj_w):
        import jax, jax.numpy as jnp
        import numpy as np
        B, DM, H, W = (2, 768, 64, 64)
        EXPAND, DSTATE, DCONV = (2, 4, 3)
        DI = DM * EXPAND
        R = DM // 16
        b, dm, h, w = hidden_states.shape
        L = h * w
        hs = jnp.transpose(hidden_states, (0, 2, 3, 1))
        x = hs @ in_proj_w.T
        xs = jnp.transpose(x, (0, 3, 1, 2))
        pad = (DCONV - 1) // 2
        xs = jax.lax.conv_general_dilated(xs, conv_w, (1, 1), ((pad, pad), (pad, pad)), feature_group_count=xs.shape[1], dimension_numbers=('NCHW', 'OIHW', 'NCHW')) + conv_b[None, :, None, None]
        xs = xs * jax.nn.sigmoid(xs)
        xs_seq = jnp.transpose(xs, (0, 2, 3, 1)).reshape(b, L, -1)
        x_dbl = xs_seq @ x_proj_w.T
        dt, Bs, Cs = jnp.split(x_dbl, [R, R + DSTATE], axis=-1)
        delta = jnp.einsum('blr,dr->bdl', dt, dt_w[0])
        delta = jax.nn.softplus(delta + dt_b[0][None, :, None])
        u = jnp.transpose(xs_seq, (0, 2, 1))
        A = -jnp.exp(A_log[0])
        dA = jnp.exp(delta[..., None] * A[None, :, None, :])
        dBu = (delta * u)[..., None] * Bs[:, None, :, :]

        def comb(e1, e2):
            a1, x1 = e1
            a2, x2 = e2
            return (a2 * a1, a2 * x1 + x2)
        _, states = jax.lax.associative_scan(comb, (dA, dBu), axis=2)
        y = jnp.einsum('bdln,bln->bdl', states, Cs) + D_param[0][None, :, None] * u
        y = jnp.transpose(y, (0, 2, 1))
        mu = y.mean(-1, keepdims=True)
        var = y.var(-1, keepdims=True)
        y = (y - mu) * jax.lax.rsqrt(var + 1e-05) * ln_g + ln_b
        y = y.reshape(b, h, w, -1)
        out = y @ out_proj_w.T
        return jnp.transpose(out, (0, 3, 1, 2))

    def _L1_conv_ref(x, w1, b1, w2, b2):
        import jax, jax.numpy as jnp
        import numpy as np
        NH = 32
        R = 4
        LMBD = 0.01
        SCALE = 0.02

        def softshrink(v, l):
            return jnp.where(v > l, v - l, jnp.where(v < -l, v + l, jnp.zeros((), v.dtype)))
        B, C, H, W = x.shape
        SH = C // NH
        xf = jnp.fft.rfft2(x, norm='ortho')
        Wf = xf.shape[-1]
        xf = xf.reshape(B, NH, SH, H, Wf).transpose(0, 3, 4, 1, 2)
        xr, xi = (xf.real, xf.imag)
        x1r = jax.nn.relu(jnp.einsum('bhwns,nsc->bhwnc', xr, w1[0]) - jnp.einsum('bhwns,nsc->bhwnc', xi, w1[1]) + b1[0])
        x1i = jax.nn.relu(jnp.einsum('bhwns,nsc->bhwnc', xi, w1[1]) + jnp.einsum('bhwns,nsc->bhwnc', xr, w1[0]) + b1[1])
        x2r = jnp.einsum('bhwnc,ncs->bhwns', x1r, w2[0]) - jnp.einsum('bhwnc,ncs->bhwns', x1i, w2[1]) + b2[0]
        x2i = jnp.einsum('bhwnc,ncs->bhwns', x1i, w2[1]) + jnp.einsum('bhwnc,ncs->bhwns', x1r, w2[0]) + b2[1]
        x2r = softshrink(x2r, LMBD)
        x2i = softshrink(x2i, LMBD)
        xc = jax.lax.complex(x2r, x2i)
        xc = xc.transpose(0, 3, 4, 1, 2).reshape(B, C, H, Wf)
        return jnp.fft.irfft2(xc, s=(H, W), norm='ortho')

    def _gn(v, G=32, eps=1e-5):
        B_, C_, H_, W_ = v.shape
        g = v.reshape(B_, G, C_ // G, H_, W_)
        m = jnp.mean(g, axis=(2, 3, 4), keepdims=True)
        s = jnp.var(g, axis=(2, 3, 4), keepdims=True)
        return ((g - m) / jnp.sqrt(s + eps)).reshape(v.shape)

    def _ln_c(v, eps=1e-6):
        m = jnp.mean(v, axis=1, keepdims=True)
        s = jnp.var(v, axis=1, keepdims=True)
        return (v - m) / jnp.sqrt(s + eps)

    def _ln_t(v, eps=1e-5):
        m = jnp.mean(v, axis=-1, keepdims=True)
        s = jnp.var(v, axis=-1, keepdims=True)
        return (v - m) / jnp.sqrt(s + eps)

    def _to_tokens(v):
        B_, C_, H_, W_ = v.shape
        return v.reshape(B_, C_, H_ * W_).transpose(0, 2, 1)
    def _from_tokens(t, like):
        B_, C_, H_, W_ = like.shape
        return t.transpose(0, 2, 1).reshape(B_, C_, H_, W_)

    x = x + _L0_conv_ref(_gn(x), L0_conv_in_proj_w, L0_conv_conv_w, L0_conv_conv_b, L0_conv_x_proj_w, L0_conv_dt_w, L0_conv_dt_b, L0_conv_A_log, L0_conv_D_param, L0_conv_ln_g, L0_conv_ln_b, L0_conv_out_proj_w)
    x = x + _L1_conv_ref(_gn(x), L1_conv_w1, L1_conv_b1, L1_conv_w2, L1_conv_b2)
    return x


_drawn_inputs = setup_inputs


def setup_inputs(seed=0):
    import zlib

    import numpy as np

    out = dict(_drawn_inputs(seed))
    spreads = {'L0_conv_conv_b': (0.0, 0.1),
     'L0_conv_D_param': (1.0, 0.2),
     'L0_conv_ln_g': (1.0, 0.2),
     'L0_conv_ln_b': (0.0, 0.1)}
    factors = {'L0_conv_x_proj_w': 8.0,
     'L0_conv_dt_w': 8.0,
     'L0_conv_dt_b': 8.0,
     'L0_conv_A_log': 8.0,
     'L1_conv_w1': 4.485,
     'L1_conv_b1': 8.0,
     'L1_conv_w2': 3.558,
     'L1_conv_b2': 3.558}
    for name, (base, spread) in spreads.items():
        noise = np.random.default_rng([zlib.crc32(name.encode()), seed]).standard_normal(out[name].shape)
        drawn = base * np.exp(spread * noise) if base else spread * noise
        out[name] = jnp.asarray(drawn.astype(out[name].dtype))
    for name, factor in factors.items():
        out[name] = (out[name] * factor).astype(out[name].dtype)
    return out
```

```python
from contextlib import ExitStack

import numpy as np

import concourse.bass as bass
from concourse import mybir

F32 = mybir.dt.float32
ALU = mybir.AluOpType
ACT = mybir.ActivationFunctionType
AX = mybir.AxisListType

P = 128
NB, C, H, W = 2, 768, 64, 64
L = H * W
DI = 2 * C
NS = 4
RANK = C // 16
KT = C // P
DT = DI // P
NP = DT // 2
ROWS = 4
T = ROWS * W
NCH = H // ROWS
TT = T // P
XR = RANK + 2 * NS
ONE = 64
NG = 32
GC = C // NG
BP = NG // 2
PC = 2 * GC
HID = 4 * GC
HM = 4 * HID // P
KW = 8
NST = W // 2 // KW
SHRINK = 0.01
GN_EPS = 1e-5
LN_EPS = 1e-5
CH2 = C // 2


class Bufs:
    pass


def setup_stage(nc, d, k):
    with ExitStack() as ctx:
        def sb(name, shape):
            return ctx.enter_context(nc.sbuf_tensor(name, shape, F32))

        def sem(name):
            return ctx.enter_context(nc.semaphore(name))

        NX = 2
        xbuf = sb("setup_x", [P, NX, L])
        group = sb("setup_group", [P, KT, C])
        stats = sb("setup_stats", [P, L // 512, 6])
        agg = sb("setup_agg", [P, KT, NB, 2])
        moments = sb("setup_moments", [P, KT, NB, 2])
        lng = sb("setup_lng", [P, DT])
        lnb = sb("setup_lnb", [P, DT])
        alog = sb("setup_alog", [P, DT * NS])
        spread = sb("setup_spread", [P, DT, P])
        mean_of = sb("setup_mean_of", [P, P])
        gsum = sb("setup_gsum", [P, C])
        gmean = sb("setup_gmean", [P, KT * NB])
        gvar = sb("setup_gvar", [P, KT * NB])
        gsq = sb("setup_gsq", [P, KT * NB])
        ps_group = ctx.enter_context(nc.psum_tensor("ps_group", [P, 512], F32))
        ps_bv = ctx.enter_context(nc.psum_tensor("ps_bv", [P, 2, 512], F32))
        ps_g = ctx.enter_context(nc.psum_tensor("ps_g", [P, 2, 512], F32))

        x_in = [sem(f"setup_x_in{n}") for n in range(NX)]
        w_in = sem("setup_w_in")
        wo_in = sem("setup_wo_in")
        x_used = sem("setup_x_used")
        stat = sem("setup_stat")
        chain = sem("setup_chain")
        moments_ok = sem("setup_moments_ok")
        grouped = sem("setup_grouped")
        spread_ok = sem("setup_spread_ok")
        bv_ok = sem("setup_bv_ok")
        bv_out = sem("setup_bv_out")
        scaled = sem("setup_scaled")
        g_ok = sem("setup_g_ok")
        exp_ok = sem("setup_exp_ok")
        var_ok, root_ok = sem("setup_var_ok"), sem("setup_root_ok")
        block = ctx.enter_context(nc.Block())

        tiles = [(b, t) for b in range(NB) for t in range(KT)]

        @block.sync
        def _(sp):
            for n, (b, t) in enumerate(tiles):
                if n >= NX:
                    sp.wait_ge(x_used, n - NX + 1)
                sp.dma_start(xbuf[:, n % NX, :], d.x[b, t * P:(t + 1) * P, 0:L]).then_inc(x_in[n % NX], 16)
            sp.wait_ge(w_in, 16 * 12)

        @block.scalar
        def _(act):
            act.dma_start(k.w_out[:, :, :], d.w_out.rearrange("(t p) c -> p t c", p=P)).then_inc(wo_in, 16)
            act.dma_start(lng[:, :], d.ln_g).then_inc(wo_in, 16)
            act.dma_start(lnb[:, :], d.ln_b).then_inc(wo_in, 16)
            act.dma_start(alog[:, :], d.a_log).then_inc(wo_in, 16)
            act.dma_start(group[:, :, :], d.group).then_inc(wo_in, 16)
            act.dma_start(k.w_in[:, :, :], d.w_in.rearrange("(t p) m -> p t m", p=P)).then_inc(w_in, 16)
            act.dma_start(k.w_x[:, :, :], d.w_x.rearrange("(t p) m -> p t m", p=P)).then_inc(w_in, 16)
            act.dma_start(k.w_dt[0:RANK, :], d.w_dt).then_inc(w_in, 16)
            act.dma_start(k.w_dt[ONE:ONE + 1, :], d.dt_b).then_inc(w_in, 16)
            act.dma_start(k.w_dt[RANK:ONE, :], d.zeros).then_inc(w_in, 16)
            act.dma_start(k.conv_w[:, :, :], d.conv_w).then_inc(w_in, 16)
            act.dma_start(k.conv_b[:, :], d.conv_b).then_inc(w_in, 16)
            act.dma_start(k.d_par[:, :], d.d_par).then_inc(w_in, 16)
            act.dma_start(k.ident[:, :], d.ident).then_inc(w_in, 16)
            act.dma_start(k.f_w[:, :], d.f_w).then_inc(w_in, 16)
            act.dma_start(k.mask[:, :], d.mask).then_inc(w_in, 16)
            act.dma_start(k.xd[RANK:ONE, :], d.zeros[:, 0:T]).then_inc(w_in, 16)
            act.wait_ge(wo_in, 16 * 5)
            act.activation(k.a_neg[:, :], alog[:, :], ACT.Exp).then_inc(exp_ok, 1)
            act.wait_ge(var_ok, 1)
            act.activation(gsq[:, :], gvar[:, :], ACT.Sqrt).then_inc(root_ok, 1)

        @block.vector
        def _(dve):
            steps = [0]

            def link(ins):
                steps[0] += 1
                ins.then_inc(chain, 1)
                dve.wait_ge(chain, steps[0])

            dve.memset(k.xd[ONE:ONE + 1, :], 1.0)
            dve.memset(k.one[:, :], 1.0)
            dve.memset(mean_of[:, :], 1.0 / DI)
            dve.memset(spread[:, :, :], 1.0).then_inc(spread_ok, 1)
            dve.wait_ge(spread_ok, 1)
            dve.wait_ge(wo_in, 16 * 5)
            for t in range(DT):
                last = dve.tensor_scalar(spread[:, t, :], spread[:, t, :], lnb[:, t:t + 1], None, ALU.mult)
            last.then_inc(spread_ok, 1)
            dve.wait_ge(exp_ok, 1)
            link(dve.tensor_scalar(k.a_neg[:, :], k.a_neg[:, :], -1.0, None, ALU.mult))
            dve.wait_ge(bv_ok, 1)
            for j in range(2):
                last = dve.tensor_copy(k.bv[:, j * CH2:(j + 1) * CH2], ps_bv[:, j, 0:CH2])
            last.then_inc(bv_out, 1)
            for t in range(DT):
                last = dve.tensor_scalar(k.w_out[:, t, :], k.w_out[:, t, :], lng[:, t:t + 1], None, ALU.mult)
            last.then_inc(scaled, 1)
            dve.wait_ge(g_ok, 1)
            link(dve.tensor_copy(gsum[:, :].rearrange("p (j c) -> p j c", j=2), ps_g[:, :, 0:CH2]))
            for t in range(DT):
                last = dve.tensor_tensor(k.w_out[:, t, :], k.w_out[:, t, :], gsum[:, :], ALU.subtract)
            link(last)
            for n, (b, t) in enumerate(tiles):
                dve.wait_ge(x_in[n % NX], 16 * (n // NX + 1))
                if n:
                    dve.wait_ge(stat, n)
                for j in range(L // 512):
                    last = dve.bn_stats(stats[:, j, :], xbuf[:, n % NX, j * 512:(j + 1) * 512])
                last.then_inc(x_used, 1)
                dve.wait_ge(x_used, n + 1)
                dve.bn_aggr(agg[:, t, b, :], stats[:, :, :]).then_inc(stat, 1)
            dve.wait_ge(stat, len(tiles))
            mean, var = agg[:, :, :, 0], agg[:, :, :, 1]
            link(dve.tensor_tensor(moments[:, :, :, 1], mean, mean, ALU.mult))
            link(dve.tensor_tensor(moments[:, :, :, 1], moments[:, :, :, 1], var, ALU.add))
            dve.tensor_copy(moments[:, :, :, 0], mean).then_inc(moments_ok, 1)
            dve.wait_ge(grouped, 1)
            both = ps_group[:, 0:KT * NB * 2].rearrange("p (t b m) -> p (t b) m", b=NB, m=2)
            link(dve.tensor_copy(gmean[:, :], both[:, :, 0]))
            link(dve.tensor_tensor(gsq[:, :], gmean[:, :], gmean[:, :], ALU.mult))
            link(dve.tensor_tensor(gvar[:, :], both[:, :, 1], gsq[:, :], ALU.subtract))
            dve.tensor_scalar(gvar[:, :], gvar[:, :], 0.0, GN_EPS, ALU.max, ALU.add).then_inc(var_ok, 1)
            rs = k.gn_scale[:, :, :].rearrange("p t b -> p (t b)")
            nb = k.gn_shift[:, :, :].rearrange("p t b -> p (t b)")
            dve.wait_ge(root_ok, 1)
            link(dve.reciprocal(rs, gsq[:, :]))
            link(dve.scalar_tensor_tensor(nb, gmean[:, :], -1.0, rs, ALU.mult, ALU.mult))

        @block.tensor
        def _(pe):
            pe.wait_ge(spread_ok, 2)
            for t in range(DT):
                for j in range(2):
                    last = pe.matmul(ps_bv[:, j, 0:CH2], spread[:, t, :], k.w_out[:, t, j * CH2:(j + 1) * CH2],
                                     start=(t == 0), stop=(t == DT - 1))
            last.then_inc(bv_ok, 1)
            pe.wait_ge(scaled, 1)
            for t in range(DT):
                for j in range(2):
                    last = pe.matmul(ps_g[:, j, 0:CH2], mean_of[:, :], k.w_out[:, t, j * CH2:(j + 1) * CH2],
                                     start=(t == 0), stop=(t == DT - 1))
            last.then_inc(g_ok, 1)
            pe.wait_ge(moments_ok, 1)
            n = NB * 2
            for c in range(KT):
                for t in range(KT):
                    last = pe.matmul(ps_group[:, c * n:(c + 1) * n], group[:, t, c * P:(c + 1) * P],
                                     moments[:, t, :, :], start=(t == 0), stop=(t == KT - 1))
            last.then_inc(grouped, 1)


def scan_stage(nc, d, k):
    with ExitStack() as ctx:
        def sb(name, shape):
            return ctx.enter_context(nc.sbuf_tensor(name, shape, F32))

        def pb(name, shape):
            return ctx.enter_context(nc.psum_tensor(name, shape, F32))

        def sem(name):
            return ctx.enter_context(nc.semaphore(name))

        xn = sb("xn", [P, KT, T])
        x0 = sb("x0", [P, KT, W])
        xs = sb("xs", [P, DT, ROWS + 2, W])
        u = sb("u", [P, DT, T])
        y = sb("y", [P, DT, T])
        ysq = sb("ysq", [P, 2, 2, T])
        bc = sb("bc", [P, 2 * NS, T])
        q = sb("q", [P, 2, 2, T])
        delta = sb("delta", [P, 2, 2, T])
        du = sb("du", [P, 2, T])
        da = sb("da", [P, 2, NS, T])
        st = sb("st", [P, 2, NS, T])
        carry = sb("carry", [P, DT, NS])
        xt = sb("xt", [P, TT, C])
        f1o = sb("f1o", [P, TT, C])
        zsq = sb("zsq", [P, C])
        accz = sb("accz", [P, C])
        accq = sb("accq", [P, C])
        ln = sb("ln", [P, 4, TT])

        ps_i = pb("ps_i", [P, 2, 512])
        ps_d = pb("ps_d", [P, 2, 512])
        ps_o = pb("ps_o", [P, 2, 512])
        ps_x = pb("ps_x", [P, 512])
        ps_y = pb("ps_y", [P, 512])

        x_in, x0_in, xt_in = sem("x_in"), sem("x0_in"), sem("xt_in")
        x_normed, x0_normed = sem("x_normed"), sem("x0_normed")
        in_done, in0_done = sem("in_done"), sem("in0_done")
        xs_ready, xs0_ready, xs_moved, xs_zero = sem("xs_ready"), sem("xs0_ready"), sem("xs_moved"), sem("xs_zero")
        centre_done, tap_done, u_ready = sem("centre_done"), sem("tap_done"), sem("u_ready")
        xp_done, xd_ready, bc_done, bc_ready = sem("xp_done"), sem("xd_ready"), sem("bc_done"), sem("bc_ready")
        dt_done, abs_done, exp_done, q_ready = sem("dt_done"), sem("abs_done"), sem("exp_done"), sem("q_ready")
        delta_ready, du_ready, da_ready, dbu_ready = sem("delta_ready"), sem("du_ready"), sem("da_ready"), sem("dbu_ready")
        scan_done, carry_kept, carry_zero, yc_done = sem("scan_done"), sem("carry_kept"), sem("carry_zero"), sem("yc_done")
        half_done, sum_done, y_ready = sem("half_done"), sem("sum_done"), sem("y_ready")
        ysq_ready, ysq_done = sem("ysq_ready"), sem("ysq_done")
        out_done, ln_step = sem("out_done"), sem("ln_step")
        var_ready, log_ready, rstd_ready = sem("var_ready"), sem("log_ready"), sem("rstd_ready")
        xb_ready, z_ready = sem("xb_ready"), sem("z_ready")
        f1_done, f1_ready = sem("f1_done"), sem("f1_ready")
        sq_done, accq_done, acc_zero, reduced = sem("sq_done"), sem("accq_done"), sem("acc_zero"), sem("reduced")
        x2_out, z1_out = sem("x2_out"), sem("z1_out")
        turn = sem("turn")
        per_chunk = [
            (in_done, NP), (xs_ready, NP), (xs_moved, NP), (centre_done, NP), (u_ready, NP), (dt_done, NP),
            (abs_done, NP), (exp_done, NP), (q_ready, NP), (delta_ready, NP), (du_ready, NP), (da_ready, NP),
            (dbu_ready, NP), (scan_done, NP), (carry_kept, NP), (yc_done, NP), (half_done, NP), (sum_done, NP),
            (y_ready, NP), (ysq_ready, NP), (ysq_done, NP), (tap_done, 16 * NP), (bc_done, NS), (bc_ready, NS),
            (out_done, TT), (z_ready, TT), (f1_done, TT), (f1_ready, TT), (sq_done, TT), (accq_done, TT), (ln_step, 3), (var_ready, 1), (rstd_ready, 1), (log_ready, 1),
            (x_normed, 1), (xp_done, 1), (xd_ready, 1), (xb_ready, 1),
            (x_in, 16), (xt_in, 16), (x2_out, 16), (z1_out, 32),
        ]
        block = ctx.enter_context(nc.Block())

        x_chunks = d.x[:, :, W:W + L].rearrange("b (t p) (i n) -> b i p t n", p=P, n=T)
        xt_chunks = d.x_tok.rearrange("(g t p) c -> g p t c", t=TT, p=P)
        x2_chunks = d.x2.rearrange("(g t p) c -> g p t c", t=TT, p=P)
        z1_chunks = d.z1.rearrange("b q (i t h) c -> b i h q t c", t=TT, h=2)

        def chunks(engine, body, b):
            first = NCH * b + 1
            with engine.Fori(0, NCH - 2) as i:
                body(i + first, i, ROWS, True)
            body(first + NCH - 2, NCH - 2, ROWS - 1, False)
            body(first + NCH - 1, NCH - 1, 0, False)

        @block.sync
        def _(sp):
            def load_x(c, b, i):
                sp.wait_ge(in_done, NP * c)
                sp.sem_inc(turn, 1)
                sp.dma_start(xn[:, :, :], x_chunks[b, i]).then_inc(x_in, 16)

            def body(b, c, i, rows, more):
                sp.wait_ge(x2_out, 16 * c)
                sp.sem_inc(turn, 1)
                sp.wait_ge(accq_done, TT * c)
                sp.sem_inc(turn, 1)
                sp.wait_ge(f1_done, TT * c)
                sp.sem_inc(turn, 1)
                sp.dma_start(xt[:, :, :], xt_chunks[i + NCH * b]).then_inc(xt_in, 16)
                if more:
                    load_x(c + 2, b, i + 2)
                sp.wait_ge(z_ready, TT * c + TT)
                sp.sem_inc(turn, 1)
                sp.dma_start(x2_chunks[i + NCH * b], xt[:, :, :]).then_inc(x2_out, 16)
                sp.wait_ge(f1_ready, TT * c + TT)
                sp.sem_inc(turn, 1)
                for h in range(2):
                    sp.dma_start(z1_chunks[b, i, h], f1o[h * W:(h + 1) * W, :, :]).then_inc(z1_out, 16)

            for b in range(NB):
                c = NCH * b + 1
                if b:
                    sp.wait_ge(in0_done, NP * b)
                sp.dma_start(x0[:, :, :], d.x[b, :, 0:W].rearrange("(t p) w -> p t w", p=P)).then_inc(x0_in, 16)
                load_x(c, b, 0)
                load_x(c + 1, b, 1)
                chunks(sp, lambda *a: body(b, *a), b)
            sp.wait_ge(x2_out, 16 * (NB * NCH + 1))
            sp.wait_ge(z1_out, 32 * (NB * NCH + 1))

        @block.tensor
        def _(pe):
            def in0(b, p):
                if p < 2:
                    pe.wait_ge(z_ready, TT * (NCH * b + 1))
                else:
                    pe.wait_ge(xs0_ready, NP * b + p - 1)
                if p == 0:
                    pe.wait_ge(x0_normed, b + 1)
                for j in range(2):
                    m = (2 * p + j) * P
                    for t in range(KT):
                        last = pe.matmul(ps_i[:, p % 2, j * T:j * T + W], k.w_in[:, t, m:m + P], x0[:, t, :],
                                         start=(t == 0), stop=(t == KT - 1))
                last.then_inc(in0_done, 1)

            def in_proj(c, p, rows, first=None):
                if p >= 2:
                    pe.wait_ge(xs_ready, NP * c + p - 1)
                elif first is None:
                    pe.wait_ge(z_ready, TT * (c - 1))
                else:
                    pe.wait_ge(xs0_ready, NP * first + NP - 1 + p)
                if p == 0:
                    pe.wait_ge(x_normed, c + 1)
                for j in range(2):
                    m = (2 * p + j) * P
                    for t in range(KT):
                        last = pe.matmul(ps_i[:, p % 2, j * T:j * T + rows * W], k.w_in[:, t, m:m + P],
                                         xn[:, t, 0:rows * W], start=(t == 0), stop=(t == KT - 1))
                last.then_inc(in_done, 1)

            def x_proj(c, p):
                if p == 0:
                    pe.wait_ge(xd_ready, c)
                pe.wait_ge(u_ready, NP * c + p + 1)
                for j in range(2):
                    t = 2 * p + j
                    last = pe.matmul(ps_x[0:XR, 0:T], k.w_x[:, t, :], u[:, t, :], start=(t == 0), stop=(t == DT - 1))
                if p == NP - 1:
                    last.then_inc(xp_done, 1)

            def step(c, p):
                if p < 2:
                    pe.wait_ge(xd_ready, c + 1)
                    pe.wait_ge(f1_ready, TT * c)
                else:
                    pe.wait_ge(delta_ready, NP * c + p - 1)
                for j in range(2):
                    m = (2 * p + j) * P
                    last = pe.matmul(ps_d[:, p % 2, j * T:(j + 1) * T], k.w_dt[0:ONE + 1, m:m + P],
                                     k.xd[0:ONE + 1, :], start=True, stop=True)
                last.then_inc(dt_done, 1)

            def spread_bc(c, r):
                if r >= 2:
                    pe.wait_ge(bc_ready, NS * c + r - 1)
                for j in range(2):
                    row = RANK + 2 * r + j
                    last = pe.matmul(ps_o[:, r % 2, j * T:(j + 1) * T], k.ident[0:XR, row:row + 1].to_broadcast([XR, P]),
                                     k.xd[0:XR, :], start=True, stop=True)
                last.then_inc(bc_done, 1)

            def square_sums(c, p):
                pe.wait_ge(ysq_ready, NP * c + p + 1)
                if p == 0:
                    pe.wait_ge(var_ready, c)
                for j in range(2):
                    for tt in range(TT):
                        n = slice(tt * P, (tt + 1) * P)
                        first, end = p == 0 and j == 0 and tt == 0, p == NP - 1 and j == 1
                        pe.matmul(ps_y[:, tt:tt + 1], ysq[:, p % 2, j, n], k.one[:, :],
                                  start=first, stop=end, skip_group_check=True)
                        last = pe.matmul(ps_y[:, TT + tt:TT + tt + 1], y[:, 2 * p + j, n], k.one[:, :],
                                         start=False, stop=end, skip_group_check=True)
                last.then_inc(ysq_done, 1)

            def out_proj(c, tt, ps):
                for t in range(DT):
                    lhs = y[:, t, tt * P:(tt + 1) * P]
                    for j in range(2):
                        last = pe.matmul(ps[:, j, 0:CH2], lhs, k.w_out[:, t, j * CH2:(j + 1) * CH2],
                                         start=(t == 0), stop=(t == DT - 1))
                last.then_inc(out_done, 1)

            def transform(c, tt, ps):
                pe.wait_ge(z_ready, TT * c + tt + 1)
                for j in range(2):
                    last = pe.matmul(ps[:, j, 0:CH2], k.f_w[:, :], xt[:, tt, j * CH2:(j + 1) * CH2], start=True, stop=True)
                last.then_inc(f1_done, 1)

            def body(c, i, rows, more):
                step(c, 0)
                step(c, 1)
                for r in range(NS):
                    spread_bc(c, r)
                for p in range(NP):
                    if rows:
                        in_proj(c + 1, p, rows)
                    if p + 2 < NP:
                        step(c, p + 2)
                    if p >= 2:
                        square_sums(c, p - 2)
                square_sums(c, NP - 2)
                square_sums(c, NP - 1)
                pe.wait_ge(y_ready, NP * c + NP)
                pe.wait_ge(bc_ready, NS * c + NS)
                out_proj(c, 0, ps_o)
                if rows:
                    x_proj(c + 1, 0)
                    pe.wait_ge(xs_ready, NP * (c + 1) + NP)
                out_proj(c, 1, ps_i)
                transform(c, 0, ps_d)
                if rows:
                    for p in range(1, NP - 1):
                        x_proj(c + 1, p)
                transform(c, 1, ps_o)
                if rows:
                    x_proj(c + 1, NP - 1)

            for b in range(NB):
                c = NCH * b + 1
                for p in range(NP):
                    in0(b, p)
                for p in range(NP):
                    in_proj(c, p, ROWS, first=b)
                for p in range(NP):
                    x_proj(c, p)
                chunks(pe, body, b)

        @block.scalar
        def _(act):
            def norm(b, tile, got, value, done):
                act.wait_ge(got, value)
                for t in range(KT):
                    last = act.activation(tile[:, t, :], tile[:, t, :], ACT.Identity,
                                          bias=k.gn_shift[:, t, b:b + 1], scale=k.gn_scale[:, t, b:b + 1])
                last.then_inc(done, 1)

            def take_xs(c, p, rows, first=None):
                a, e = 2 * p, 2 * p + 2
                if first is None:
                    act.wait_ge(tap_done, 16 * (NP * (c - 1) + p + 1))
                    act.activation(xs[:, a:e, 0:2, :], xs[:, a:e, ROWS:ROWS + 2, :], ACT.Copy).then_inc(xs_moved, 1)
                    act.wait_ge(xs_moved, NP * c + p + 1)
                else:
                    act.sem_inc(xs_moved, 1)
                act.wait_ge(in_done, NP * c + p + 1)
                act.activation(xs[:, a:e, 2:2 + rows, :],
                               ps_i[:, p % 2, :].rearrange("p (j r w) -> p j r w", j=2, w=W)[:, :, 0:rows, :],
                               ACT.Copy).then_inc(xs_ready, 1)

            def centre(c, p, used):
                act.wait_ge(y_ready, NP * (c - 1) + used)
                act.wait_ge(xs_ready, NP * c + p + 1)
                for t in (2 * p, 2 * p + 1):
                    last = act.activation(u[:, t, :], xs[:, t, 1:1 + ROWS, :], ACT.Identity,
                                          bias=k.conv_b[:, t:t + 1], scale=k.conv_w[:, t, 4:5])
                last.then_inc(centre_done, 1)

            def silu(c, p):
                act.wait_ge(tap_done, 16 * (NP * c + p + 1))
                act.activation(u[:, 2 * p:2 * p + 2, :], u[:, 2 * p:2 * p + 2, :], ACT.Silu).then_inc(u_ready, 1)

            def log_part(c, p):
                act.wait_ge(dt_done, NP * c + p + 1)
                act.wait_ge(delta_ready, NP * c + max(p - 1, 0))
                v = q[:, p % 2, :, :].rearrange("p j n -> p (j n)")
                act.activation(v, ps_d[:, p % 2, :], ACT.Abs).then_inc(abs_done, 1)
                act.wait_ge(abs_done, NP * c + p + 1)
                act.activation(v, v, ACT.Exp, scale=-1.0).then_inc(exp_done, 1)
                act.wait_ge(exp_done, NP * c + p + 1)
                act.activation(v, v, ACT.Ln, bias=1.0).then_inc(q_ready, 1)

            def decay(c, p):
                act.wait_ge(delta_ready, NP * c + p + 1)
                act.wait_ge(scan_done, NP * c + p)
                for j in range(2):
                    for n in range(NS):
                        a = (2 * p + j) * NS + n
                        last = act.activation(da[:, j, n, :], delta[:, p % 2, j, :], ACT.Exp, scale=k.a_neg[:, a:a + 1])
                last.then_inc(da_ready, 1)

            def square(c, p):
                act.wait_ge(y_ready, NP * c + p + 1)
                act.wait_ge(ysq_done, NP * c + max(p - 1, 0))
                act.activation(ysq[:, p % 2, :, :], y[:, 2 * p:2 * p + 2, :], ACT.Square).then_inc(ysq_ready, 1)

            def take_transform(c, tt, ps):
                act.wait_ge(f1_done, TT * c + tt + 1)
                if tt == 0:
                    act.wait_ge(z1_out, 32 * c)
                act.activation(f1o[:, tt, :].rearrange("p (j c) -> p j c", j=2), ps[:, :, 0:CH2],
                               ACT.Copy).then_inc(f1_ready, 1)

            def body(b, c, i, rows, more):
                act.wait_ge(xp_done, c + 1)
                act.wait_ge(dt_done, NP * c)
                act.activation(k.xd[0:XR, :], ps_x[0:XR, 0:T], ACT.Copy).then_inc(xd_ready, 1)
                log_part(c, 0)
                act.wait_ge(yc_done, NP * c)
                for r in range(NS):
                    act.wait_ge(bc_done, NS * c + r + 1)
                    act.activation(bc[:, 2 * r:2 * r + 2, :].rearrange("p j n -> p (j n)"), ps_o[:, r % 2, :],
                                   ACT.Copy).then_inc(bc_ready, 1)
                for p in range(NP):
                    if p + 1 < NP:
                        log_part(c, p + 1)
                    decay(c, p)
                    if rows:
                        take_xs(c + 1, p, rows)
                    if p >= 2:
                        square(c, p - 2)
                        if rows:
                            centre(c + 1, p - 2, p - 1)
                for p in (NP - 2, NP - 1):
                    square(c, p)
                    if rows:
                        centre(c + 1, p, p + 1)
                if more:
                    norm(b, xn, x_in, 16 * (c + 3), x_normed)
                act.wait_ge(var_ready, c + 1)
                act.activation(ln[:, 3, :], ln[:, 2, :], ACT.Ln).then_inc(log_ready, 1)
                act.wait_ge(log_ready, c + 1)
                act.activation(ln[:, 3, :], ln[:, 3, :], ACT.Exp, scale=-0.5).then_inc(rstd_ready, 1)
                for p in range(NP):
                    if rows:
                        silu(c + 1, p)
                    if p == 2:
                        take_transform(c, 0, ps_d)
                    if p == NP - 2:
                        take_transform(c, 1, ps_o)

            for b in range(NB):
                c = NCH * b + 1
                norm(b, x0, x0_in, 16 * (b + 1), x0_normed)
                norm(b, xn, x_in, 16 * (c + 1), x_normed)
                for p in range(NP):
                    act.wait_ge(in0_done, NP * b + p + 1)
                    if p == 0 and b:
                        act.wait_ge(tap_done, 16 * NP * c)
                    act.activation(xs[:, 2 * p:2 * p + 2, 1, :],
                                   ps_i[:, p % 2, :].rearrange("p (j r w) -> p j r w", j=2, w=W)[:, :, 0, :],
                                   ACT.Copy).then_inc(xs0_ready, 1)
                act.wait_ge(xs_zero, 2 * b + 1)
                for p in range(NP):
                    take_xs(c, p, ROWS, first=b)
                    centre(c, p, NP)
                norm(b, xn, x_in, 16 * (c + 2), x_normed)
                for p in range(NP):
                    silu(c, p)
                chunks(act, lambda *a: body(b, *a), b)

        @block.vector
        def _(dve):
            taps = [(dy, dx) for dy in range(3) for dx in range(3) if (dy, dx) != (1, 1)]

            def convolve(c, p):
                dve.wait_ge(centre_done, NP * c + p + 1)
                base = 16 * (NP * c + p)
                for n, (dy, dx) in enumerate(taps):
                    for j in range(2):
                        t = 2 * p + j
                        if n:
                            dve.wait_ge(tap_done, base + 2 * n - 1 + j)
                        a, e = max(0, 1 - dx), W - max(0, dx - 1)
                        out = u[:, t, :].rearrange("p (r w) -> p r w", w=W)[:, :, a:e]
                        dve.scalar_tensor_tensor(out, xs[:, t, dy:dy + ROWS, a + dx - 1:e + dx - 1],
                                                 k.conv_w[:, t, 3 * dy + dx:3 * dy + dx + 1], out,
                                                 ALU.mult, ALU.add).then_inc(tap_done, 1)

            def step(c, p):
                dve.wait_ge(q_ready, NP * c + p + 1)
                dve.wait_ge(da_ready, NP * c + max(p - 1, 0))
                dve.scalar_tensor_tensor(delta[:, p % 2, :, :].rearrange("p j n -> p (j n)"), ps_d[:, p % 2, :], 0.0,
                                         q[:, p % 2, :, :].rearrange("p j n -> p (j n)"),
                                         ALU.max, ALU.add).then_inc(delta_ready, 1)
                dve.wait_ge(delta_ready, NP * c + p + 1)
                dve.wait_ge(dbu_ready, NP * c + p)
                dve.tensor_tensor(du[:, :, :], delta[:, p % 2, :, :], u[:, 2 * p:2 * p + 2, :],
                                  ALU.mult).then_inc(du_ready, 1)

            def inflow(c, p):
                dve.wait_ge(du_ready, NP * c + p + 1)
                dve.wait_ge(bc_ready, NS * c + NS // 2)
                dve.wait_ge(y_ready, NP * c + p)
                dve.tensor_tensor(st[:, :, :, :], du[:, :, None, :].to_broadcast([P, 2, NS, T]),
                                  bc[:, None, 0:NS, :].to_broadcast([P, 2, NS, T]), ALU.mult).then_inc(dbu_ready, 1)

            def scan(c, p):
                dve.wait_ge(da_ready, NP * c + p + 1)
                dve.wait_ge(dbu_ready, NP * c + p + 1)
                dve.wait_ge(carry_kept, NP * c + p)
                for j in range(2):
                    for n in range(NS):
                        last = dve.tensor_tensor_scan(st[:, j, n, :], da[:, j, n, :], st[:, j, n, :],
                                                      carry[:, 2 * p + j, n:n + 1], ALU.mult, ALU.add)
                last.then_inc(scan_done, 1)
                dve.wait_ge(scan_done, NP * c + p + 1)
                dve.tensor_copy(carry[:, 2 * p:2 * p + 2, :], st[:, :, :, T - 1]).then_inc(carry_kept, 1)

            def outflow(c, p):
                dve.wait_ge(bc_ready, NS * c + NS)
                dve.wait_ge(carry_kept, NP * c + p + 1)
                dve.tensor_tensor(st[:, :, :, :], st[:, :, :, :], bc[:, None, NS:2 * NS, :].to_broadcast([P, 2, NS, T]),
                                  ALU.mult).then_inc(yc_done, 1)
                dve.wait_ge(yc_done, NP * c + p + 1)
                dve.tensor_tensor(st[:, :, 0:2, :], st[:, :, 0:2, :], st[:, :, 2:4, :], ALU.add).then_inc(half_done, 1)
                dve.wait_ge(half_done, NP * c + p + 1)
                if p == 0:
                    dve.wait_ge(out_done, TT * c)
                dve.tensor_tensor(y[:, 2 * p:2 * p + 2, :], st[:, :, 0, :], st[:, :, 1, :], ALU.add).then_inc(sum_done, 1)
                dve.wait_ge(sum_done, NP * c + p + 1)
                for t in (2 * p, 2 * p + 1):
                    last = dve.scalar_tensor_tensor(y[:, t, :], u[:, t, :], k.d_par[:, t:t + 1], y[:, t, :],
                                                    ALU.mult, ALU.add)
                last.then_inc(y_ready, 1)

            def layer_norm(c):
                n = 3 * c
                mean, sq, var = (ln[:, m, :] for m in range(3))
                dve.wait_ge(ysq_done, NP * c + NP)
                dve.wait_ge(rstd_ready, c)
                dve.tensor_scalar(mean, ps_y[:, TT:2 * TT], 1.0 / DI, None, ALU.mult).then_inc(ln_step, 1)
                dve.wait_ge(ln_step, n + 1)
                dve.tensor_tensor(sq, mean, mean, ALU.mult).then_inc(ln_step, 1)
                dve.wait_ge(ln_step, n + 2)
                dve.scalar_tensor_tensor(var, ps_y[:, 0:TT], 1.0 / DI, sq, ALU.mult, ALU.subtract).then_inc(ln_step, 1)
                dve.wait_ge(ln_step, n + 3)
                dve.tensor_scalar(var, var, 0.0, LN_EPS, ALU.max, ALU.add).then_inc(var_ready, 1)

            def result(c, tt, ps):
                dve.wait_ge(out_done, TT * c + tt + 1)
                dve.wait_ge(rstd_ready, c + 1)
                dve.wait_ge(xb_ready, c + 1)
                tile = xt[:, tt, :].rearrange("p (j c) -> p j c", j=2)
                dve.scalar_tensor_tensor(tile, ps[:, :, 0:CH2], ln[:, 3, tt:tt + 1], tile, ALU.mult, ALU.add).then_inc(z_ready, 1)

            def body(b, c, i, rows, more):
                step(c, 0)
                inflow(c, 0)
                for p in range(NP):
                    if p + 1 < NP:
                        step(c, p + 1)
                    scan(c, p)
                    outflow(c, p)
                    if p + 1 < NP:
                        inflow(c, p + 1)
                if 0 < rows < ROWS:
                    dve.wait_ge(xs_moved, NP * (c + 1) + NP)
                    dve.memset(xs[:, :, 2 + rows, :], 0.0).then_inc(xs_zero, 1)
                    dve.wait_ge(xs_zero, 2 * b + 2)
                for p in range(NP):
                    if rows:
                        convolve(c + 1, p)
                    if p == 0:
                        layer_norm(c)
                    if p == 2:
                        result(c, 0, ps_o)
                    if p == NP - 2:
                        result(c, 1, ps_i)

            for b in range(NB):
                c = NCH * b + 1
                if b:
                    dve.wait_ge(tap_done, 16 * NP * c)
                    dve.wait_ge(carry_kept, NP * c)
                dve.memset(xs[:, :, 0, :], 0.0).then_inc(xs_zero, 1)
                dve.memset(carry[:, :, :], 0.0).then_inc(carry_zero, 1)
                dve.wait_ge(carry_zero, b + 1)
                for p in range(NP):
                    convolve(c, p)
                chunks(dve, lambda *a: body(b, *a), b)
                dve.wait_ge(accq_done, TT * (c + NCH))
                for m, acc in enumerate((accz, accq)):
                    last = dve.tensor_reduce(k.sums[:, b, m, :], acc[:, :].rearrange("p (g c) -> p g c", c=GC), AX.X, ALU.add)
                last.then_inc(reduced, 1)

        @block.gpsimd
        def _(pool):
            for s, n in per_chunk:
                pool.sem_inc(s, n)

            def body(c, i, rows, more):
                pool.wait_ge(xt_in, 16 * (c + 1))
                for tt in range(TT):
                    last = pool.tensor_tensor(xt[:, tt, :], xt[:, tt, :], k.bv[:, :], ALU.add)
                last.then_inc(xb_ready, 1)
                for tt in range(TT):
                    pool.wait_ge(z_ready, TT * c + tt + 1)
                    pool.wait_ge(accq_done, TT * c + tt)
                    pool.tensor_tensor(zsq[:, :], xt[:, tt, :], xt[:, tt, :], ALU.mult).then_inc(sq_done, 1)
                    pool.tensor_tensor(accz[:, :], accz[:, :], xt[:, tt, :], ALU.add)
                    pool.wait_ge(sq_done, TT * c + tt + 1)
                    pool.tensor_tensor(accq[:, :], accq[:, :], zsq[:, :], ALU.add).then_inc(accq_done, 1)

            for b in range(NB):
                if b:
                    pool.wait_ge(reduced, b)
                pool.memset(accz[:, :], 0.0)
                pool.memset(accq[:, :], 0.0).then_inc(acc_zero, 1)
                pool.wait_ge(acc_zero, b + 1)
                chunks(pool, body, b)


def mlp_stage(nc, d, k):
    with ExitStack() as ctx:
        def sb(name, shape):
            return ctx.enter_context(nc.sbuf_tensor(name, shape, F32))

        def pb(name, shape):
            return ctx.enter_context(nc.psum_tensor(name, shape, F32))

        def sem(name):
            return ctx.enter_context(nc.semaphore(name))

        PAD = 16
        NPOS = KW * H
        QC = C // 4
        UNITS = 16
        LAG = 5
        zt = sb("zt", [P, 2, KW, C + PAD])
        zt0 = sb("zt0", [P, C + PAD])
        w1 = sb("mlp_w1", [P, BP, HM * P])
        w2 = sb("mlp_w2", [P, BP, HM, 2 * PC])
        b1 = sb("mlp_b1", [P, BP, HM])
        b2 = sb("mlp_b2", [P, BP, 2 * PC])
        f_h = sb("f_h", [P, 3, 2, H])
        i_h = sb("i_h", [P, P])
        spec = sb("spec", [P, 2, NPOS])
        hid = sb("hid", [P, 2, HM, NPOS])
        val = sb("val", [P, 2, KW // 2, 2 * PC])
        clip = sb("clip", [P, 2, KW // 2, 2 * PC])
        shr = sb("shr", [P, KW // 2, 2, C])
        inv = sb("inv", [P, KW, C])
        cols = sb("cols", [P, KW, C])
        ones = sb("mlp_ones", [P, P])
        gm = sb("gm", [P, NB, NG])
        gv = sb("gv", [P, NB, NG])
        gt = sb("gt", [P, NB, NG])
        pick = sb("pick", [P, NB, BP])
        scale = sb("scale", [P, NB, BP])
        shift = sb("shift", [P, NB, BP])

        ps_f = pb("ps_f", [P, 2, 512])
        ps_h = pb("ps_h", [P, HM, 512])
        ps_v = pb("ps_v", [P, 2, 512])
        ps_c = pb("ps_c", [P, 512])

        w_in, z0_in = sem("mlp_w_in"), sem("z0_in")
        z_in = [sem(f"z_in{n}") for n in range(2)]
        chain, ones_ok, stats_ok, sign_ok, pad_ok = sem("m_chain"), sem("ones_ok"), sem("stats_ok"), sem("sign_ok"), sem("pad_ok")
        var_ok, root_ok = sem("m_var_ok"), sem("m_root_ok")
        f_done, spec_ready, dc_done = sem("f_done"), sem("spec_ready"), sem("dc_done")
        h_done, hid_act, hid_dve = sem("h_done"), sem("hid_act"), sem("hid_dve")
        v_done, val_ready, clip_ready, shr_ready = sem("v_done"), sem("val_ready"), sem("clip_ready"), sem("shr_ready")
        inv_in = [sem(f"inv_in{quarter}") for quarter in range(4)]
        c_done, cols_ready, z2_out = sem("c_done"), sem("cols_ready"), sem("z2_out")
        per_step = [(f_done, BP), (spec_ready, BP), (h_done, HM * BP), (hid_act, 2 * BP), (hid_dve, BP), (v_done, BP),
                    (val_ready, BP), (clip_ready, BP), (shr_ready, BP), (c_done, UNITS),
                    (cols_ready, UNITS), (z2_out, 32)] + [(s, 64) for s in inv_in]
        block = ctx.enter_context(nc.Block())

        z1_tiles = d.z1.rearrange("b (t r) h c -> b t (r h) c", r=2)
        z2_cols = d.z2.rearrange("b h (t r) c -> b r h t c", r=2)
        PER = NST + 1

        def steps(engine, step):
            for b in range(NB):
                with engine.Fori(0, NST // 2) as i:
                    for e in range(2):
                        step(b, 2 * i + (PER * b + e), e, i + (NST // 2 * b + 1), KW)
                step(b, PER * b + NST, None, b + 1, 2)

        @block.sync
        def _(sp):
            sp.dma_start(w1[:, :, :], d.mlp_w1).then_inc(w_in, 16)
            sp.dma_start(w2[:, :, :, :], d.mlp_w2).then_inc(w_in, 16)
            sp.dma_start(b1[:, :, :], d.mlp_b1).then_inc(w_in, 16)
            sp.dma_start(b2[:, :, :].rearrange("p a c -> p (a c)"), d.mlp_b2.to_broadcast([P, BP * 2 * PC])).then_inc(w_in, 16)
            sp.dma_start(f_h[:, :, :, :], d.f_h).then_inc(w_in, 16)
            sp.dma_start(i_h[:, :], d.i_h).then_inc(w_in, 16)

            def load(g):
                b, s = g // NST, g % NST
                sp.dma_start(zt[:, g % 2, :, 0:C], z1_tiles[b, s * KW:(s + 1) * KW].rearrange("t p c -> p t c")
                             ).then_inc(z_in[g % 2], 16)

            load(0)
            load(1)
            for n in range(NB * PER):
                b, s = n // PER, n % PER
                m = KW if s < NST else 2
                if s == 0:
                    if b:
                        sp.wait_ge(f_done, BP * (PER * b + 2))
                    sp.dma_start(zt0[:, 0:C], z1_tiles[b, 0]).then_inc(z0_in, 16)
                sp.wait_ge(c_done, UNITS * (n + 2))
                for quarter in range(4):
                    sp.wait_ge(shr_ready, BP * (n + 2) + 4 * quarter + 4)
                    part = slice(quarter * QC, (quarter + 1) * QC)
                    for f in range(2):
                        for r in range(2):
                            sp.dma_start(inv[r * H:(r + 1) * H, f:m:2, part],
                                         shr[f * H:(f + 1) * H, 0:m // 2, r, part]).then_inc(inv_in[quarter], 16)
                g = NST * b + s + 2
                if s < NST and g < NB * NST:
                    sp.wait_ge(f_done, BP * (n + 3))
                    load(g)
                sp.wait_ge(cols_ready, UNITS * (n + 3))
                if s < NST:
                    for r in range(2):
                        sp.dma_start(z2_cols[b, r, :, s * KW:(s + 1) * KW, :], cols[r * H:(r + 1) * H, :, :]).then_inc(z2_out, 16)
                else:
                    sp.wait_ge(z2_out, 32 * (n + 2))
                    sp.dma_start(d.z2[b, :, 0:2, :], cols[0:H, 0:2, :]).then_inc(z2_out, 32)
            sp.wait_ge(z2_out, 32 * (NB * PER + 2))

        @block.gpsimd
        def _(pool):
            for s, n in per_step:
                pool.sem_inc(s, 2 * n)
            pool.memset(zt[:, :, :, C:C + PAD], 0.0)
            pool.memset(zt0[:, C:C + PAD], 0.0).then_inc(pad_ok, 1)

        @block.tensor
        def _(pe):
            pe.wait_ge(ones_ok, 1)
            pe.matmul(ps_c[:, 0:NB * 2 * NG], ones[:, :], k.sums[:, :, :, :], start=True, stop=True).then_inc(stats_ok, 1)
            pe.wait_ge(w_in, 16 * 6)
            pe.wait_ge(sign_ok, 1)
            pe.wait_ge(pad_ok, 1)

            def transform(n, a, buf, width):
                pe.wait_ge(spec_ready, BP * (n + 2) + max(a - 1, 0))
                for j in range(width):
                    cut = slice(a * PC, a * PC + PC + PAD)
                    lhs, f = (zt0[:, cut], 1 + j) if buf is None else (zt[:, buf, j, cut], 0)
                    for r in range(2):
                        last = pe.matmul(ps_f[r * H:(r + 1) * H, a % 2, j * H:(j + 1) * H], lhs, f_h[:, f, r, :],
                                         start=True, stop=True)
                last.then_inc(f_done, 1)

            def hidden(b, n, a, buf, width):
                pe.wait_ge(spec_ready, BP * (n + 2) + a + 1)
                if buf is None:
                    pe.wait_ge(dc_done, b * BP + a + 1)
                pe.wait_ge(hid_act, 2 * (BP * (n + 2) + a))
                pe.wait_ge(hid_dve, BP * (n + 2) + a)
                for t in range(HM):
                    pe.matmul(ps_h[:, t, 0:width * H], w1[:, a, t * P:(t + 1) * P], spec[:, a % 2, 0:width * H],
                              start=True, stop=True).then_inc(h_done, 1)

            def second(n, a, width):
                pe.wait_ge(hid_act, 2 * (BP * (n + 2) + a + 1))
                pe.wait_ge(hid_dve, BP * (n + 2) + a + 1)
                pe.wait_ge(val_ready, BP * (n + 2) + max(a - 1, 0))
                for f in range(width // 2):
                    for t in range(HM):
                        last = pe.matmul(ps_v[:, a % 2, f * 2 * PC:(f + 1) * 2 * PC], hid[:, a % 2, t, f * P:(f + 1) * P],
                                         w2[:, a, t, :], start=(t == 0), stop=(t == HM - 1))
                last.then_inc(v_done, 1)

            def inverse(n, unit, width):
                per = width // 2
                quarter, f = unit // per, unit % per
                share = UNITS // (4 * per)
                pe.wait_ge(inv_in[quarter], 64 * (n + 3))
                pe.wait_ge(cols_ready, UNITS * (n + 2) + share * unit)
                pe.matmul(ps_c[:, 0:2 * QC], i_h[:, :], inv[:, 2 * f:2 * f + 2, quarter * QC:(quarter + 1) * QC],
                          start=True, stop=True).then_inc(c_done, share)

            def step(b, n, buf, loads, width):
                units = 2 * width
                if buf is None:
                    pe.wait_ge(z0_in, 16 * loads)
                else:
                    pe.wait_ge(z_in[buf], 16 * loads)
                transform(n, 0, buf, width)
                for a in range(BP):
                    if a + 1 < BP:
                        transform(n, a + 1, buf, width)
                    hidden(b, n, a, buf, width)
                    if a:
                        second(n, a - 1, width)
                    if units == UNITS and a > LAG:
                        inverse(n, a - LAG - 1, width)
                second(n, BP - 1, width)
                for unit in range(BP - LAG - 1 if units == UNITS else 0, units):
                    inverse(n, unit, width)

            steps(pe, step)

        @block.scalar
        def _(act):
            def relu(n, a, width):
                act.wait_ge(v_done, BP * (n + 2) + max(a - 1, 0))
                for t in range(2):
                    act.wait_ge(h_done, HM * (BP * (n + 2) + a) + t + 1)
                    act.activation(hid[:, a % 2, t, 0:width * H], ps_h[:, t, 0:width * H], ACT.Relu,
                                   bias=b1[:, a, t:t + 1]).then_inc(hid_act, 1)

            def take_cols(n, unit, width):
                per = width // 2
                quarter, f = unit // per, unit % per
                share = UNITS // (4 * per)
                if unit == 0:
                    act.wait_ge(z2_out, 32 * (n + 2))
                act.wait_ge(c_done, UNITS * (n + 2) + share * (unit + 1))
                act.activation(cols[:, 2 * f:2 * f + 2, quarter * QC:(quarter + 1) * QC],
                               ps_c[:, 0:2 * QC].rearrange("p (f c) -> p f c", f=2), ACT.Copy).then_inc(cols_ready, share)

            def step(b, n, buf, loads, width):
                units = 2 * width
                for a in range(BP):
                    relu(n, a, width)
                    if units == UNITS and a > LAG:
                        take_cols(n, a - LAG - 1, width)
                for unit in range(BP - LAG - 1 if units == UNITS else 0, units):
                    take_cols(n, unit, width)

            act.wait_ge(var_ok, 1)
            act.activation(gt[:, :, :], gt[:, :, :], ACT.Sqrt).then_inc(root_ok, 1)
            act.wait_ge(w_in, 16 * 6)
            steps(act, step)

        @block.vector
        def _(dve):
            links = [0]

            def link(ins):
                links[0] += 1
                ins.then_inc(chain, 1)
                dve.wait_ge(chain, links[0])

            dve.memset(ones[:, :], 1.0).then_inc(ones_ok, 1)
            dve.wait_ge(stats_ok, 1)
            sums = ps_c[:, 0:NB * 2 * NG].rearrange("p (b m g) -> p b m g", b=NB, m=2)
            link(dve.tensor_scalar(gm[:, :, :], sums[:, :, 0, :], 1.0 / (GC * L), None, ALU.mult))
            link(dve.tensor_tensor(gt[:, :, :], gm[:, :, :], gm[:, :, :], ALU.mult))
            for b in range(NB):
                last = dve.scalar_tensor_tensor(gv[:, b, :], sums[:, b, 1, :], 1.0 / (GC * L), gt[:, b, :],
                                                ALU.mult, ALU.subtract)
            link(last)
            dve.tensor_scalar(gt[:, :, :], gv[:, :, :], 0.0, GN_EPS, ALU.max, ALU.add).then_inc(var_ok, 1)
            dve.wait_ge(root_ok, 1)
            link(dve.reciprocal(gv[:, :, :], gt[:, :, :]))
            for b in range(NB):
                last = dve.scalar_tensor_tensor(gm[:, b, :], gm[:, b, :], -float(H), gv[:, b, :], ALU.mult, ALU.mult)
            link(last)
            for table, out in ((gv, scale), (gm, shift)):
                pairs = table[:, :, :].rearrange("p b (a e) -> p b a e", e=2)
                link(dve.tensor_scalar(pick[:, :, :], pairs[:, :, :, 0], k.mask[:, 0:1], None, ALU.mult))
                for b in range(NB):
                    last = dve.scalar_tensor_tensor(out[:, b, :], pairs[:, b, :, 1], k.mask[:, 1:2], pick[:, b, :],
                                                    ALU.mult, ALU.add)
                link(last)
            dve.wait_ge(w_in, 16 * 6)
            im_re = w1[H:P, :, :].rearrange("p a (e r m) -> p (a e) r m", e=2, r=2)[:, :, 0, :]
            dve.tensor_scalar(im_re, im_re, -1.0, None, ALU.mult)
            for p0, p1, t in ((96, 128, 0), (0, 64, 1), (32, 64, 2), (64, 128, 2)):
                last = dve.tensor_scalar(w2[p0:p1, :, t, 0:PC], w2[p0:p1, :, t, 0:PC], -1.0, None, ALU.mult)
            last.then_inc(sign_ok, 1)

            def take_spec(b, n, a, buf, width):
                dve.wait_ge(f_done, BP * (n + 2) + a + 1)
                dve.wait_ge(h_done, HM * (BP * (n + 2) + max(a - 1, 0)))
                dve.tensor_scalar(spec[:, a % 2, 0:width * H], ps_f[:, a % 2, 0:width * H], scale[:, b, a:a + 1], None,
                                  ALU.mult).then_inc(spec_ready, 1)
                if buf is None:
                    dve.wait_ge(spec_ready, BP * (n + 2) + a + 1)
                    dve.tensor_scalar(spec[0:H, a % 2, 0:1], spec[0:H, a % 2, 0:1], shift[0:H, b, a:a + 1], None,
                                      ALU.add).then_inc(dc_done, 1)

            def relu(n, a, width):
                t = HM - 1
                dve.wait_ge(v_done, BP * (n + 2) + max(a - 1, 0))
                dve.wait_ge(h_done, HM * (BP * (n + 2) + a + 1))
                dve.tensor_scalar(hid[:, a % 2, t, 0:width * H], ps_h[:, t, 0:width * H], b1[:, a, t:t + 1], 0.0,
                                  ALU.add, ALU.max).then_inc(hid_dve, 1)

            def shrink(n, a, width):
                m = width // 2
                v, cl = val[:, a % 2, 0:m, :], clip[:, a % 2, 0:m, :]
                dve.wait_ge(v_done, BP * (n + 2) + a + 1)
                dve.wait_ge(shr_ready, BP * (n + 2) + max(a - 1, 0))
                dve.tensor_tensor(v, ps_v[:, a % 2, 0:m * 2 * PC].rearrange("p (f c) -> p f c", f=m),
                                  b2[:, a:a + 1, :].to_broadcast([P, m, 2 * PC]), ALU.add).then_inc(val_ready, 1)
                dve.wait_ge(val_ready, BP * (n + 2) + a + 1)
                dve.tensor_scalar(cl, v, -SHRINK, SHRINK, ALU.max, ALU.min).then_inc(clip_ready, 1)
                dve.wait_ge(clip_ready, BP * (n + 2) + a + 1)
                if a == 0:
                    for s in inv_in:
                        dve.wait_ge(s, 64 * (n + 2))
                dve.tensor_tensor(shr[:, 0:m, :, a * PC:(a + 1) * PC], v.rearrange("p f (r c) -> p f r c", r=2),
                                  cl.rearrange("p f (r c) -> p f r c", r=2), ALU.subtract).then_inc(shr_ready, 1)

            def step(b, n, buf, loads, width):
                take_spec(b, n, 0, buf, width)
                for a in range(BP):
                    if a + 1 < BP:
                        take_spec(b, n, a + 1, buf, width)
                    relu(n, a, width)
                    if a:
                        shrink(n, a - 1, width)
                shrink(n, BP - 1, width)

            steps(dve, step)


def last_stage(nc, d, k):
    with ExitStack() as ctx:
        def sb(name, shape):
            return ctx.enter_context(nc.sbuf_tensor(name, shape, F32))

        def sem(name):
            return ctx.enter_context(nc.semaphore(name))

        U = 2
        N = NB * L // (U * P)
        z = sb("last_z", [P, 2, U, C])
        x = sb("last_x", [P, 2, U, C])
        o = sb("last_o", [P, 2, U, C])
        i_w = sb("i_w", [P, P])
        ps = ctx.enter_context(nc.psum_tensor("ps_last", [P, 2, U, 2, 512], F32))
        m_in = sem("i_w_in")
        z_in = [sem(f"last_z_in{e}") for e in range(2)]
        x_in = [sem(f"last_x_in{e}") for e in range(2)]
        o_out = [sem(f"last_o_out{e}") for e in range(2)]
        back, summed = sem("last_back"), sem("last_summed")
        turn = sem("last_turn")
        block = ctx.enter_context(nc.Block())
        zs = d.z2.rearrange("b h q c -> (b h q) c").rearrange("(g t p) c -> g p t c", t=U, p=P)
        xx = d.x2.rearrange("(g t p) c -> g p t c", t=U, p=P)
        out = d.out.rearrange("(g t p) c -> g p t c", t=U, p=P)

        @block.gpsimd
        def _(pool):
            for s in (back, summed):
                pool.sem_inc(s, 2 * U)
            for e in range(2):
                pool.sem_inc(o_out[e], 16)

        @block.sync
        def _(sp):
            sp.dma_start(i_w[:, :], d.i_w).then_inc(m_in, 16)
            with sp.Fori(0, N // 2) as i:
                for e in range(2):
                    m = 2 * i + e
                    sp.wait_ge(back, U * (m + 1))
                    sp.sem_inc(turn, 1)
                    sp.dma_start(z[:, e, :, :], zs[m]).then_inc(z_in[e], 16)
                    sp.wait_ge(summed, U * (m + 1))
                    sp.sem_inc(turn, 1)
                    sp.dma_start(x[:, e, :, :], xx[m]).then_inc(x_in[e], 16)

        @block.tensor
        def _(pe):
            pe.wait_ge(m_in, 16)
            with pe.Fori(0, N // 2) as i:
                for e in range(2):
                    m = 2 * i + e
                    pe.wait_ge(z_in[e], 16 * (i + 1))
                    pe.wait_ge(summed, U * (m + 1))
                    for t in range(U):
                        for j in range(2):
                            last = pe.matmul(ps[:, e, t, j, 0:CH2], i_w[:, :], z[:, e, t, j * CH2:(j + 1) * CH2],
                                             start=True, stop=True)
                        last.then_inc(back, 1)

        @block.vector
        def _(dve):
            with dve.Fori(0, N // 2) as i:
                for e in range(2):
                    m = 2 * i + e
                    dve.wait_ge(x_in[e], 16 * (i + 1))
                    dve.wait_ge(o_out[e], 16 * (i + 1))
                    for t in range(U):
                        dve.wait_ge(back, U * (m + 2) + t + 1)
                        dve.tensor_tensor(o[:, e, t, :].rearrange("p (j c) -> p j c", j=2), ps[:, e, t, :, 0:CH2],
                                          x[:, e, t, :].rearrange("p (j c) -> p j c", j=2), ALU.add).then_inc(summed, 1)

        @block.scalar
        def _(act):
            with act.Fori(0, N // 2) as i:
                for e in range(2):
                    m = 2 * i + e
                    act.wait_ge(summed, U * (m + 3))
                    act.dma_start(out[m], o[:, e, :, :]).then_inc(o_out[e], 16)
            for e in range(2):
                act.wait_ge(o_out[e], 16 * (N // 2 + 1))


def build(nc, d):
    with ExitStack() as kept:
        k = Bufs()

        def keep(ctx, name, shape):
            return ctx.enter_context(nc.sbuf_tensor(name, shape, F32))

        k.sums = keep(kept, "sums", [P, NB, 2, NG])
        k.mask = keep(kept, "mask", [P, 2])
        with ExitStack() as first:
            k.w_in = keep(first, "w_in", [P, KT, DI])
            k.w_out = keep(first, "w_out", [P, DT, C])
            k.one = keep(first, "one", [P, 1])
            k.w_x = keep(first, "w_x", [P, DT, XR])
            k.w_dt = keep(first, "w_dt", [ONE + 1, DI])
            k.conv_w = keep(first, "conv_w", [P, DT, 9])
            k.conv_b = keep(first, "conv_b", [P, DT])
            k.d_par = keep(first, "d_par", [P, DT])
            k.a_neg = keep(first, "a_neg", [P, DT * NS])
            k.gn_scale = keep(first, "gn_scale", [P, KT, NB])
            k.gn_shift = keep(first, "gn_shift", [P, KT, NB])
            k.bv = keep(first, "bv", [P, C])
            k.ident = keep(first, "ident", [P, P])
            k.f_w = keep(first, "f_w", [P, P])
            k.xd = keep(first, "xd", [ONE + 1, T])
            setup_stage(nc, d, k)
            scan_stage(nc, d, k)
        mlp_stage(nc, d, k)
        last_stage(nc, d, k)


def constants():
    n = np.arange(H)
    angle = 2 * np.pi * np.outer(n, n) / H
    cos, sin = np.cos(angle), np.sin(angle)
    norm = 1 / np.sqrt(H)
    f = np.zeros((W, W))
    f[:, 0], f[:, 1] = 1, cos[:, W // 2]
    f[:, 2::2], f[:, 3::2] = cos[:, 1:W // 2], -sin[:, 1:W // 2]
    i = 2 * f.T
    i[0:2] /= 2
    two = np.eye(2)
    zero = np.zeros((H, H))
    f_h = np.stack([
        np.stack([np.vstack([cos, sin]), np.vstack([-sin, cos])], 1),
        np.stack([np.vstack([cos, zero]), np.vstack([-sin, zero])], 1),
        np.stack([np.vstack([zero, cos]), np.vstack([zero, -sin])], 1),
    ], 1)
    i_h = np.block([[cos, sin], [-sin, cos]])
    group = np.zeros((C, C))
    for g in range(NG):
        group[g * GC:(g + 1) * GC, g * GC:(g + 1) * GC] = 1 / GC
    first = (np.arange(P) % H < GC).astype(np.float64)
    tables = dict(
        f_w=np.kron(two, f) * norm, i_w=np.kron(two, i) * norm, f_h=f_h * norm, i_h=i_h * norm,
        group=group.reshape(KT, P, C).transpose(1, 0, 2), mask=np.stack([first, 1 - first], 1), ident=np.eye(P),
        zeros=np.zeros((ONE - RANK, DI)),
    )
    return {name: np.ascontiguousarray(a, dtype=np.float32) for name, a in tables.items()}


def layouts(x, L0_conv_in_proj_w, L0_conv_conv_w, L0_conv_conv_b, L0_conv_x_proj_w, L0_conv_dt_w, L0_conv_dt_b,
            L0_conv_A_log, L0_conv_D_param, L0_conv_ln_g, L0_conv_ln_b, L0_conv_out_proj_w, L1_conv_w1, L1_conv_b1,
            L1_conv_w2, L1_conv_b2):
    x = np.asarray(x)
    f32 = np.float32
    padded = np.zeros((NB, C, L + W), f32)
    padded[:, :, 0:L] = x.reshape(NB, C, L)

    def by_tile(a):
        a = np.asarray(a)
        return a.reshape(DT, P, -1).transpose(1, 0, 2)

    w1, b1 = np.asarray(L1_conv_w1), np.asarray(L1_conv_b1)
    w2, b2 = np.asarray(L1_conv_w2), np.asarray(L1_conv_b2)
    m1 = np.zeros((BP, P, 2, 2, HID), f32)
    m2 = np.zeros((BP, 2, 2, HID, 2, 2, GC), f32)
    v1 = np.zeros((BP, 2, 2, HID), f32)
    v2 = np.zeros((BP, 2, 2, GC), f32)
    for a in range(BP):
        for e in range(2):
            g = 2 * a + e
            for r in range(2):
                m1[a, e * GC:(e + 1) * GC, e, r] = w1[0, g]
                m1[a, H + e * GC:H + (e + 1) * GC, e, r] = w1[1, g]
                m2[a, e, 0, :, r, e] = w2[0, g]
                m2[a, e, 1, :, r, e] = w2[1, g]
                v1[a, e, r] = b1[r, g]
                v2[a, r, e] = b2[r, g]
    return dict(
        x=padded, x_tok=x.transpose(0, 2, 3, 1).reshape(NB * L, C),
        w_in=np.asarray(L0_conv_in_proj_w).T, w_out=np.asarray(L0_conv_out_proj_w).T,
        w_x=np.asarray(L0_conv_x_proj_w).T, w_dt=np.asarray(L0_conv_dt_w)[0].T, dt_b=np.asarray(L0_conv_dt_b),
        conv_w=by_tile(np.asarray(L0_conv_conv_w).reshape(DI, 9)), conv_b=by_tile(L0_conv_conv_b)[:, :, 0],
        d_par=by_tile(L0_conv_D_param)[:, :, 0], a_log=by_tile(L0_conv_A_log).reshape(P, DT * NS),
        ln_g=by_tile(L0_conv_ln_g)[:, :, 0], ln_b=by_tile(L0_conv_ln_b)[:, :, 0],
        mlp_w1=m1.reshape(BP, P, HM * P).transpose(1, 0, 2),
        mlp_w2=m2.reshape(BP, HM, P, 2 * PC).transpose(2, 0, 1, 3),
        mlp_b1=v1.reshape(BP, HM, P).transpose(2, 0, 1), mlp_b2=v2.reshape(1, BP * 2 * PC),
    )


def kernel(**inputs):
    import concourse.bacc as bacc
    from concourse.bass_utils import run_bass_kernel_spmd

    nc = bacc.Bacc("TRN2", target_bir_lowering=False, num_devices=1)
    d = Bufs()
    arrays = {}
    for name, a in {**layouts(**inputs), **constants()}.items():
        arrays[f"in_{name}"] = np.ascontiguousarray(a)
        ap = nc.dram_tensor(f"in_{name}", a.shape, F32, kind="ExternalInput").ap()
        d.__dict__[name] = ap
    d.x2 = nc.dram_tensor("x2", (NB * L, C), F32, kind="Internal").ap()
    d.z1 = nc.dram_tensor("z1", (NB, W, H, C), F32, kind="Internal").ap()
    d.z2 = nc.dram_tensor("z2", (NB, H, W, C), F32, kind="Internal").ap()
    d.out = nc.dram_tensor("out_tok", (NB * L, C), F32, kind="ExternalOutput").ap()
    build(nc, d)
    r = run_bass_kernel_spmd(nc, [arrays], core_ids=[0])
    return r.results[0]["out_tok"].reshape(NB, H, W, C).transpose(0, 3, 1, 2)
```

```python
from contextlib import ExitStack

import numpy as np

import concourse.bass as bass
from concourse import mybir

F32 = mybir.dt.float32
ALU = mybir.AluOpType
ACT = mybir.ActivationFunctionType
AX = mybir.AxisListType

P = 128
NB, C, H, W = 2, 768, 64, 64
L = H * W
DI = 2 * C
NS = 4
RANK = C // 16
KT = C // P
DT = DI // P
NP = DT // 2
ROWS = 4
T = ROWS * W
NCH = H // ROWS
TT = T // P
XR = RANK + 2 * NS
ONE = 64
NG = 32
GC = C // NG
BP = NG // 2
PC = 2 * GC
HID = 4 * GC
HM = 4 * HID // P
KW = 8
NST = W // 2 // KW
SHRINK = 0.01
GN_EPS = 1e-5
LN_EPS = 1e-5
CH2 = C // 2


class Bufs:
    pass


def setup_stage(nc, d, k):
    with ExitStack() as ctx:
        def sb(name, shape):
            return ctx.enter_context(nc.sbuf_tensor(name, shape, F32))

        def sem(name):
            return ctx.enter_context(nc.semaphore(name))

        NX = 2
        xbuf = sb("setup_x", [P, NX, L])
        group = sb("setup_group", [P, KT, C])
        stats = sb("setup_stats", [P, L // 512, 6])
        agg = sb("setup_agg", [P, KT, NB, 2])
        moments = sb("setup_moments", [P, KT, NB, 2])
        lng = sb("setup_lng", [P, DT])
        lnb = sb("setup_lnb", [P, DT])
        alog = sb("setup_alog", [P, DT * NS])
        spread = sb("setup_spread", [P, DT, P])
        mean_of = sb("setup_mean_of", [P, P])
        gsum = sb("setup_gsum", [P, C])
        gmean = sb("setup_gmean", [P, KT * NB])
        gvar = sb("setup_gvar", [P, KT * NB])
        gsq = sb("setup_gsq", [P, KT * NB])
        ps_group = ctx.enter_context(nc.psum_tensor("ps_group", [P, 512], F32))
        ps_bv = ctx.enter_context(nc.psum_tensor("ps_bv", [P, 2, 512], F32))
        ps_g = ctx.enter_context(nc.psum_tensor("ps_g", [P, 2, 512], F32))

        x_in = [sem(f"setup_x_in{n}") for n in range(NX)]
        w_in = sem("setup_w_in")
        wo_in = sem("setup_wo_in")
        x_used = sem("setup_x_used")
        stat = sem("setup_stat")
        chain = sem("setup_chain")
        moments_ok = sem("setup_moments_ok")
        grouped = sem("setup_grouped")
        spread_ok = sem("setup_spread_ok")
        bv_ok = sem("setup_bv_ok")
        bv_out = sem("setup_bv_out")
        scaled = sem("setup_scaled")
        g_ok = sem("setup_g_ok")
        exp_ok = sem("setup_exp_ok")
        var_ok, root_ok = sem("setup_var_ok"), sem("setup_root_ok")
        block = ctx.enter_context(nc.Block())

        tiles = [(b, t) for b in range(NB) for t in range(KT)]

        @block.sync
        def _(sp):
            for n, (b, t) in enumerate(tiles):
                if n >= NX:
                    sp.wait_ge(x_used, n - NX + 1)
                sp.dma_start(xbuf[:, n % NX, :], d.x[b, t * P:(t + 1) * P, 0:L]).then_inc(x_in[n % NX], 16)
            sp.wait_ge(w_in, 16 * 12)

        @block.scalar
        def _(act):
            wo = d.w_out.rearrange("(t p) c -> p t c", p=P)
            act.dma_start(k.w_out[:, :, 0:CH2], wo[:, :, 0:CH2]).then_inc(wo_in, 16)
            act.dma_start(k.w_out[:, :, CH2 + 1:C + 1], wo[:, :, CH2:C]).then_inc(wo_in, 16)
            act.dma_start(lng[:, :], d.ln_g).then_inc(wo_in, 16)
            act.dma_start(lnb[:, :], d.ln_b).then_inc(wo_in, 16)
            act.dma_start(alog[:, :], d.a_log).then_inc(wo_in, 16)
            act.dma_start(group[:, :, :], d.group).then_inc(wo_in, 16)
            act.dma_start(k.w_in[:, :, :], d.w_in.rearrange("(t p) m -> p t m", p=P)).then_inc(w_in, 16)
            act.dma_start(k.w_x[:, :, :], d.w_x.rearrange("(t p) m -> p t m", p=P)).then_inc(w_in, 16)
            act.dma_start(k.w_dt[0:RANK, :], d.w_dt).then_inc(w_in, 16)
            act.dma_start(k.w_dt[ONE:ONE + 1, :], d.dt_b).then_inc(w_in, 16)
            act.dma_start(k.w_dt[RANK:ONE, :], d.zeros).then_inc(w_in, 16)
            act.dma_start(k.conv_w[:, :, :], d.conv_w).then_inc(w_in, 16)
            act.dma_start(k.conv_b[:, :], d.conv_b).then_inc(w_in, 16)
            act.dma_start(k.d_par[:, :], d.d_par).then_inc(w_in, 16)
            act.dma_start(k.ident[:, :], d.ident).then_inc(w_in, 16)
            act.dma_start(k.f_w[:, :], d.f_w).then_inc(w_in, 16)
            act.dma_start(k.mask[:, :], d.mask).then_inc(w_in, 16)
            act.dma_start(k.xd[RANK:ONE, :], d.zeros[:, 0:T]).then_inc(w_in, 16)
            act.wait_ge(wo_in, 16 * 6)
            act.activation(k.a_neg[:, :], alog[:, :], ACT.Exp).then_inc(exp_ok, 1)
            act.wait_ge(var_ok, 1)
            act.activation(gsq[:, :], gvar[:, :], ACT.Sqrt).then_inc(root_ok, 1)

        @block.vector
        def _(dve):
            steps = [0]

            def link(ins):
                steps[0] += 1
                ins.then_inc(chain, 1)
                dve.wait_ge(chain, steps[0])

            dve.memset(k.xd[ONE:ONE + 1, :], 1.0)
            dve.memset(k.one[:, :], 1.0)
            dve.memset(k.w_out[:, :, CH2:CH2 + 1], 1.0)
            dve.memset(mean_of[:, :], 1.0 / DI)
            dve.memset(spread[:, :, :], 1.0).then_inc(spread_ok, 1)
            dve.wait_ge(spread_ok, 1)
            dve.wait_ge(wo_in, 16 * 6)
            for t in range(DT):
                last = dve.tensor_scalar(spread[:, t, :], spread[:, t, :], lnb[:, t:t + 1], None, ALU.mult)
            last.then_inc(spread_ok, 1)
            dve.wait_ge(exp_ok, 1)
            link(dve.tensor_scalar(k.a_neg[:, :], k.a_neg[:, :], -1.0, None, ALU.mult))
            dve.wait_ge(bv_ok, 1)
            for j in range(2):
                last = dve.tensor_copy(k.bv[:, j * CH2:(j + 1) * CH2], ps_bv[:, j, 0:CH2])
            last.then_inc(bv_out, 1)
            for t in range(DT):
                for j in range(2):
                    half = k.w_out[:, t, j * (CH2 + 1):j * (CH2 + 1) + CH2]
                    last = dve.tensor_scalar(half, half, lng[:, t:t + 1], None, ALU.mult)
            last.then_inc(scaled, 1)
            dve.wait_ge(g_ok, 1)
            link(dve.tensor_copy(gsum[:, :].rearrange("p (j c) -> p j c", j=2), ps_g[:, :, 0:CH2]))
            for t in range(DT):
                for j in range(2):
                    half = k.w_out[:, t, j * (CH2 + 1):j * (CH2 + 1) + CH2]
                    last = dve.tensor_tensor(half, half, gsum[:, j * CH2:(j + 1) * CH2], ALU.subtract)
            link(last)
            for n, (b, t) in enumerate(tiles):
                dve.wait_ge(x_in[n % NX], 16 * (n // NX + 1))
                if n:
                    dve.wait_ge(stat, n)
                for j in range(L // 512):
                    last = dve.bn_stats(stats[:, j, :], xbuf[:, n % NX, j * 512:(j + 1) * 512])
                last.then_inc(x_used, 1)
                dve.wait_ge(x_used, n + 1)
                dve.bn_aggr(agg[:, t, b, :], stats[:, :, :]).then_inc(stat, 1)
            dve.wait_ge(stat, len(tiles))
            mean, var = agg[:, :, :, 0], agg[:, :, :, 1]
            link(dve.tensor_tensor(moments[:, :, :, 1], mean, mean, ALU.mult))
            link(dve.tensor_tensor(moments[:, :, :, 1], moments[:, :, :, 1], var, ALU.add))
            dve.tensor_copy(moments[:, :, :, 0], mean).then_inc(moments_ok, 1)
            dve.wait_ge(grouped, 1)
            both = ps_group[:, 0:KT * NB * 2].rearrange("p (t b m) -> p (t b) m", b=NB, m=2)
            link(dve.tensor_copy(gmean[:, :], both[:, :, 0]))
            link(dve.tensor_tensor(gsq[:, :], gmean[:, :], gmean[:, :], ALU.mult))
            link(dve.tensor_tensor(gvar[:, :], both[:, :, 1], gsq[:, :], ALU.subtract))
            dve.tensor_scalar(gvar[:, :], gvar[:, :], 0.0, GN_EPS, ALU.max, ALU.add).then_inc(var_ok, 1)
            rs = k.gn_scale[:, :, :].rearrange("p t b -> p (t b)")
            nb = k.gn_shift[:, :, :].rearrange("p t b -> p (t b)")
            dve.wait_ge(root_ok, 1)
            link(dve.reciprocal(rs, gsq[:, :]))
            link(dve.scalar_tensor_tensor(nb, gmean[:, :], -1.0, rs, ALU.mult, ALU.mult))

        @block.tensor
        def _(pe):
            pe.wait_ge(spread_ok, 2)
            for t in range(DT):
                for j in range(2):
                    last = pe.matmul(ps_bv[:, j, 0:CH2], spread[:, t, :], k.w_out[:, t, j * (CH2 + 1):j * (CH2 + 1) + CH2],
                                     start=(t == 0), stop=(t == DT - 1))
            last.then_inc(bv_ok, 1)
            pe.wait_ge(scaled, 1)
            for t in range(DT):
                for j in range(2):
                    last = pe.matmul(ps_g[:, j, 0:CH2], mean_of[:, :], k.w_out[:, t, j * (CH2 + 1):j * (CH2 + 1) + CH2],
                                     start=(t == 0), stop=(t == DT - 1))
            last.then_inc(g_ok, 1)
            pe.wait_ge(moments_ok, 1)
            n = NB * 2
            for c in range(KT):
                for t in range(KT):
                    last = pe.matmul(ps_group[:, c * n:(c + 1) * n], group[:, t, c * P:(c + 1) * P],
                                     moments[:, t, :, :], start=(t == 0), stop=(t == KT - 1))
            last.then_inc(grouped, 1)


class Chunk:

    def __init__(self, c, b=None, i=None, odd=None):
        self.c = c
        self.b = (c - 1) // NCH if b is None else b
        self.i = (c - 1) % NCH if i is None else i
        self.odd = c % 2 if odd is None else odd
        fixed = isinstance(c, int)
        self.fixed = fixed
        self.there = not fixed or 1 <= c <= NB * NCH
        self.first = fixed and self.there and self.i == 0
        self.last = fixed and self.there and self.i == NCH - 1
        self.rows = ROWS - 1 if self.last else ROWS

    def __add__(self, n):
        if self.fixed:
            return Chunk(self.c + n)
        return Chunk(self.c + n, self.b, self.i + n, (self.odd + n) % 2)


def chunk_loop(engine, body):
    for b in range(NB):
        start = NCH * b + 1
        body(Chunk(start))
        with engine.Fori(0, (NCH - 4) // 2) as r:
            for e in range(2):
                i = 2 * r + (1 + e)
                body(Chunk(2 * r + (start + 1 + e), b, i, (start + 1 + e) % 2))
        for i in range(NCH - 3, NCH):
            body(Chunk(start + i))


def scan_stage(nc, d, k):
    with ExitStack() as ctx:
        def sb(name, shape):
            return ctx.enter_context(nc.sbuf_tensor(name, shape, F32))

        def pb(name, shape):
            return ctx.enter_context(nc.psum_tensor(name, shape, F32))

        def sem(name):
            return ctx.enter_context(nc.semaphore(name))

        RING = 3
        xn = sb("xn", [P, KT, T])
        x0 = sb("x0", [P, KT, W])
        xs = sb("xs", [P, DT, ROWS + 2, W])
        u = sb("u", [P, 2, DT, T])
        y = sb("y", [P, RING, 2, T])
        ysq = sb("ysq", [P, 2, 2, T])
        bc = sb("bc", [P, 2 * NS, T])
        q = sb("q", [P, 2, T])
        delta = sb("delta", [P, 2, T])
        du = sb("du", [P, 2, T])
        da = sb("da", [P, 2, NS, T + 1])
        st = sb("st", [P, 2, NS, T + 1])
        carry = sb("carry", [P, DT, NS])
        xt = sb("xt", [P, TT, C])
        f1o = sb("f1o", [P, TT, C])
        zsq = sb("zsq", [P, C])
        ln = sb("ln", [P, 4, TT])

        ps_o = pb("ps_o", [P, TT, 2, 512])
        ps_i = pb("ps_i", [P, 512])
        ps_d = pb("ps_d", [P, 512])
        ps_x = pb("ps_x", [P, 512])
        ps_y = pb("ps_y", [P, 512])

        x_in, x0_in, xt_in = sem("x_in"), sem("x0_in"), sem("xt_in")
        x_normed, x0_normed = sem("x_normed"), sem("x0_normed")
        in_done, in0_done = sem("in_done"), sem("in0_done")
        xs_ready, xs0_ready, xs_moved, xs_zero = sem("xs_ready"), sem("xs0_ready"), sem("xs_moved"), sem("xs_zero")
        centre_done, tap_done, u_ready = sem("centre_done"), sem("tap_done"), sem("u_ready")
        xp_done, xd_ready, bc_done, bc_ready = sem("xp_done"), sem("xd_ready"), sem("bc_done"), sem("bc_ready")
        dt_done, abs_done, exp_done, q_ready = sem("dt_done"), sem("abs_done"), sem("exp_done"), sem("q_ready")
        delta_ready, du_ready, da_ready, dbu_ready = sem("delta_ready"), sem("du_ready"), sem("da_ready"), sem("dbu_ready")
        scan_done, carry_kept, carry_zero, yc_done = sem("scan_done"), sem("carry_kept"), sem("carry_zero"), sem("yc_done")
        half_done, sum_done, y_ready, y_used = sem("half_done"), sem("sum_done"), sem("y_ready"), sem("y_used")
        ysq_ready, ysq_done = sem("ysq_ready"), sem("ysq_done")
        ln_step, var_ready, log_ready, rstd_ready = sem("ln_step"), sem("var_ready"), sem("log_ready"), sem("rstd_ready")
        xb_ready, z_ready, zsq_ready, zst_done, zst_kept = sem("xb_ready"), sem("z_ready"), sem("zsq_ready"), sem("zst_done"), sem("zst_kept")
        f1_done, f1_ready = sem("f1_done"), sem("f1_ready")
        x2_out, z1_out = sem("x2_out"), sem("z1_out")
        turn = sem("turn")
        per_chunk = [
            (in_done, NP), (xs_ready, NP), (xs_moved, NP), (centre_done, NP), (u_ready, NP), (dt_done, NP),
            (abs_done, NP), (exp_done, NP), (q_ready, NP), (delta_ready, NP), (du_ready, NP), (da_ready, NP),
            (dbu_ready, NP), (scan_done, NP), (carry_kept, NP), (yc_done, NP), (half_done, NP), (sum_done, NP),
            (y_ready, NP), (y_used, NP), (ysq_ready, NP), (ysq_done, NP), (tap_done, 16 * NP), (bc_done, NS), (bc_ready, NS),
            (z_ready, TT), (zsq_ready, TT), (zst_done, TT), (f1_done, TT), (f1_ready, TT),
            (ln_step, 3), (var_ready, 1), (log_ready, 1), (rstd_ready, 1), (zst_kept, 1),
            (x_normed, 1), (xp_done, 1), (xd_ready, 1), (xb_ready, 1),
            (x_in, 16), (xt_in, 16), (x2_out, 16), (z1_out, 32),
        ]
        block = ctx.enter_context(nc.Block())

        x_chunks = d.x[:, :, W:W + L].rearrange("b (t p) (i n) -> b i p t n", p=P, n=T)
        xt_chunks = d.x_tok.rearrange("(g t p) c -> g p t c", t=TT, p=P)
        x2_chunks = d.x2.rearrange("(g t p) c -> g p t c", t=TT, p=P)
        z1_chunks = d.z1.rearrange("b q (i t h) c -> b i h q t c", t=TT, h=2)
        END = Chunk(NB * NCH)

        @block.sync
        def _(sp):
            def load_x(ch):
                if ch.c > 1 if ch.fixed else True:
                    sp.wait_ge(in_done, NP * ch.c)
                    sp.sem_inc(turn, 1)
                sp.dma_start(xn[:, :, :], x_chunks[ch.b, ch.i]).then_inc(x_in, 16)

            def load_x0(b):
                sp.dma_start(x0[:, :, :], d.x[b, :, 0:W].rearrange("(t p) w -> p t w", p=P)).then_inc(x0_in, 16)

            def store(ch):
                sp.wait_ge(z_ready, TT * ch.c + TT)
                sp.sem_inc(turn, 1)
                sp.dma_start(x2_chunks[ch.c - 1], xt[:, :, :]).then_inc(x2_out, 16)
                sp.wait_ge(f1_ready, TT * ch.c + TT)
                sp.sem_inc(turn, 1)
                for h in range(2):
                    sp.dma_start(z1_chunks[ch.b, ch.i, h], f1o[h * W:(h + 1) * W, :, :]).then_inc(z1_out, 16)

            def body(ch):
                if (ch + -1).there:
                    store(ch + -1)
                sp.wait_ge(x2_out, 16 * ch.c)
                sp.sem_inc(turn, 1)
                sp.wait_ge(zst_done, TT * ch.c)
                sp.sem_inc(turn, 1)
                sp.wait_ge(f1_done, TT * ch.c)
                sp.sem_inc(turn, 1)
                sp.dma_start(xt[:, :, :], xt_chunks[ch.c - 1]).then_inc(xt_in, 16)
                if (ch + 3).first:
                    sp.wait_ge(in0_done, NP * (ch + 3).b)
                    load_x0((ch + 3).b)
                if (ch + 3).there:
                    load_x(ch + 3)

            load_x0(0)
            for c in range(1, 4):
                load_x(Chunk(c))
            chunk_loop(sp, body)
            store(END)
            sp.wait_ge(x2_out, 16 * (END.c + 1))
            sp.wait_ge(z1_out, 32 * (END.c + 1))

        @block.tensor
        def _(pe):
            def in_proj(ch, p):
                pe.wait_ge(xs_ready, NP * ch.c + p)
                if p == 0:
                    pe.wait_ge(x_normed, ch.c + 1)
                if ch.first:
                    if p == 0:
                        pe.wait_ge(x0_normed, ch.b + 1)
                    for j in range(2):
                        m = (2 * p + j) * P
                        for t in range(KT):
                            last = pe.matmul(ps_i[:, j * T:j * T + W], k.w_in[:, t, m:m + P], x0[:, t, :],
                                             start=(t == 0), stop=(t == KT - 1))
                    last.then_inc(in0_done, 1)
                    pe.wait_ge(xs0_ready, NP * ch.b + p + 1)
                n = ch.rows * W
                for j in range(2):
                    m = (2 * p + j) * P
                    for t in range(KT):
                        last = pe.matmul(ps_i[:, j * T:j * T + n], k.w_in[:, t, m:m + P], xn[:, t, 0:n],
                                         start=(t == 0), stop=(t == KT - 1))
                last.then_inc(in_done, 1)

            def x_proj(ch, p):
                if p == 0:
                    pe.wait_ge(bc_ready, NS * ch.c)
                    if not ch.fixed or ch.c > 1:
                        pe.wait_ge(zst_kept, ch.c - 1)
                pe.wait_ge(u_ready, NP * ch.c + p + 1)
                for j in range(2):
                    t = 2 * p + j
                    last = pe.matmul(ps_x[0:XR, 0:T], k.w_x[:, t, :], u[:, ch.odd, t, :], start=(t == 0), stop=(t == DT - 1))
                if p == NP - 1:
                    last.then_inc(xp_done, 1)

            def step(ch, p):
                if p == 0:
                    pe.wait_ge(xd_ready, ch.c + 1)
                pe.wait_ge(delta_ready, NP * ch.c + p)
                for j in range(2):
                    m = (2 * p + j) * P
                    last = pe.matmul(ps_d[:, j * T:(j + 1) * T], k.w_dt[0:ONE + 1, m:m + P],
                                     k.xd[0:ONE + 1, :], start=True, stop=True)
                last.then_inc(dt_done, 1)

            def spread_bc(ch, r):
                if r == 0:
                    pe.wait_ge(xd_ready, ch.c + 1)
                pe.wait_ge(bc_ready, NS * ch.c + r)
                for j in range(2):
                    row = RANK + 2 * r + j
                    last = pe.matmul(ps_x[:, j * T:(j + 1) * T], k.ident[0:XR, row:row + 1].to_broadcast([XR, P]),
                                     k.xd[0:XR, :], start=True, stop=True)
                last.then_inc(bc_done, 1)

            def square_sums(ch, p):
                pe.wait_ge(ysq_ready, NP * ch.c + p + 1)
                if p == 0:
                    pe.wait_ge(var_ready, ch.c)
                for j in range(2):
                    for tt in range(TT):
                        last = pe.matmul(ps_y[:, tt:tt + 1], ysq[:, p % 2, j, tt * P:(tt + 1) * P], k.one[:, :],
                                         start=(p == 0 and j == 0 and tt == 0), stop=(p == NP - 1 and j == 1),
                                         skip_group_check=True)
                last.then_inc(ysq_done, 1)

            def out_proj(ch, p):
                pe.wait_ge(y_ready, NP * ch.c + p + 1)
                if p == 0:
                    pe.wait_ge(f1_ready, TT * ch.c)
                for j in range(2):
                    t = 2 * p + j
                    for tt in range(TT):
                        lhs = y[:, p % RING, j, tt * P:(tt + 1) * P]
                        pe.matmul(ps_o[:, tt, 0, 0:CH2 + 1], lhs, k.w_out[:, t, 0:CH2 + 1],
                                  start=(t == 0), stop=(t == DT - 1))
                        last = pe.matmul(ps_o[:, tt, 1, 0:CH2], lhs, k.w_out[:, t, CH2 + 1:C + 1],
                                         start=(t == 0), stop=(t == DT - 1))
                last.then_inc(y_used, 1)

            def transform(ch, tt):
                pe.wait_ge(z_ready, TT * ch.c + tt + 1)
                for j in range(2):
                    last = pe.matmul(ps_o[:, tt, j, 0:CH2], k.f_w[:, :], xt[:, tt, j * CH2:(j + 1) * CH2],
                                     start=True, stop=True)
                last.then_inc(f1_done, 1)

            def result_sums(ch):
                after = ch + 1
                pe.wait_ge(bc_ready, NS * after.c + (NS if after.there else 0))
                for tt in range(TT):
                    for m in range(2):
                        if m:
                            pe.wait_ge(zsq_ready, TT * ch.c + tt + 1)
                        for t in range(KT):
                            cut = slice(t * P, (t + 1) * P)
                            last = pe.matmul(ps_x[:, m * KT + t:m * KT + t + 1], zsq[:, cut] if m else xt[:, tt, cut], k.one[:, :],
                                             start=(tt == 0 and m == 0 and t == 0), stop=(tt == TT - 1), skip_group_check=True)
                    last.then_inc(zst_done, 1)

            def body(ch):
                prev, nxt, far = ch + -1, ch + 1, ch + 2

                def project(p, late=False):
                    if far.there and late == (far.first and p in (1, 4, 5)):
                        in_proj(far, p)

                if prev.there:
                    out_proj(prev, NP - 1)
                    square_sums(prev, NP - 1)
                step(ch, 2)
                project(0)
                step(ch, 3)
                project(1)
                if prev.there:
                    transform(prev, 0)
                    transform(prev, 1)
                    result_sums(prev)
                project(1, late=True)
                out_proj(ch, 0)
                square_sums(ch, 0)
                step(ch, 4)
                project(2)
                out_proj(ch, 1)
                square_sums(ch, 1)
                step(ch, 5)
                project(3)
                out_proj(ch, 2)
                project(4)
                if nxt.there:
                    for p in range(NP):
                        x_proj(nxt, p)
                square_sums(ch, 2)
                if nxt.there:
                    step(nxt, 0)
                    spread_bc(nxt, 0)
                out_proj(ch, 3)
                if nxt.there:
                    spread_bc(nxt, 1)
                square_sums(ch, 3)
                project(4, late=True)
                project(5)
                if nxt.there:
                    spread_bc(nxt, 2)
                    step(nxt, 1)
                    spread_bc(nxt, 3)
                out_proj(ch, 4)
                square_sums(ch, 4)
                project(5, late=True)

            one, two = Chunk(1), Chunk(2)
            for p in range(NP):
                in_proj(one, p)
            for p in range(NP):
                x_proj(one, p)
            step(one, 0)
            for r in range(NS):
                spread_bc(one, r)
            for p in range(NP):
                in_proj(two, p)
            step(one, 1)
            chunk_loop(pe, body)
            out_proj(END, NP - 1)
            square_sums(END, NP - 1)
            for tt in range(TT):
                transform(END, tt)
            result_sums(END)

        @block.scalar
        def _(act):
            def norm(ch):
                act.wait_ge(x_in, 16 * (ch.c + 1))
                tiles = [(xn, x_normed)]
                if ch.first:
                    act.wait_ge(x0_in, 16 * (ch.b + 1))
                    tiles.append((x0, x0_normed))
                for tile, done in tiles:
                    for t in range(KT):
                        last = act.activation(tile[:, t, :], tile[:, t, :], ACT.Identity,
                                              bias=k.gn_shift[:, t, ch.b:ch.b + 1], scale=k.gn_scale[:, t, ch.b:ch.b + 1])
                    last.then_inc(done, 1)

            def take_xs(ch, p):
                a, e = 2 * p, 2 * p + 2
                act.wait_ge(tap_done, 16 * (NP * (ch.c - 1) + p + 1))
                if ch.first:
                    act.sem_inc(xs_moved, 1)
                    act.wait_ge(in0_done, NP * ch.b + p + 1)
                    act.activation(xs[:, a:e, 1, :], ps_i[:, :].rearrange("p (j r w) -> p j r w", j=2, w=W)[:, :, 0, :],
                                   ACT.Copy).then_inc(xs0_ready, 1)
                else:
                    act.activation(xs[:, a:e, 0:2, :], xs[:, a:e, ROWS:ROWS + 2, :], ACT.Copy).then_inc(xs_moved, 1)
                    act.wait_ge(xs_moved, NP * ch.c + p + 1)
                act.wait_ge(in_done, NP * ch.c + p + 1)
                act.activation(xs[:, a:e, 2:2 + ch.rows, :],
                               ps_i[:, :].rearrange("p (j r w) -> p j r w", j=2, w=W)[:, :, 0:ch.rows, :],
                               ACT.Copy).then_inc(xs_ready, 1)

            def centre(ch, p):
                if not ch.fixed or ch.c > 1:
                    act.wait_ge(y_ready, NP * (ch.c - 2) + p + 1)
                act.wait_ge(xs_ready, NP * ch.c + p + 1)
                for t in (2 * p, 2 * p + 1):
                    last = act.activation(u[:, ch.odd, t, :], xs[:, t, 1:1 + ROWS, :], ACT.Identity,
                                          bias=k.conv_b[:, t:t + 1], scale=k.conv_w[:, t, 4:5])
                last.then_inc(centre_done, 1)

            def silu(ch):
                for p in range(NP):
                    act.wait_ge(tap_done, 16 * (NP * ch.c + p + 1))
                    v = u[:, ch.odd, 2 * p:2 * p + 2, :]
                    act.activation(v, v, ACT.Silu).then_inc(u_ready, 1)
                act.preload_act_table_set("natural_log_exp_and_others")

            def take_xd(ch):
                act.wait_ge(xp_done, ch.c + 1)
                act.wait_ge(dt_done, NP * ch.c)
                act.wait_ge(bc_done, NS * ch.c)
                act.activation(k.xd[0:XR, :], ps_x[0:XR, 0:T], ACT.Copy).then_inc(xd_ready, 1)

            def take_bc(ch, r):
                if r < NS // 2:
                    act.wait_ge(dbu_ready, NP * ch.c)
                else:
                    act.wait_ge(yc_done, NP * ch.c)
                act.wait_ge(bc_done, NS * ch.c + r + 1)
                act.activation(bc[:, 2 * r:2 * r + 2, :].rearrange("p j n -> p (j n)"), ps_x[:, :], ACT.Copy).then_inc(bc_ready, 1)

            def log_part(ch, p):
                n = NP * ch.c + p
                act.wait_ge(dt_done, n + 1)
                act.wait_ge(delta_ready, n)
                v = q[:, :, :].rearrange("p j n -> p (j n)")
                act.activation(v, ps_d[:, :], ACT.Abs).then_inc(abs_done, 1)
                act.wait_ge(abs_done, n + 1)
                act.activation(v, v, ACT.Exp, scale=-1.0).then_inc(exp_done, 1)
                act.wait_ge(exp_done, n + 1)
                act.activation(v, v, ACT.Ln, bias=1.0).then_inc(q_ready, 1)

            def decay(ch, p):
                act.wait_ge(delta_ready, NP * ch.c + p + 1)
                act.wait_ge(scan_done, NP * ch.c + p)
                for j in range(2):
                    for n in range(NS):
                        a = (2 * p + j) * NS + n
                        last = act.activation(da[:, j, n, 1:T + 1], delta[:, j, :], ACT.Exp, scale=k.a_neg[:, a:a + 1])
                last.then_inc(da_ready, 1)

            def square(ch, p):
                act.wait_ge(y_ready, NP * ch.c + p + 1)
                act.wait_ge(ysq_done, NP * ch.c + p - 1)
                act.activation(ysq[:, p % 2, :, :], y[:, p % RING, :, :], ACT.Square).then_inc(ysq_ready, 1)

            def inverse_deviation(ch):
                act.wait_ge(var_ready, ch.c + 1)
                act.activation(ln[:, 3, :], ln[:, 2, :], ACT.Ln).then_inc(log_ready, 1)
                act.wait_ge(log_ready, ch.c + 1)
                act.activation(ln[:, 3, :], ln[:, 3, :], ACT.Exp, scale=-0.5).then_inc(rstd_ready, 1)

            def square_result(ch, tt):
                act.wait_ge(z_ready, TT * ch.c + tt + 1)
                act.wait_ge(zst_done, TT * ch.c + tt)
                act.activation(zsq[:, :], xt[:, tt, :], ACT.Square).then_inc(zsq_ready, 1)

            def take_transform(ch, tt):
                act.wait_ge(f1_done, TT * ch.c + tt + 1)
                if tt == 0:
                    act.wait_ge(z1_out, 32 * ch.c)
                act.activation(f1o[:, tt, :].rearrange("p (j c) -> p j c", j=2), ps_o[:, tt, :, 0:CH2],
                               ACT.Copy).then_inc(f1_ready, 1)

            def finish(ch):
                for tt in range(TT):
                    take_transform(ch, tt)
                for tt in range(TT):
                    square_result(ch, tt)

            def body(ch):
                prev, nxt, far = ch + -1, ch + 1, ch + 2
                if nxt.there:
                    take_xs(nxt, 5)
                    centre(nxt, 5)
                if prev.there:
                    square(prev, 5)
                if far.there:
                    norm(far)
                act.preload_act_table_set("natural_log_exp_and_others")
                decay(ch, 1)
                log_part(ch, 2)
                if prev.there:
                    inverse_deviation(prev)
                for p in range(1, 4):
                    square(ch, p - 1)
                    if far.there:
                        take_xs(far, p - 1)
                        centre(far, p - 1)
                    decay(ch, p + 1)
                    log_part(ch, p + 2)
                    if p == 1 and prev.there:
                        finish(prev)
                if far.there:
                    take_xs(far, 3)
                if nxt.there:
                    silu(nxt)
                square(ch, 3)
                decay(ch, 5)
                if nxt.there:
                    take_xd(nxt)
                    log_part(nxt, 0)
                if far.there:
                    centre(far, 3)
                if nxt.there:
                    take_bc(nxt, 0)
                    take_bc(nxt, 1)
                square(ch, 4)
                if far.there:
                    take_xs(far, 4)
                    centre(far, 4)
                if nxt.there:
                    take_bc(nxt, 2)
                    decay(nxt, 0)
                    log_part(nxt, 1)
                    take_bc(nxt, 3)

            one, two = Chunk(1), Chunk(2)
            norm(one)
            for p in range(NP):
                take_xs(one, p)
                centre(one, p)
            norm(two)
            silu(one)
            take_xd(one)
            log_part(one, 0)
            for r in range(NS):
                take_bc(one, r)
            act.wait_ge(carry_zero, 1)
            decay(one, 0)
            for p in range(NP - 1):
                take_xs(two, p)
                centre(two, p)
            log_part(one, 1)
            chunk_loop(act, body)
            square(END, 5)
            inverse_deviation(END)
            finish(END)

        @block.vector
        def _(dve):
            taps = [(dy, dx) for dy in range(3) for dx in range(3) if (dy, dx) != (1, 1)]

            def convolve(ch, p):
                dve.wait_ge(centre_done, NP * ch.c + p + 1)
                if ch.first:
                    dve.wait_ge(xs_zero, 2 * NP * ch.b + p + 1)
                if ch.last:
                    dve.wait_ge(xs_zero, 2 * NP * ch.b + NP + p + 1)
                base = 16 * (NP * ch.c + p)
                for n, (dy, dx) in enumerate(taps):
                    for j in range(2):
                        t = 2 * p + j
                        if n:
                            dve.wait_ge(tap_done, base + 2 * n - 1 + j)
                        a, e = max(0, 1 - dx), W - max(0, dx - 1)
                        out = u[:, ch.odd, t, :].rearrange("p (r w) -> p r w", w=W)[:, :, a:e]
                        dve.scalar_tensor_tensor(out, xs[:, t, dy:dy + ROWS, a + dx - 1:e + dx - 1],
                                                 k.conv_w[:, t, 3 * dy + dx:3 * dy + dx + 1], out,
                                                 ALU.mult, ALU.add).then_inc(tap_done, 1)

            def step(ch, p):
                n = NP * ch.c + p
                dve.wait_ge(q_ready, n + 1)
                dve.wait_ge(da_ready, n)
                dve.scalar_tensor_tensor(delta[:, :, :].rearrange("p j n -> p (j n)"), ps_d[:, :], 0.0,
                                         q[:, :, :].rearrange("p j n -> p (j n)"), ALU.max, ALU.add).then_inc(delta_ready, 1)
                dve.wait_ge(delta_ready, n + 1)
                dve.wait_ge(dbu_ready, n)
                dve.tensor_tensor(du[:, :, :], delta[:, :, :], u[:, ch.odd, 2 * p:2 * p + 2, :], ALU.mult).then_inc(du_ready, 1)

            def inflow(ch, p):
                n = NP * ch.c + p
                dve.wait_ge(sum_done, n)
                dve.tensor_copy(st[:, :, :, 0], carry[:, 2 * p:2 * p + 2, :])
                dve.wait_ge(du_ready, n + 1)
                dve.wait_ge(bc_ready, NS * ch.c + NS // 2)
                dve.tensor_tensor(st[:, :, :, 1:T + 1], du[:, :, None, :].to_broadcast([P, 2, NS, T]),
                                  bc[:, None, 0:NS, :].to_broadcast([P, 2, NS, T]), ALU.mult).then_inc(dbu_ready, 1)

            def scan(ch, p):
                n = NP * ch.c + p
                dve.wait_ge(da_ready, n + 1)
                dve.wait_ge(dbu_ready, n + 1)
                states = st[:, :, :, :].rearrange("p j n t -> p (j n t)")
                dve.tensor_tensor_scan(states, da[:, :, :, :].rearrange("p j n t -> p (j n t)"), states, 0.0,
                                       ALU.mult, ALU.add).then_inc(scan_done, 1)
                dve.wait_ge(scan_done, n + 1)
                dve.tensor_copy(carry[:, 2 * p:2 * p + 2, :], st[:, :, :, T]).then_inc(carry_kept, 1)

            def times_c(ch, p):
                n = NP * ch.c + p
                dve.wait_ge(bc_ready, NS * ch.c + NS)
                dve.wait_ge(carry_kept, n + 1)
                v = st[:, :, :, 1:T + 1]
                dve.tensor_tensor(v, v, bc[:, None, NS:2 * NS, :].to_broadcast([P, 2, NS, T]), ALU.mult).then_inc(yc_done, 1)

            def outflow(ch, p):
                n = NP * ch.c + p
                s = [st[:, :, m, 1:T + 1] for m in range(NS)]
                dve.wait_ge(yc_done, n + 1)
                dve.tensor_tensor(st[:, :, 0:2, 1:T + 1], st[:, :, 0:2, 1:T + 1], st[:, :, 2:4, 1:T + 1], ALU.add).then_inc(half_done, 1)
                dve.wait_ge(half_done, n + 1)
                dve.wait_ge(y_used, n + 1 - RING)
                dve.wait_ge(ysq_ready, n + 1 - RING)
                dve.tensor_tensor(y[:, p % RING, :, :], s[0], s[1], ALU.add).then_inc(sum_done, 1)
                dve.wait_ge(sum_done, n + 1)
                for j in range(2):
                    t = 2 * p + j
                    last = dve.scalar_tensor_tensor(y[:, p % RING, j, :], u[:, ch.odd, t, :], k.d_par[:, t:t + 1],
                                                    y[:, p % RING, j, :], ALU.mult, ALU.add)
                last.then_inc(y_ready, 1)

            def layer_norm(ch):
                n = 3 * ch.c
                mean, sq, var = (ln[:, m, :] for m in range(3))
                dve.wait_ge(y_used, NP * ch.c + NP)
                dve.wait_ge(ysq_done, NP * ch.c + NP)
                dve.wait_ge(rstd_ready, ch.c)
                dve.tensor_scalar(mean, ps_o[:, :, 0, CH2], 1.0 / DI, None, ALU.mult).then_inc(ln_step, 1)
                dve.wait_ge(ln_step, n + 1)
                dve.tensor_tensor(sq, mean, mean, ALU.mult).then_inc(ln_step, 1)
                dve.wait_ge(ln_step, n + 2)
                dve.scalar_tensor_tensor(var, ps_y[:, 0:TT], 1.0 / DI, sq, ALU.mult, ALU.subtract).then_inc(ln_step, 1)
                dve.wait_ge(ln_step, n + 3)
                dve.tensor_scalar(var, var, 0.0, LN_EPS, ALU.max, ALU.add).then_inc(var_ready, 1)

            def result(ch):
                dve.wait_ge(rstd_ready, ch.c + 1)
                dve.wait_ge(xb_ready, ch.c + 1)
                for tt in range(TT):
                    tile = xt[:, tt, :].rearrange("p (j c) -> p j c", j=2)
                    dve.scalar_tensor_tensor(tile, ps_o[:, tt, :, 0:CH2], ln[:, 3, tt:tt + 1], tile,
                                             ALU.mult, ALU.add).then_inc(z_ready, 1)

            def keep_sums(ch):
                dve.wait_ge(zst_done, TT * ch.c + TT)
                dve.wait_ge(zst_kept, ch.c)
                dve.tensor_tensor(k.sums[:, ch.b, :], k.sums[:, ch.b, :], ps_x[:, 0:2 * KT], ALU.add).then_inc(zst_kept, 1)

            def body(ch):
                prev, nxt, far = ch + -1, ch + 1, ch + 2
                for p in range(NP):
                    after, q_ = (ch, p + 1) if p + 1 < NP else (nxt, 0)
                    conv, r = (nxt, p + 2) if p + 2 < NP else (far, p + 2 - NP)
                    scan(ch, p)
                    times_c(ch, p)
                    if after.there:
                        step(after, q_)
                    outflow(ch, p)
                    if p == NP - 1 and ch.last and after.there:
                        dve.wait_ge(carry_kept, NP * ch.c + NP)
                        dve.memset(carry[:, :, :], 0.0).then_inc(carry_zero, 1)
                        dve.wait_ge(carry_zero, 2 + ch.b)
                    if after.there:
                        inflow(after, q_)
                    if p == 1 and prev.there:
                        result(prev)
                    if conv.there:
                        convolve(conv, r)
                    if p == 0 and prev.there:
                        layer_norm(prev)
                    if p == 2 and prev.there:
                        keep_sums(prev)

            one, two = Chunk(1), Chunk(2)
            dve.memset(da[:, :, :, 0], 0.0)
            dve.memset(k.sums[:, :, :], 0.0)
            dve.memset(carry[:, :, :], 0.0).then_inc(carry_zero, 1)
            dve.wait_ge(carry_zero, 1)
            for p in range(NP):
                convolve(one, p)
            step(one, 0)
            inflow(one, 0)
            for p in range(2):
                convolve(two, p)
            chunk_loop(dve, body)
            layer_norm(END)
            result(END)
            keep_sums(END)

        @block.gpsimd
        def _(pool):
            for s, n in per_chunk:
                pool.sem_inc(s, n)

            def edge(ch):
                for p in range(NP):
                    if ch.first:
                        pool.wait_ge(tap_done, 16 * (NP * (ch.c - 1) + p + 1))
                        pool.memset(xs[:, 2 * p:2 * p + 2, 0, :], 0.0).then_inc(xs_zero, 1)
                    if ch.last:
                        pool.wait_ge(xs_moved, NP * ch.c + p + 1)
                        pool.memset(xs[:, 2 * p:2 * p + 2, ROWS + 1, :], 0.0).then_inc(xs_zero, 1)

            def body(ch):
                if (ch + 2).there:
                    edge(ch + 2)
                pool.wait_ge(xt_in, 16 * (ch.c + 1))
                for tt in range(TT):
                    last = pool.tensor_tensor(xt[:, tt, :], xt[:, tt, :], k.bv[:, :], ALU.add)
                last.then_inc(xb_ready, 1)

            edge(Chunk(1))
            chunk_loop(pool, body)


def mlp_stage(nc, d, k):
    with ExitStack() as ctx:
        def sb(name, shape):
            return ctx.enter_context(nc.sbuf_tensor(name, shape, F32))

        def pb(name, shape):
            return ctx.enter_context(nc.psum_tensor(name, shape, F32))

        def sem(name):
            return ctx.enter_context(nc.semaphore(name))

        PAD = 16
        NPOS = KW * H
        QC = C // 4
        UNITS = 16
        LAG = 5
        zt = sb("zt", [P, 2, KW, C + PAD])
        zt0 = sb("zt0", [P, C + PAD])
        w1 = sb("mlp_w1", [P, BP, HM * P])
        w2 = sb("mlp_w2", [P, BP, HM, 2 * PC])
        b1 = sb("mlp_b1", [P, BP, HM])
        b2 = sb("mlp_b2", [P, BP, 2 * PC])
        f_h = sb("f_h", [P, 3, 2, H])
        i_h = sb("i_h", [P, P])
        spec = sb("spec", [P, 2, NPOS])
        hid = sb("hid", [P, 2, HM, NPOS])
        val = sb("val", [P, 2, KW // 2, 2 * PC])
        clip = sb("clip", [P, 2, KW // 2, 2 * PC])
        shr = sb("shr", [P, KW // 2, 2, C])
        inv = sb("inv", [P, KW, C])
        cols = sb("cols", [P, KW, C])
        member = sb("member", [P, KT, NG])
        gm = sb("gm", [P, NB, NG])
        gv = sb("gv", [P, NB, NG])
        gt = sb("gt", [P, NB, NG])
        pick = sb("pick", [P, NB, BP])
        scale = sb("scale", [P, NB, BP])
        shift = sb("shift", [P, NB, BP])

        ps_f = pb("ps_f", [P, 2, 512])
        ps_h = pb("ps_h", [P, HM, 512])
        ps_v = pb("ps_v", [P, 2, 512])
        ps_c = pb("ps_c", [P, 512])

        w_in, z0_in = sem("mlp_w_in"), sem("z0_in")
        z_in = [sem(f"z_in{n}") for n in range(2)]
        chain, stats_ok, sign_ok, pad_ok = sem("m_chain"), sem("stats_ok"), sem("sign_ok"), sem("pad_ok")
        var_ok, root_ok = sem("m_var_ok"), sem("m_root_ok")
        f_done, spec_ready, dc_done = sem("f_done"), sem("spec_ready"), sem("dc_done")
        h_done, hid_act, hid_dve = sem("h_done"), sem("hid_act"), sem("hid_dve")
        v_done, val_ready, clip_ready, shr_ready = sem("v_done"), sem("val_ready"), sem("clip_ready"), sem("shr_ready")
        inv_in = [sem(f"inv_in{quarter}") for quarter in range(4)]
        c_done, cols_ready, z2_out = sem("c_done"), sem("cols_ready"), sem("z2_out")
        per_step = [(f_done, BP), (spec_ready, BP), (h_done, HM * BP), (hid_act, 2 * BP), (hid_dve, BP), (v_done, BP),
                    (val_ready, BP), (clip_ready, BP), (shr_ready, BP), (c_done, UNITS),
                    (cols_ready, UNITS), (z2_out, 32)] + [(s, 64) for s in inv_in]
        block = ctx.enter_context(nc.Block())

        z1_tiles = d.z1.rearrange("b (t r) h c -> b t (r h) c", r=2)
        z2_cols = d.z2.rearrange("b h (t r) c -> b r h t c", r=2)
        PER = NST + 1

        def steps(engine, step):
            for b in range(NB):
                with engine.Fori(0, NST // 2) as i:
                    for e in range(2):
                        step(b, 2 * i + (PER * b + e), e, i + (NST // 2 * b + 1), KW)
                step(b, PER * b + NST, None, b + 1, 2)

        @block.sync
        def _(sp):
            sp.dma_start(w1[:, :, :], d.mlp_w1).then_inc(w_in, 16)
            sp.dma_start(w2[:, :, :, :], d.mlp_w2).then_inc(w_in, 16)
            sp.dma_start(b1[:, :, :], d.mlp_b1).then_inc(w_in, 16)
            sp.dma_start(b2[:, :, :].rearrange("p a c -> p (a c)"), d.mlp_b2.to_broadcast([P, BP * 2 * PC])).then_inc(w_in, 16)
            sp.dma_start(f_h[:, :, :, :], d.f_h).then_inc(w_in, 16)
            sp.dma_start(i_h[:, :], d.i_h).then_inc(w_in, 16)
            sp.dma_start(member[:, :, :], d.member).then_inc(w_in, 16)

            def load(g):
                b, s = g // NST, g % NST
                sp.dma_start(zt[:, g % 2, :, 0:C], z1_tiles[b, s * KW:(s + 1) * KW].rearrange("t p c -> p t c")
                             ).then_inc(z_in[g % 2], 16)

            load(0)
            load(1)
            for n in range(NB * PER):
                b, s = n // PER, n % PER
                m = KW if s < NST else 2
                if s == 0:
                    if b:
                        sp.wait_ge(f_done, BP * (PER * b + 2))
                    sp.dma_start(zt0[:, 0:C], z1_tiles[b, 0]).then_inc(z0_in, 16)
                sp.wait_ge(c_done, UNITS * (n + 2))
                for quarter in range(4):
                    sp.wait_ge(shr_ready, BP * (n + 2) + 4 * quarter + 4)
                    part = slice(quarter * QC, (quarter + 1) * QC)
                    for f in range(2):
                        for r in range(2):
                            sp.dma_start(inv[r * H:(r + 1) * H, f:m:2, part],
                                         shr[f * H:(f + 1) * H, 0:m // 2, r, part]).then_inc(inv_in[quarter], 16)
                g = NST * b + s + 2
                if s < NST and g < NB * NST:
                    sp.wait_ge(f_done, BP * (n + 3))
                    load(g)
                sp.wait_ge(cols_ready, UNITS * (n + 3))
                if s < NST:
                    for r in range(2):
                        sp.dma_start(z2_cols[b, r, :, s * KW:(s + 1) * KW, :], cols[r * H:(r + 1) * H, :, :]).then_inc(z2_out, 16)
                else:
                    sp.wait_ge(z2_out, 32 * (n + 2))
                    sp.dma_start(d.z2[b, :, 0:2, :], cols[0:H, 0:2, :]).then_inc(z2_out, 32)
            sp.wait_ge(z2_out, 32 * (NB * PER + 2))

        @block.gpsimd
        def _(pool):
            for s, n in per_step:
                pool.sem_inc(s, 2 * n)
            pool.memset(zt[:, :, :, C:C + PAD], 0.0)
            pool.memset(zt0[:, C:C + PAD], 0.0).then_inc(pad_ok, 1)

        @block.tensor
        def _(pe):
            pe.wait_ge(w_in, 16 * 7)
            for b in range(NB):
                for m in range(2):
                    for t in range(KT):
                        n = (b * 2 + m) * NG
                        last = pe.matmul(ps_c[:, n:n + NG], k.sums[:, b, m * KT + t:m * KT + t + 1].to_broadcast([P, P]),
                                         member[:, t, :], start=(t == 0), stop=(t == KT - 1))
            last.then_inc(stats_ok, 1)
            pe.wait_ge(sign_ok, 1)
            pe.wait_ge(pad_ok, 1)

            def transform(n, a, buf, width):
                pe.wait_ge(spec_ready, BP * (n + 2) + max(a - 1, 0))
                for j in range(width):
                    cut = slice(a * PC, a * PC + PC + PAD)
                    lhs, f = (zt0[:, cut], 1 + j) if buf is None else (zt[:, buf, j, cut], 0)
                    for r in range(2):
                        last = pe.matmul(ps_f[r * H:(r + 1) * H, a % 2, j * H:(j + 1) * H], lhs, f_h[:, f, r, :],
                                         start=True, stop=True)
                last.then_inc(f_done, 1)

            def hidden(b, n, a, buf, width):
                pe.wait_ge(spec_ready, BP * (n + 2) + a + 1)
                if buf is None:
                    pe.wait_ge(dc_done, b * BP + a + 1)
                pe.wait_ge(hid_act, 2 * (BP * (n + 2) + a))
                pe.wait_ge(hid_dve, BP * (n + 2) + a)
                for t in range(HM):
                    pe.matmul(ps_h[:, t, 0:width * H], w1[:, a, t * P:(t + 1) * P], spec[:, a % 2, 0:width * H],
                              start=True, stop=True).then_inc(h_done, 1)

            def second(n, a, width):
                pe.wait_ge(hid_act, 2 * (BP * (n + 2) + a + 1))
                pe.wait_ge(hid_dve, BP * (n + 2) + a + 1)
                pe.wait_ge(val_ready, BP * (n + 2) + max(a - 1, 0))
                for f in range(width // 2):
                    for t in range(HM):
                        last = pe.matmul(ps_v[:, a % 2, f * 2 * PC:(f + 1) * 2 * PC], hid[:, a % 2, t, f * P:(f + 1) * P],
                                         w2[:, a, t, :], start=(t == 0), stop=(t == HM - 1))
                last.then_inc(v_done, 1)

            def inverse(n, unit, width):
                per = width // 2
                quarter, f = unit // per, unit % per
                share = UNITS // (4 * per)
                pe.wait_ge(inv_in[quarter], 64 * (n + 3))
                pe.wait_ge(cols_ready, UNITS * (n + 2) + share * unit)
                pe.matmul(ps_c[:, 0:2 * QC], i_h[:, :], inv[:, 2 * f:2 * f + 2, quarter * QC:(quarter + 1) * QC],
                          start=True, stop=True).then_inc(c_done, share)

            def step(b, n, buf, loads, width):
                units = 2 * width
                if buf is None:
                    pe.wait_ge(z0_in, 16 * loads)
                else:
                    pe.wait_ge(z_in[buf], 16 * loads)
                transform(n, 0, buf, width)
                for a in range(BP):
                    if a + 1 < BP:
                        transform(n, a + 1, buf, width)
                    hidden(b, n, a, buf, width)
                    if a:
                        second(n, a - 1, width)
                    if units == UNITS and a > LAG:
                        inverse(n, a - LAG - 1, width)
                second(n, BP - 1, width)
                for unit in range(BP - LAG - 1 if units == UNITS else 0, units):
                    inverse(n, unit, width)

            steps(pe, step)

        @block.scalar
        def _(act):
            def relu(n, a, width):
                act.wait_ge(v_done, BP * (n + 2) + max(a - 1, 0))
                for t in range(2):
                    act.wait_ge(h_done, HM * (BP * (n + 2) + a) + t + 1)
                    act.activation(hid[:, a % 2, t, 0:width * H], ps_h[:, t, 0:width * H], ACT.Relu,
                                   bias=b1[:, a, t:t + 1]).then_inc(hid_act, 1)

            def take_cols(n, unit, width):
                per = width // 2
                quarter, f = unit // per, unit % per
                share = UNITS // (4 * per)
                if unit == 0:
                    act.wait_ge(z2_out, 32 * (n + 2))
                act.wait_ge(c_done, UNITS * (n + 2) + share * (unit + 1))
                act.activation(cols[:, 2 * f:2 * f + 2, quarter * QC:(quarter + 1) * QC],
                               ps_c[:, 0:2 * QC].rearrange("p (f c) -> p f c", f=2), ACT.Copy).then_inc(cols_ready, share)

            def step(b, n, buf, loads, width):
                units = 2 * width
                for a in range(BP):
                    relu(n, a, width)
                    if units == UNITS and a > LAG:
                        take_cols(n, a - LAG - 1, width)
                for unit in range(BP - LAG - 1 if units == UNITS else 0, units):
                    take_cols(n, unit, width)

            act.wait_ge(var_ok, 1)
            act.activation(gt[:, :, :], gt[:, :, :], ACT.Sqrt).then_inc(root_ok, 1)
            act.wait_ge(w_in, 16 * 7)
            steps(act, step)

        @block.vector
        def _(dve):
            links = [0]

            def link(ins):
                links[0] += 1
                ins.then_inc(chain, 1)
                dve.wait_ge(chain, links[0])

            dve.wait_ge(stats_ok, 1)
            sums = ps_c[:, 0:NB * 2 * NG].rearrange("p (b m g) -> p b m g", b=NB, m=2)
            link(dve.tensor_scalar(gm[:, :, :], sums[:, :, 0, :], 1.0 / (GC * L), None, ALU.mult))
            link(dve.tensor_tensor(gt[:, :, :], gm[:, :, :], gm[:, :, :], ALU.mult))
            for b in range(NB):
                last = dve.scalar_tensor_tensor(gv[:, b, :], sums[:, b, 1, :], 1.0 / (GC * L), gt[:, b, :],
                                                ALU.mult, ALU.subtract)
            link(last)
            dve.tensor_scalar(gt[:, :, :], gv[:, :, :], 0.0, GN_EPS, ALU.max, ALU.add).then_inc(var_ok, 1)
            dve.wait_ge(root_ok, 1)
            link(dve.reciprocal(gv[:, :, :], gt[:, :, :]))
            for b in range(NB):
                last = dve.scalar_tensor_tensor(gm[:, b, :], gm[:, b, :], -float(H), gv[:, b, :], ALU.mult, ALU.mult)
            link(last)
            for table, out in ((gv, scale), (gm, shift)):
                pairs = table[:, :, :].rearrange("p b (a e) -> p b a e", e=2)
                link(dve.tensor_scalar(pick[:, :, :], pairs[:, :, :, 0], k.mask[:, 0:1], None, ALU.mult))
                for b in range(NB):
                    last = dve.scalar_tensor_tensor(out[:, b, :], pairs[:, b, :, 1], k.mask[:, 1:2], pick[:, b, :],
                                                    ALU.mult, ALU.add)
                link(last)
            dve.wait_ge(w_in, 16 * 7)
            im_re = w1[H:P, :, :].rearrange("p a (e r m) -> p (a e) r m", e=2, r=2)[:, :, 0, :]
            dve.tensor_scalar(im_re, im_re, -1.0, None, ALU.mult)
            for p0, p1, t in ((96, 128, 0), (0, 64, 1), (32, 64, 2), (64, 128, 2)):
                last = dve.tensor_scalar(w2[p0:p1, :, t, 0:PC], w2[p0:p1, :, t, 0:PC], -1.0, None, ALU.mult)
            last.then_inc(sign_ok, 1)

            def take_spec(b, n, a, buf, width):
                dve.wait_ge(f_done, BP * (n + 2) + a + 1)
                dve.wait_ge(h_done, HM * (BP * (n + 2) + max(a - 1, 0)))
                dve.tensor_scalar(spec[:, a % 2, 0:width * H], ps_f[:, a % 2, 0:width * H], scale[:, b, a:a + 1], None,
                                  ALU.mult).then_inc(spec_ready, 1)
                if buf is None:
                    dve.wait_ge(spec_ready, BP * (n + 2) + a + 1)
                    dve.tensor_scalar(spec[0:H, a % 2, 0:1], spec[0:H, a % 2, 0:1], shift[0:H, b, a:a + 1], None,
                                      ALU.add).then_inc(dc_done, 1)

            def relu(n, a, width):
                t = HM - 1
                dve.wait_ge(v_done, BP * (n + 2) + max(a - 1, 0))
                dve.wait_ge(h_done, HM * (BP * (n + 2) + a + 1))
                dve.tensor_scalar(hid[:, a % 2, t, 0:width * H], ps_h[:, t, 0:width * H], b1[:, a, t:t + 1], 0.0,
                                  ALU.add, ALU.max).then_inc(hid_dve, 1)

            def shrink(n, a, width):
                m = width // 2
                v, cl = val[:, a % 2, 0:m, :], clip[:, a % 2, 0:m, :]
                dve.wait_ge(v_done, BP * (n + 2) + a + 1)
                dve.wait_ge(shr_ready, BP * (n + 2) + max(a - 1, 0))
                dve.tensor_tensor(v, ps_v[:, a % 2, 0:m * 2 * PC].rearrange("p (f c) -> p f c", f=m),
                                  b2[:, a:a + 1, :].to_broadcast([P, m, 2 * PC]), ALU.add).then_inc(val_ready, 1)
                dve.wait_ge(val_ready, BP * (n + 2) + a + 1)
                dve.tensor_scalar(cl, v, -SHRINK, SHRINK, ALU.max, ALU.min).then_inc(clip_ready, 1)
                dve.wait_ge(clip_ready, BP * (n + 2) + a + 1)
                if a == 0:
                    for s in inv_in:
                        dve.wait_ge(s, 64 * (n + 2))
                dve.tensor_tensor(shr[:, 0:m, :, a * PC:(a + 1) * PC], v.rearrange("p f (r c) -> p f r c", r=2),
                                  cl.rearrange("p f (r c) -> p f r c", r=2), ALU.subtract).then_inc(shr_ready, 1)

            def step(b, n, buf, loads, width):
                take_spec(b, n, 0, buf, width)
                for a in range(BP):
                    if a + 1 < BP:
                        take_spec(b, n, a + 1, buf, width)
                    relu(n, a, width)
                    if a:
                        shrink(n, a - 1, width)
                shrink(n, BP - 1, width)

            steps(dve, step)


def last_stage(nc, d, k):
    with ExitStack() as ctx:
        def sb(name, shape):
            return ctx.enter_context(nc.sbuf_tensor(name, shape, F32))

        def sem(name):
            return ctx.enter_context(nc.semaphore(name))

        U = 2
        N = NB * L // (U * P)
        z = sb("last_z", [P, 2, U, C])
        x = sb("last_x", [P, 2, U, C])
        o = sb("last_o", [P, 2, U, C])
        i_w = sb("i_w", [P, P])
        ps = ctx.enter_context(nc.psum_tensor("ps_last", [P, 2, U, 2, 512], F32))
        m_in = sem("i_w_in")
        z_in = [sem(f"last_z_in{e}") for e in range(2)]
        x_in = [sem(f"last_x_in{e}") for e in range(2)]
        o_out = [sem(f"last_o_out{e}") for e in range(2)]
        back, summed = sem("last_back"), sem("last_summed")
        turn = sem("last_turn")
        block = ctx.enter_context(nc.Block())
        zs = d.z2.rearrange("b h q c -> (b h q) c").rearrange("(g t p) c -> g p t c", t=U, p=P)
        xx = d.x2.rearrange("(g t p) c -> g p t c", t=U, p=P)
        out = d.out.rearrange("(g t p) c -> g p t c", t=U, p=P)

        @block.gpsimd
        def _(pool):
            for s in (back, summed):
                pool.sem_inc(s, 2 * U)
            for e in range(2):
                pool.sem_inc(o_out[e], 16)

        @block.sync
        def _(sp):
            sp.dma_start(i_w[:, :], d.i_w).then_inc(m_in, 16)
            with sp.Fori(0, N // 2) as i:
                for e in range(2):
                    m = 2 * i + e
                    sp.wait_ge(back, U * (m + 1))
                    sp.sem_inc(turn, 1)
                    sp.dma_start(z[:, e, :, :], zs[m]).then_inc(z_in[e], 16)
                    sp.wait_ge(summed, U * (m + 1))
                    sp.sem_inc(turn, 1)
                    sp.dma_start(x[:, e, :, :], xx[m]).then_inc(x_in[e], 16)

        @block.tensor
        def _(pe):
            pe.wait_ge(m_in, 16)
            with pe.Fori(0, N // 2) as i:
                for e in range(2):
                    m = 2 * i + e
                    pe.wait_ge(z_in[e], 16 * (i + 1))
                    pe.wait_ge(summed, U * (m + 1))
                    for t in range(U):
                        for j in range(2):
                            last = pe.matmul(ps[:, e, t, j, 0:CH2], i_w[:, :], z[:, e, t, j * CH2:(j + 1) * CH2],
                                             start=True, stop=True)
                        last.then_inc(back, 1)

        @block.vector
        def _(dve):
            with dve.Fori(0, N // 2) as i:
                for e in range(2):
                    m = 2 * i + e
                    dve.wait_ge(x_in[e], 16 * (i + 1))
                    dve.wait_ge(o_out[e], 16 * (i + 1))
                    for t in range(U):
                        dve.wait_ge(back, U * (m + 2) + t + 1)
                        dve.tensor_tensor(o[:, e, t, :].rearrange("p (j c) -> p j c", j=2), ps[:, e, t, :, 0:CH2],
                                          x[:, e, t, :].rearrange("p (j c) -> p j c", j=2), ALU.add).then_inc(summed, 1)

        @block.scalar
        def _(act):
            with act.Fori(0, N // 2) as i:
                for e in range(2):
                    m = 2 * i + e
                    act.wait_ge(summed, U * (m + 3))
                    act.dma_start(out[m], o[:, e, :, :]).then_inc(o_out[e], 16)
            for e in range(2):
                act.wait_ge(o_out[e], 16 * (N // 2 + 1))


def build(nc, d):
    with ExitStack() as kept:
        k = Bufs()

        def keep(ctx, name, shape):
            return ctx.enter_context(nc.sbuf_tensor(name, shape, F32))

        k.sums = keep(kept, "sums", [P, NB, 2 * KT])
        k.mask = keep(kept, "mask", [P, 2])
        with ExitStack() as first:
            k.w_in = keep(first, "w_in", [P, KT, DI])
            k.w_out = keep(first, "w_out", [P, DT, C + 1])
            k.one = keep(first, "one", [P, 1])
            k.w_x = keep(first, "w_x", [P, DT, XR])
            k.w_dt = keep(first, "w_dt", [ONE + 1, DI])
            k.conv_w = keep(first, "conv_w", [P, DT, 9])
            k.conv_b = keep(first, "conv_b", [P, DT])
            k.d_par = keep(first, "d_par", [P, DT])
            k.a_neg = keep(first, "a_neg", [P, DT * NS])
            k.gn_scale = keep(first, "gn_scale", [P, KT, NB])
            k.gn_shift = keep(first, "gn_shift", [P, KT, NB])
            k.bv = keep(first, "bv", [P, C])
            k.ident = keep(first, "ident", [P, P])
            k.f_w = keep(first, "f_w", [P, P])
            k.xd = keep(first, "xd", [ONE + 1, T])
            setup_stage(nc, d, k)
            scan_stage(nc, d, k)
        mlp_stage(nc, d, k)
        last_stage(nc, d, k)


def constants():
    n = np.arange(H)
    angle = 2 * np.pi * np.outer(n, n) / H
    cos, sin = np.cos(angle), np.sin(angle)
    norm = 1 / np.sqrt(H)
    f = np.zeros((W, W))
    f[:, 0], f[:, 1] = 1, cos[:, W // 2]
    f[:, 2::2], f[:, 3::2] = cos[:, 1:W // 2], -sin[:, 1:W // 2]
    i = 2 * f.T
    i[0:2] /= 2
    two = np.eye(2)
    zero = np.zeros((H, H))
    f_h = np.stack([
        np.stack([np.vstack([cos, sin]), np.vstack([-sin, cos])], 1),
        np.stack([np.vstack([cos, zero]), np.vstack([-sin, zero])], 1),
        np.stack([np.vstack([zero, cos]), np.vstack([zero, -sin])], 1),
    ], 1)
    i_h = np.block([[cos, sin], [-sin, cos]])
    group = np.zeros((C, C))
    for g in range(NG):
        group[g * GC:(g + 1) * GC, g * GC:(g + 1) * GC] = 1 / GC
    member = np.repeat(np.eye(NG), GC, axis=0)
    first = (np.arange(P) % H < GC).astype(np.float64)
    tables = dict(
        f_w=np.kron(two, f) * norm, i_w=np.kron(two, i) * norm, f_h=f_h * norm, i_h=i_h * norm,
        group=group.reshape(KT, P, C).transpose(1, 0, 2), member=member.reshape(KT, P, NG).transpose(1, 0, 2),
        mask=np.stack([first, 1 - first], 1), ident=np.eye(P),
        zeros=np.zeros((ONE - RANK, DI)),
    )
    return {name: np.ascontiguousarray(a, dtype=np.float32) for name, a in tables.items()}


def layouts(x, L0_conv_in_proj_w, L0_conv_conv_w, L0_conv_conv_b, L0_conv_x_proj_w, L0_conv_dt_w, L0_conv_dt_b,
            L0_conv_A_log, L0_conv_D_param, L0_conv_ln_g, L0_conv_ln_b, L0_conv_out_proj_w, L1_conv_w1, L1_conv_b1,
            L1_conv_w2, L1_conv_b2):
    x = np.asarray(x)
    f32 = np.float32
    padded = np.zeros((NB, C, L + W), f32)
    padded[:, :, 0:L] = x.reshape(NB, C, L)

    def by_tile(a):
        a = np.asarray(a)
        return a.reshape(DT, P, -1).transpose(1, 0, 2)

    w1, b1 = np.asarray(L1_conv_w1), np.asarray(L1_conv_b1)
    w2, b2 = np.asarray(L1_conv_w2), np.asarray(L1_conv_b2)
    m1 = np.zeros((BP, P, 2, 2, HID), f32)
    m2 = np.zeros((BP, 2, 2, HID, 2, 2, GC), f32)
    v1 = np.zeros((BP, 2, 2, HID), f32)
    v2 = np.zeros((BP, 2, 2, GC), f32)
    for a in range(BP):
        for e in range(2):
            g = 2 * a + e
            for r in range(2):
                m1[a, e * GC:(e + 1) * GC, e, r] = w1[0, g]
                m1[a, H + e * GC:H + (e + 1) * GC, e, r] = w1[1, g]
                m2[a, e, 0, :, r, e] = w2[0, g]
                m2[a, e, 1, :, r, e] = w2[1, g]
                v1[a, e, r] = b1[r, g]
                v2[a, r, e] = b2[r, g]
    return dict(
        x=padded, x_tok=x.transpose(0, 2, 3, 1).reshape(NB * L, C),
        w_in=np.asarray(L0_conv_in_proj_w).T, w_out=np.asarray(L0_conv_out_proj_w).T,
        w_x=np.asarray(L0_conv_x_proj_w).T, w_dt=np.asarray(L0_conv_dt_w)[0].T, dt_b=np.asarray(L0_conv_dt_b),
        conv_w=by_tile(np.asarray(L0_conv_conv_w).reshape(DI, 9)), conv_b=by_tile(L0_conv_conv_b)[:, :, 0],
        d_par=by_tile(L0_conv_D_param)[:, :, 0], a_log=by_tile(L0_conv_A_log).reshape(P, DT * NS),
        ln_g=by_tile(L0_conv_ln_g)[:, :, 0], ln_b=by_tile(L0_conv_ln_b)[:, :, 0],
        mlp_w1=m1.reshape(BP, P, HM * P).transpose(1, 0, 2),
        mlp_w2=m2.reshape(BP, HM, P, 2 * PC).transpose(2, 0, 1, 3),
        mlp_b1=v1.reshape(BP, HM, P).transpose(2, 0, 1), mlp_b2=v2.reshape(1, BP * 2 * PC),
    )


def kernel(**inputs):
    import concourse.bacc as bacc
    from concourse.bass_utils import run_bass_kernel_spmd

    nc = bacc.Bacc("TRN2", target_bir_lowering=False, num_devices=1)
    d = Bufs()
    arrays = {}
    for name, a in {**layouts(**inputs), **constants()}.items():
        arrays[f"in_{name}"] = np.ascontiguousarray(a)
        ap = nc.dram_tensor(f"in_{name}", a.shape, F32, kind="ExternalInput").ap()
        d.__dict__[name] = ap
    d.x2 = nc.dram_tensor("x2", (NB * L, C), F32, kind="Internal").ap()
    d.z1 = nc.dram_tensor("z1", (NB, W, H, C), F32, kind="Internal").ap()
    d.z2 = nc.dram_tensor("z2", (NB, H, W, C), F32, kind="Internal").ap()
    d.out = nc.dram_tensor("out_tok", (NB * L, C), F32, kind="ExternalOutput").ap()
    build(nc, d)
    r = run_bass_kernel_spmd(nc, [arrays], core_ids=[0])
    return r.results[0]["out_tok"].reshape(NB, H, W, C).transpose(0, 3, 1, 2)
```

```python
from contextlib import ExitStack

import numpy as np

import concourse.bass as bass
from concourse import mybir

F32 = mybir.dt.float32
ALU = mybir.AluOpType
ACT = mybir.ActivationFunctionType
AX = mybir.AxisListType

P = 128
NB, C, H, W = 2, 768, 64, 64
L = H * W
DI = 2 * C
NS = 4
RANK = C // 16
KT = C // P
DT = DI // P
NP = DT // 2
ROWS = 4
T = ROWS * W
NCH = H // ROWS
TT = T // P
XR = RANK + 2 * NS
ONE = 64
NG = 32
GC = C // NG
BP = NG // 2
PC = 2 * GC
HID = 4 * GC
HM = 4 * HID // P
KW = 8
NST = W // 2 // KW
PE_PAIR = NP - 1
SHARED = NP - 2
TAPS = [(1, 1), (0, 1), (2, 1), (1, 0), (1, 2), (0, 0), (0, 2), (2, 0), (2, 2)]
PE_TAPS = {SHARED: TAPS[:6], PE_PAIR: TAPS}
DIAGS = [(p, j, tap) for p in PE_TAPS for tap in PE_TAPS[p] for j in range(2)]
SHRINK = 0.01
GN_EPS = 1e-5
LN_EPS = 1e-5
CH2 = C // 2


class Bufs:
    pass


def setup_stage(nc, d, k):
    with ExitStack() as ctx:
        def sb(name, shape):
            return ctx.enter_context(nc.sbuf_tensor(name, shape, F32))

        def sem(name):
            return ctx.enter_context(nc.semaphore(name))

        NX = 4
        xbuf = sb("setup_x", [P, NX, L])
        group = sb("setup_group", [P, KT, C])
        stats = sb("setup_stats", [P, L // 512, 6])
        agg = sb("setup_agg", [P, KT, NB, 2])
        moments = sb("setup_moments", [P, KT, NB, 2])
        lng = sb("setup_lng", [P, DT])
        lnb = sb("setup_lnb", [P, DT])
        alog = sb("setup_alog", [P, DT * NS])
        ident = sb("setup_ident", [P, P])
        spread = sb("setup_spread", [P, 2, DT, P])
        gsum = sb("setup_gsum", [P, C])
        gmean = sb("setup_gmean", [P, KT * NB])
        gvar = sb("setup_gvar", [P, KT * NB])
        gsq = sb("setup_gsq", [P, KT * NB])
        ps_group = ctx.enter_context(nc.psum_tensor("ps_group", [P, 512], F32))
        ps_bv = ctx.enter_context(nc.psum_tensor("ps_bv", [P, 2, 512], F32))
        ps_g = ctx.enter_context(nc.psum_tensor("ps_g", [P, 2, 512], F32))

        x_in = [sem(f"setup_x_in{n}") for n in range(NX)]
        w_in = sem("setup_w_in")
        wo_in = sem("setup_wo_in")
        x_used = sem("setup_x_used")
        stat = sem("setup_stat")
        chain = sem("setup_chain")
        moments_ok = sem("setup_moments_ok")
        grouped = sem("setup_grouped")
        spread_ok = sem("setup_spread_ok")
        small_in, group_in = sem("setup_small_in"), sem("setup_group_in")
        g_ok = sem("setup_g_ok")
        exp_ok = sem("setup_exp_ok")
        var_ok, log_ok, root_ok = sem("setup_var_ok"), sem("setup_log_ok"), sem("setup_root_ok")
        block = ctx.enter_context(nc.Block())

        tiles = [(b, t) for b in range(NB) for t in range(KT)]

        @block.sync
        def _(sp):
            for n, (b, t) in enumerate(tiles):
                if n >= NX:
                    sp.wait_ge(x_used, n - NX + 1)
                sp.dma_start(xbuf[:, n % NX, :], d.x[b, t * P:(t + 1) * P, 0:L]).then_inc(x_in[n % NX], 16)
            sp.wait_ge(w_in, 16 * 10)

        @block.scalar
        def _(act):
            act.dma_start(lng[:, :], d.ln_g).then_inc(small_in, 16)
            act.dma_start(lnb[:, :], d.ln_b).then_inc(small_in, 16)
            act.dma_start(alog[:, :], d.a_log).then_inc(small_in, 16)
            act.dma_start(k.conv_w[:, :, :], d.conv_w).then_inc(small_in, 16)
            act.dma_start(ident[:, :], d.ident).then_inc(small_in, 16)
            act.wait_ge(small_in, 16 * 5)
            act.preload_act_table_set("natural_log_exp_and_others")
            act.activation(k.a_neg[:, :], alog[:, :], ACT.Exp).then_inc(exp_ok, 1)
            act.wait_ge(x_used, 2)
            wo = d.w_out.rearrange("(t p) c -> p t c", p=P)
            act.dma_start(k.w_out[:, :, 0:CH2], wo[:, :, 0:CH2]).then_inc(wo_in, 16)
            act.dma_start(k.w_out[:, :, CH2 + 1:C + 1], wo[:, :, CH2:C]).then_inc(wo_in, 16)
            act.wait_ge(x_used, len(tiles) - NX)
            act.dma_start(group[:, :, :], d.group).then_inc(group_in, 16)
            act.dma_start(k.w_in[:, :, :], d.w_in.rearrange("(t p) m -> p t m", p=P)).then_inc(w_in, 16)
            act.dma_start(k.w_x[:, :, :], d.w_x.rearrange("(t p) m -> p t m", p=P)).then_inc(w_in, 16)
            act.dma_start(k.w_dt[0:RANK, :], d.w_dt).then_inc(w_in, 16)
            act.dma_start(k.w_dt[ONE:ONE + 1, :], d.dt_b).then_inc(w_in, 16)
            act.dma_start(k.w_dt[RANK:ONE, :], d.zeros).then_inc(w_in, 16)
            act.dma_start(k.conv_b[:, :], d.conv_b).then_inc(w_in, 16)
            act.dma_start(k.d_par[:, :], d.d_par).then_inc(w_in, 16)
            act.dma_start(k.f_w[:, :], d.f_w).then_inc(w_in, 16)
            act.dma_start(k.mask[:, :], d.mask).then_inc(w_in, 16)
            act.dma_start(k.xd[RANK:ONE, :], d.zeros[:, 0:T]).then_inc(w_in, 16)
            act.wait_ge(var_ok, 1)
            act.activation(gsq[:, :], gvar[:, :], ACT.Ln).then_inc(log_ok, 1)
            act.wait_ge(log_ok, 1)
            act.activation(k.gn_scale[:, :, :].rearrange("p t b -> p (t b)"), gsq[:, :], ACT.Exp, scale=-0.5).then_inc(root_ok, 1)

        @block.vector
        def _(dve):
            steps = [0]

            def link(ins):
                steps[0] += 1
                ins.then_inc(chain, 1)
                dve.wait_ge(chain, steps[0])

            def moments_of(some):
                for n in some:
                    b, t = tiles[n]
                    dve.wait_ge(x_in[n % NX], 16 * (n // NX + 1))
                    if n:
                        dve.wait_ge(stat, n)
                    for j in range(L // 512):
                        last = dve.bn_stats(stats[:, j, :], xbuf[:, n % NX, j * 512:(j + 1) * 512])
                    last.then_inc(x_used, 1)
                    dve.wait_ge(x_used, n + 1)
                    dve.bn_aggr(agg[:, t, b, :], stats[:, :, :]).then_inc(stat, 1)

            def halves(t):
                return [k.w_out[:, t, j * (CH2 + 1):j * (CH2 + 1) + CH2] for j in range(2)]

            dve.memset(k.xd[ONE:ONE + 1, :], 1.0)
            dve.memset(k.one[:, :], 1.0)
            dve.memset(k.w_out[:, :, CH2:CH2 + 1], 1.0)
            dve.memset(spread[:, :, :, :], 1.0).then_inc(spread_ok, 1)
            moments_of(range(3))
            dve.wait_ge(spread_ok, 1)
            dve.wait_ge(small_in, 16 * 5)
            for t in range(DT):
                dve.tensor_scalar(spread[:, 0, t, :], spread[:, 0, t, :], lnb[:, t:t + 1], None, ALU.mult)
                last = dve.tensor_scalar(spread[:, 1, t, :], spread[:, 1, t, :], lng[:, t:t + 1], 1.0 / DI, ALU.mult, ALU.mult)
            last.then_inc(spread_ok, 1)
            moments_of(range(3, 6))
            for n, (p, j, (dy, dx)) in enumerate(DIAGS):
                dve.tensor_scalar(k.conv_diag[:, n, :], ident[:, :],
                                  k.conv_w[:, 2 * p + j, 3 * dy + dx:3 * dy + dx + 1], None, ALU.mult)
            moments_of(range(6, len(tiles)))
            dve.wait_ge(stat, len(tiles))
            mean, var = agg[:, :, :, 0], agg[:, :, :, 1]
            link(dve.tensor_tensor(moments[:, :, :, 1], mean, mean, ALU.mult))
            link(dve.tensor_tensor(moments[:, :, :, 1], moments[:, :, :, 1], var, ALU.add))
            dve.tensor_copy(moments[:, :, :, 0], mean).then_inc(moments_ok, 1)
            dve.wait_ge(g_ok, 1)
            dve.tensor_copy(k.bv[:, :].rearrange("p (j c) -> p j c", j=2), ps_bv[:, :, 0:CH2])
            link(dve.tensor_copy(gsum[:, :].rearrange("p (j c) -> p j c", j=2), ps_g[:, :, 0:CH2]))
            for t in range(DT):
                for j, half in enumerate(halves(t)):
                    last = dve.scalar_tensor_tensor(half, half, lng[:, t:t + 1], gsum[:, j * CH2:(j + 1) * CH2],
                                                    ALU.mult, ALU.subtract)
            link(last)
            dve.wait_ge(grouped, 1)
            both = ps_group[:, 0:KT * NB * 2].rearrange("p (t b m) -> p (t b) m", b=NB, m=2)
            link(dve.tensor_copy(gmean[:, :], both[:, :, 0]))
            link(dve.tensor_tensor(gsq[:, :], gmean[:, :], gmean[:, :], ALU.mult))
            link(dve.tensor_tensor(gvar[:, :], both[:, :, 1], gsq[:, :], ALU.subtract))
            dve.tensor_scalar(gvar[:, :], gvar[:, :], 0.0, GN_EPS, ALU.max, ALU.add).then_inc(var_ok, 1)
            dve.wait_ge(exp_ok, 1)
            dve.tensor_scalar(k.a_neg[:, :], k.a_neg[:, :], -1.0, None, ALU.mult)
            rs = k.gn_scale[:, :, :].rearrange("p t b -> p (t b)")
            nb = k.gn_shift[:, :, :].rearrange("p t b -> p (t b)")
            dve.wait_ge(root_ok, 1)
            dve.scalar_tensor_tensor(nb, gmean[:, :], -1.0, rs, ALU.mult, ALU.mult)

        @block.tensor
        def _(pe):
            pe.wait_ge(spread_ok, 2)
            pe.wait_ge(wo_in, 16 * 2)
            for m, ps in enumerate((ps_bv, ps_g)):
                for t in range(DT):
                    for j in range(2):
                        last = pe.matmul(ps[:, j, 0:CH2], spread[:, m, t, :], k.w_out[:, t, j * (CH2 + 1):j * (CH2 + 1) + CH2],
                                         start=(t == 0), stop=(t == DT - 1))
            last.then_inc(g_ok, 1)
            pe.wait_ge(moments_ok, 1)
            pe.wait_ge(group_in, 16)
            n = NB * 2
            for c in range(KT):
                near = range(max(c - 1, 0), min(c + 2, KT))
                for t in near:
                    last = pe.matmul(ps_group[:, c * n:(c + 1) * n], group[:, t, c * P:(c + 1) * P],
                                     moments[:, t, :, :], start=(t == near[0]), stop=(t == near[-1]))
            last.then_inc(grouped, 1)


class Chunk:

    def __init__(self, c, b=None, i=None, odd=None):
        self.c = c
        self.b = (c - 1) // NCH if b is None else b
        self.i = (c - 1) % NCH if i is None else i
        self.odd = c % 2 if odd is None else odd
        fixed = isinstance(c, int)
        self.fixed = fixed
        self.there = not fixed or 1 <= c <= NB * NCH
        self.first = fixed and self.there and self.i == 0
        self.last = fixed and self.there and self.i == NCH - 1
        self.rows = ROWS - 1 if self.last else ROWS

    def __add__(self, n):
        if self.fixed:
            return Chunk(self.c + n)
        return Chunk(self.c + n, self.b, self.i + n, (self.odd + n) % 2)


def chunk_loop(engine, body):
    for b in range(NB):
        start = NCH * b + 1
        body(Chunk(start))
        with engine.Fori(0, (NCH - 4) // 2) as r:
            for e in range(2):
                i = 2 * r + (1 + e)
                body(Chunk(2 * r + (start + 1 + e), b, i, (start + 1 + e) % 2))
        for i in range(NCH - 3, NCH):
            body(Chunk(start + i))


def scan_stage(nc, d, k):
    with ExitStack() as ctx:
        def sb(name, shape):
            return ctx.enter_context(nc.sbuf_tensor(name, shape, F32))

        def pb(name, shape):
            return ctx.enter_context(nc.psum_tensor(name, shape, F32))

        def sem(name):
            return ctx.enter_context(nc.semaphore(name))

        RING = 3
        ROW_PARTS = [(0, range(2 * p, 2 * p + 2)) for p in range(NP)] + [(1, range(0, 8)), (1, range(8, DT))]
        ROW_END = [NP, len(ROW_PARTS)]
        DVE_TAPS = [[tap for tap in TAPS[1:] if tap not in PE_TAPS.get(p, [])] for p in range(NP)]
        TAP_END = [2 * sum(map(len, DVE_TAPS[:p + 1])) for p in range(NP)]
        TAPPED = TAP_END[-1]
        xn = sb("xn", [P, KT, T])
        x0 = sb("x0", [P, KT, W])
        xs = sb("xs", [P, DT, ROWS + 2, W])
        u = sb("u", [P, 2, DT, T])
        y = sb("y", [P, RING, 2, T])
        ysq = sb("ysq", [P, 2, 2, T])
        bc = sb("bc", [P, 2, NS, T])
        q = sb("q", [P, 2, T])
        delta = sb("delta", [P, 2, T])
        du = sb("du", [P, 2, T])
        da = sb("da", [P, 2, NS, T + 1])
        st = sb("st", [P, 2, NS, T + 1])
        carry = sb("carry", [P, DT, NS])
        xt = sb("xt", [P, TT, C])
        side = sb("side", [P, TT, C])
        row0 = sb("row0", [P, DT, W])
        ln = sb("ln", [P, 4, TT])

        ps_o = pb("ps_o", [P, TT, 2, 512])
        ps_i = pb("ps_i", [P, 512])
        ps_d = pb("ps_d", [P, 512])
        ps_x = pb("ps_x", [P, 512])
        ps_y = pb("ps_y", [P, 512])

        x_in, x0_in, xt_in = sem("x_in"), sem("x0_in"), sem("xt_in")
        x_normed, x0_normed = sem("x_normed"), sem("x0_normed")
        in_done, in0_done = sem("in_done"), sem("in0_done")
        xs_ready, row0_ready, xs_moved, xs_zero = sem("xs_ready"), sem("row0_ready"), sem("xs_moved"), sem("xs_zero")
        centre_done, tap_done, u_ready = sem("centre_done"), sem("tap_done"), sem("u_ready")
        conv_done, conv_taken = sem("conv_done"), sem("conv_taken")
        xp_done, xd_ready, bc_out, bc_in = sem("xp_done"), sem("xd_ready"), sem("bc_out"), [sem("b_in"), sem("c_in")]
        dt_done, abs_done, exp_done, q_ready = sem("dt_done"), sem("abs_done"), sem("exp_done"), sem("q_ready")
        delta_ready, du_ready, da_ready, dbu_ready = sem("delta_ready"), sem("du_ready"), sem("da_ready"), sem("dbu_ready")
        scan_done, carry_kept, carry_zero, yc_done = sem("scan_done"), sem("carry_kept"), sem("carry_zero"), sem("yc_done")
        half_done, sum_done, skip_ready, y_ready, y_used = sem("half_done"), sem("sum_done"), sem("skip_ready"), sem("y_ready"), sem("y_used")
        ysq_ready = sem("ysq_ready")
        ln_step, var_ready, log_ready, rstd_ready = sem("ln_step"), sem("var_ready"), sem("log_ready"), sem("rstd_ready")
        xb_ready, z_ready, zsq_ready, zst_done, zst_kept = sem("xb_ready"), sem("z_ready"), sem("zsq_ready"), sem("zst_done"), sem("zst_kept")
        f1_done, f1_ready = sem("f1_done"), sem("f1_ready")
        z1_out = sem("z1_out")
        turn = sem("turn")
        per_chunk = [
            (in_done, NP), (xs_ready, NP), (xs_moved, NP), (centre_done, PE_PAIR), (u_ready, NP), (dt_done, NP),
            (abs_done, NP), (exp_done, NP), (q_ready, NP), (delta_ready, NP), (du_ready, NP), (da_ready, NP),
            (dbu_ready, NP), (scan_done, NP), (carry_kept, NP), (yc_done, NP), (half_done, NP), (sum_done, NP),
            (y_ready, NP), (y_used, NP), (ysq_ready, NP), (tap_done, TAPPED), (conv_done, 2), (skip_ready, NP), (conv_taken, 1), (bc_out, 16), (bc_in[0], 16), (bc_in[1], 16),
            (z_ready, TT), (zsq_ready, TT), (zst_done, TT), (f1_done, TT), (f1_ready, TT),
            (ln_step, 3), (var_ready, 1), (log_ready, 1), (rstd_ready, 1), (zst_kept, 1),
            (x_normed, 1), (xp_done, 1), (xd_ready, 1), (xb_ready, 1),
            (x_in, 16), (xt_in, 16), (z1_out, 32),
        ]
        block = ctx.enter_context(nc.Block())

        x_chunks = d.x[:, :, W:W + L].rearrange("b (t p) (i n) -> b i p t n", p=P, n=T)
        xt_chunks = d.x_tok.rearrange("(g t p) c -> g p t c", t=TT, p=P)
        z1_chunks = d.z1.rearrange("b q (i t h) c -> b i h q t c", t=TT, h=2)
        END = Chunk(NB * NCH)

        def squares(ch):
            if ch.fixed and ch.c == END.c:
                return xn[:, :, :].rearrange("p t n -> p (t n)").rearrange("p (t c) -> p t c", c=C)
            return side

        @block.sync
        def _(sp):
            def load_x(ch):
                if ch.c > 1 if ch.fixed else True:
                    sp.wait_ge(in_done, NP * ch.c)
                    sp.sem_inc(turn, 1)
                sp.dma_start(xn[:, :, :], x_chunks[ch.b, ch.i]).then_inc(x_in, 16)

            def load_x0(b):
                sp.dma_start(x0[:, :, :], d.x[b, :, 0:W].rearrange("(t p) w -> p t w", p=P)).then_inc(x0_in, 16)

            def spread_bc(ch):
                sp.wait_ge(xd_ready, ch.c + 1)
                sp.sem_inc(turn, 1)
                for part in bc_in:
                    sp.wait_ge(part, 16 * ch.c)
                    sp.sem_inc(turn, 1)
                sp.dma_start(d.bc.rearrange("o (n t) -> (o n) t", t=T), k.xd[RANK:XR, :]).then_inc(bc_out, 16)
                sp.wait_ge(bc_out, 16 * (ch.c + 1))
                sp.sem_inc(turn, 1)
                for m, used in enumerate((dbu_ready, yc_done)):
                    sp.wait_ge(used, NP * ch.c)
                    sp.sem_inc(turn, 1)
                    sp.dma_start(bc[:, m, :, :].rearrange("p n t -> p (n t)"),
                                 d.bc[:, m * NS * T:(m + 1) * NS * T].to_broadcast([P, NS * T])).then_inc(bc_in[m], 16)

            def store(ch):
                sp.wait_ge(f1_ready, TT * ch.c + TT)
                sp.sem_inc(turn, 1)
                for h in range(2):
                    sp.dma_start(z1_chunks[ch.b, ch.i, h], side[h * W:(h + 1) * W, :, :]).then_inc(z1_out, 16)

            def body(ch):
                if (ch + 3).first:
                    sp.wait_ge(in0_done, NP)
                    load_x0((ch + 3).b)
                if (ch + -1).there:
                    store(ch + -1)
                sp.wait_ge(zsq_ready, TT * ch.c)
                sp.sem_inc(turn, 1)
                sp.wait_ge(f1_done, TT * ch.c)
                sp.sem_inc(turn, 1)
                sp.dma_start(xt[:, :, :], xt_chunks[ch.c - 1]).then_inc(xt_in, 16)
                if (ch + 1).there:
                    spread_bc(ch + 1)
                if (ch + 3).there:
                    load_x(ch + 3)

            load_x0(0)
            for c in range(1, 3):
                load_x(Chunk(c))
            spread_bc(Chunk(1))
            load_x(Chunk(3))
            chunk_loop(sp, body)
            store(END)
            sp.wait_ge(z1_out, 32 * (END.c + 1))

        @block.tensor
        def _(pe):
            def in_proj(ch, p):
                pe.wait_ge(xs_ready, NP * ch.c + p)
                if p == 0:
                    pe.wait_ge(x_normed, ch.c + 1)
                n = ch.rows * W
                for j in range(2):
                    m = (2 * p + j) * P
                    for t in range(KT):
                        last = pe.matmul(ps_i[:, j * T:j * T + n], k.w_in[:, t, m:m + P], xn[:, t, 0:n],
                                         start=(t == 0), stop=(t == KT - 1))
                last.then_inc(in_done, 1)

            def first_row(b, part):
                n = ROW_PARTS.index((b, part))
                pe.wait_ge(x0_normed, b + 1)
                if part.start:
                    pe.wait_ge(row0_ready, n)
                for j, m in enumerate(part):
                    for t in range(KT):
                        last = pe.matmul(ps_x[:, j * W:(j + 1) * W], k.w_in[:, t, m * P:(m + 1) * P], x0[:, t, :],
                                         start=(t == 0), stop=(t == KT - 1))
                last.then_inc(in0_done, 1)

            def convolve(ch, p):
                if p == SHARED:
                    pe.wait_ge(xd_ready, ch.c)
                    if not ch.fixed or ch.c > 2:
                        pe.wait_ge(zst_kept, ch.c - 2)
                    if ch.fixed and ch.c == 1:
                        pe.wait_ge(row0_ready, NP)
                else:
                    pe.wait_ge(centre_done, PE_PAIR * ch.c + PE_PAIR)
                pe.wait_ge(xs_ready, NP * ch.c + p + 1)
                if ch.first:
                    pe.wait_ge(xs_zero, 2 * NP * ch.b + p + 1)
                if ch.last:
                    pe.wait_ge(xs_zero, 2 * NP * ch.b + NP + p + 1)
                for j in range(2):
                    out = ps_x[:, j * T:(j + 1) * T].rearrange("p (r w) -> p r w", w=W)
                    for dy, dx in PE_TAPS[p]:
                        a, e = max(0, 1 - dx), W - max(0, dx - 1)
                        last = pe.matmul(out[:, :, a:e], k.conv_diag[:, DIAGS.index((p, j, (dy, dx))), :],
                                         xs[:, 2 * p + j, dy:dy + ROWS, a + dx - 1:e + dx - 1],
                                         start=((dy, dx) == TAPS[0]), stop=((dy, dx) == PE_TAPS[p][-1]), skip_group_check=True)
                last.then_inc(conv_done, 1)

            def x_proj(ch, p):
                if p == 0:
                    pe.wait_ge(conv_taken, ch.c + 1)
                    if (ch + 2).first:
                        pe.wait_ge(row0_ready, ROW_END[(ch + 2).b])
                pe.wait_ge(u_ready, NP * ch.c + p + 1)
                for j in range(2):
                    t = 2 * p + j
                    last = pe.matmul(ps_x[0:XR, 0:T], k.w_x[:, t, :], u[:, ch.odd, t, :], start=(t == 0), stop=(t == DT - 1))
                if p == NP - 1:
                    last.then_inc(xp_done, 1)

            def step(ch, p):
                if p == 0:
                    pe.wait_ge(xd_ready, ch.c + 1)
                pe.wait_ge(delta_ready, NP * ch.c + p)
                for j in range(2):
                    m = (2 * p + j) * P
                    last = pe.matmul(ps_d[:, j * T:(j + 1) * T], k.w_dt[0:ONE + 1, m:m + P],
                                     k.xd[0:ONE + 1, :], start=True, stop=True)
                last.then_inc(dt_done, 1)

            def out_proj(ch, p, beside=None):
                pe.wait_ge(y_ready, NP * ch.c + p + 1)
                if p == 0:
                    pe.wait_ge(f1_ready, TT * ch.c)
                    pe.wait_ge(var_ready, ch.c)
                pe.wait_ge(ysq_ready, NP * ch.c + p + 1)
                for j in range(2):
                    t = 2 * p + j
                    for tt in range(TT):
                        cut = slice(tt * P, (tt + 1) * P)
                        lhs = y[:, p % RING, j, cut]
                        pe.matmul(ps_o[:, tt, 0, 0:CH2 + 1], lhs, k.w_out[:, t, 0:CH2 + 1],
                                  start=(t == 0), stop=(t == DT - 1))
                        if beside is not None:
                            result_sums(beside, 2 * j + tt)
                        pe.matmul(ps_o[:, tt, 1, 0:CH2], lhs, k.w_out[:, t, CH2 + 1:C + 1],
                                  start=(t == 0), stop=(t == DT - 1))
                        last = pe.matmul(ps_y[:, tt:tt + 1], ysq[:, p % 2, j, cut], k.one[:, :],
                                         start=(t == 0 and tt == 0), stop=(t == DT - 1), skip_group_check=True)
                last.then_inc(y_used, 1)

            def transform(ch, tt):
                pe.wait_ge(z_ready, TT * ch.c + tt + 1)
                for j in range(2):
                    last = pe.matmul(ps_o[:, tt, j, 0:CH2], k.f_w[:, :], xt[:, tt, j * CH2:(j + 1) * CH2],
                                     start=True, stop=True)
                last.then_inc(f1_done, 1)

            def result_sums(ch, part):
                if part == 0:
                    pe.wait_ge(xd_ready, (ch + 2).c + 1 if (ch + 2).there else END.c + 1)
                tt, half = part // 2, part % 2
                if half == 0:
                    pe.wait_ge(zsq_ready, TT * ch.c + tt + 1)
                for t in range(half * KT // 2, (half + 1) * KT // 2):
                    last = pe.matmul(ps_x[:, t:t + 1], squares(ch)[:, tt, t * P:(t + 1) * P], k.one[:, :],
                                     start=(part == 0 and t == 0), stop=(tt == TT - 1), skip_group_check=True)
                if half:
                    last.then_inc(zst_done, 1)

            def body(ch):
                prev, nxt, far = ch + -1, ch + 1, ch + 2

                def project(p):
                    if far.there:
                        in_proj(far, p)

                if prev.there:
                    out_proj(prev, NP - 1)
                step(ch, 2)
                project(0)
                if nxt.there:
                    convolve(nxt, SHARED)
                project(1)
                step(ch, 3)
                if nxt.there:
                    convolve(nxt, PE_PAIR)
                if prev.there:
                    for tt in range(TT):
                        transform(prev, tt)
                project(2)
                step(ch, 4)
                out_proj(ch, 0)
                project(3)
                step(ch, 5)
                out_proj(ch, 1)
                if (ch + 3).first:
                    pe.wait_ge(conv_taken, nxt.c + 1)
                    for b, part in ROW_PARTS[NP:]:
                        first_row(b, part)
                project(4)
                if nxt.there:
                    for p in range(NP):
                        x_proj(nxt, p)
                out_proj(ch, 2)
                if nxt.there:
                    step(nxt, 0)
                project(5)
                if nxt.there:
                    step(nxt, 1)
                out_proj(ch, 3, beside=prev if prev.there else None)
                out_proj(ch, 4)

            one, two = Chunk(1), Chunk(2)
            for p in range(NP):
                first_row(*ROW_PARTS[p])
                in_proj(one, p)
            for p in (SHARED, PE_PAIR):
                convolve(one, p)
            for p in range(3):
                in_proj(two, p)
            for p in range(NP):
                x_proj(one, p)
            step(one, 0)
            for p in range(3, NP):
                in_proj(two, p)
            step(one, 1)
            chunk_loop(pe, body)
            out_proj(END, NP - 1)
            for tt in range(TT):
                transform(END, tt)
            pe.wait_ge(zst_kept, END.c)
            for part in range(4):
                result_sums(END, part)

        @block.scalar
        def _(act):
            def norm(ch):
                act.wait_ge(x_in, 16 * (ch.c + 1))
                for t in range(KT):
                    last = act.activation(xn[:, t, :], xn[:, t, :], ACT.Identity,
                                          bias=k.gn_shift[:, t, ch.b:ch.b + 1], scale=k.gn_scale[:, t, ch.b:ch.b + 1])
                last.then_inc(x_normed, 1)

            def norm_row(b):
                act.wait_ge(x0_in, 16 * (b + 1))
                for t in range(KT):
                    last = act.activation(x0[:, t, :], x0[:, t, :], ACT.Identity,
                                          bias=k.gn_shift[:, t, b:b + 1], scale=k.gn_scale[:, t, b:b + 1])
                last.then_inc(x0_normed, 1)

            def take_row(b, part):
                act.wait_ge(in0_done, ROW_PARTS.index((b, part)) + 1)
                act.activation(row0[:, part.start:part.stop, :], ps_x[:, 0:len(part) * W].rearrange("p (m w) -> p m w", w=W),
                               ACT.Copy).then_inc(row0_ready, 1)

            def take_xs(ch, p):
                a, e = 2 * p, 2 * p + 2
                if p == PE_PAIR:
                    act.wait_ge(conv_done, 2 * ch.c)
                else:
                    act.wait_ge(tap_done, TAPPED * (ch.c - 1) + TAP_END[p])
                if ch.first:
                    act.wait_ge(row0_ready, ROW_END[1] if ch.b else p + 1)
                    act.activation(xs[:, a:e, 1, :], row0[:, a:e, :], ACT.Copy).then_inc(xs_moved, 1)
                else:
                    act.activation(xs[:, a:e, 0:2, :], xs[:, a:e, ROWS:ROWS + 2, :], ACT.Copy).then_inc(xs_moved, 1)
                    act.wait_ge(xs_moved, NP * ch.c + p + 1)
                act.wait_ge(in_done, NP * ch.c + p + 1)
                act.activation(xs[:, a:e, 2:2 + ch.rows, :],
                               ps_i[:, :].rearrange("p (j r w) -> p j r w", j=2, w=W)[:, :, 0:ch.rows, :],
                               ACT.Copy).then_inc(xs_ready, 1)

            def centre(ch, p):
                if not ch.fixed or ch.c > 1:
                    act.wait_ge(y_ready, NP * (ch.c - 2) + p + 1)
                if p in PE_TAPS:
                    act.wait_ge(conv_done, 2 * ch.c + (p - SHARED + 1))
                else:
                    act.wait_ge(xs_ready, NP * ch.c + p + 1)
                for j in range(2):
                    t = 2 * p + j
                    if p in PE_TAPS:
                        last = act.activation(u[:, ch.odd, t, :], ps_x[:, j * T:(j + 1) * T], ACT.Identity, bias=k.conv_b[:, t:t + 1])
                    else:
                        last = act.activation(u[:, ch.odd, t, :], xs[:, t, 1:1 + ROWS, :], ACT.Identity,
                                              bias=k.conv_b[:, t:t + 1], scale=k.conv_w[:, t, 4:5])
                last.then_inc(conv_taken if p == PE_PAIR else centre_done, 1)

            def silu(ch):
                for p in range(NP):
                    if p == PE_PAIR:
                        act.wait_ge(conv_taken, ch.c + 1)
                    else:
                        act.wait_ge(tap_done, TAPPED * ch.c + TAP_END[p])
                    v = u[:, ch.odd, 2 * p:2 * p + 2, :]
                    act.activation(v, v, ACT.Silu).then_inc(u_ready, 1)
                act.preload_act_table_set("natural_log_exp_and_others")

            def take_xd(ch):
                act.wait_ge(xp_done, ch.c + 1)
                act.wait_ge(dt_done, NP * ch.c)
                act.wait_ge(bc_out, 16 * ch.c)
                act.activation(k.xd[0:XR, :], ps_x[0:XR, 0:T], ACT.Copy).then_inc(xd_ready, 1)

            def log_part(ch, p):
                n = NP * ch.c + p
                act.wait_ge(dt_done, n + 1)
                act.wait_ge(delta_ready, n)
                v = q[:, :, :].rearrange("p j n -> p (j n)")
                act.activation(v, ps_d[:, :], ACT.Abs).then_inc(abs_done, 1)
                act.wait_ge(abs_done, n + 1)
                act.activation(v, v, ACT.Exp, scale=-1.0).then_inc(exp_done, 1)
                act.wait_ge(exp_done, n + 1)
                act.activation(v, v, ACT.Ln, bias=1.0).then_inc(q_ready, 1)

            def decay(ch, p):
                act.wait_ge(delta_ready, NP * ch.c + p + 1)
                act.wait_ge(scan_done, NP * ch.c + p)
                for j in range(2):
                    for n in range(NS):
                        a = (2 * p + j) * NS + n
                        last = act.activation(da[:, j, n, 1:T + 1], delta[:, j, :], ACT.Exp, scale=k.a_neg[:, a:a + 1])
                last.then_inc(da_ready, 1)

            def times_d(ch, p):
                act.wait_ge(du_ready, NP * ch.c + p + 1)
                for j in range(2):
                    t = 2 * p + j
                    last = act.activation(u[:, ch.odd, t, :], u[:, ch.odd, t, :], ACT.Copy, scale=k.d_par[:, t:t + 1])
                last.then_inc(skip_ready, 1)

            def square(ch, p):
                act.wait_ge(y_ready, NP * ch.c + p + 1)
                act.wait_ge(y_used, NP * ch.c + p - 1)
                act.activation(ysq[:, p % 2, :, :], y[:, p % RING, :, :], ACT.Square).then_inc(ysq_ready, 1)

            def inverse_deviation(ch):
                act.wait_ge(var_ready, ch.c + 1)
                act.activation(ln[:, 3, :], ln[:, 2, :], ACT.Ln).then_inc(log_ready, 1)
                act.wait_ge(log_ready, ch.c + 1)
                act.activation(ln[:, 3, :], ln[:, 3, :], ACT.Exp, scale=-0.5).then_inc(rstd_ready, 1)

            def square_result(ch, tt):
                act.wait_ge(z_ready, TT * ch.c + tt + 1)
                if not (ch.fixed and ch.c == END.c):
                    act.wait_ge(z1_out, 32 * (ch.c + 1))
                act.activation(squares(ch)[:, tt, :], xt[:, tt, :], ACT.Square).then_inc(zsq_ready, 1)

            def take_transform(ch, tt):
                act.wait_ge(f1_done, TT * ch.c + tt + 1)
                act.wait_ge(zst_done, TT * ch.c)
                act.activation(side[:, tt, :].rearrange("p (j c) -> p j c", j=2), ps_o[:, tt, :, 0:CH2],
                               ACT.Copy).then_inc(f1_ready, 1)

            def body(ch):
                prev, nxt, far = ch + -1, ch + 1, ch + 2
                if nxt.there:
                    take_xs(nxt, 5)
                if prev.there:
                    square(prev, 5)
                times_d(ch, 0)
                if far.there:
                    norm(far)
                act.preload_act_table_set("natural_log_exp_and_others")
                decay(ch, 1)
                log_part(ch, 2)
                for p in range(1, 4):
                    if far.there:
                        take_xs(far, p - 1)
                    if p == 1 and prev.there:
                        inverse_deviation(prev)
                    square(ch, p - 1)
                    times_d(ch, p)
                    if p == 1 and nxt.there:
                        centre(nxt, SHARED)
                    if p == 2:
                        if nxt.there:
                            centre(nxt, PE_PAIR)
                        if prev.there:
                            for tt in range(TT):
                                take_transform(prev, tt)
                    if far.there:
                        centre(far, p - 1)
                    decay(ch, p + 1)
                    if p == 3 and prev.there:
                        for tt in range(TT):
                            square_result(prev, tt)
                    log_part(ch, p + 2)
                    if (ch + 3).first and p == 2:
                        norm_row((ch + 3).b)
                    if (ch + 3).first and p == 3:
                        for b, part in ROW_PARTS[NP:]:
                            take_row(b, part)
                if far.there:
                    take_xs(far, 3)
                square(ch, 3)
                times_d(ch, 4)
                if nxt.there:
                    silu(nxt)
                decay(ch, 5)
                if nxt.there:
                    take_xd(nxt)
                if far.there:
                    centre(far, 3)
                    take_xs(far, 4)
                if nxt.there:
                    log_part(nxt, 0)
                square(ch, 4)
                times_d(ch, 5)
                if nxt.there:
                    decay(nxt, 0)
                    log_part(nxt, 1)

            one, two = Chunk(1), Chunk(2)
            norm_row(0)
            norm(one)
            for p in range(NP):
                take_row(*ROW_PARTS[p])
                take_xs(one, p)
                if p < SHARED:
                    centre(one, p)
            norm(two)
            for p in (SHARED, PE_PAIR):
                centre(one, p)
            for p in range(2):
                take_xs(two, p)
                centre(two, p)
            silu(one)
            take_xd(one)
            log_part(one, 0)
            act.wait_ge(carry_zero, 1)
            decay(one, 0)
            for p in range(2, NP - 1):
                take_xs(two, p)
                if p < SHARED:
                    centre(two, p)
            log_part(one, 1)
            chunk_loop(act, body)
            square(END, 5)
            inverse_deviation(END)
            for tt in range(TT):
                square_result(END, tt)
            for tt in range(TT):
                take_transform(END, tt)

        @block.vector
        def _(dve):
            def convolve(ch, p):
                dve.wait_ge(centre_done, PE_PAIR * ch.c + p + 1)
                if ch.first:
                    dve.wait_ge(xs_zero, 2 * NP * ch.b + p + 1)
                if ch.last:
                    dve.wait_ge(xs_zero, 2 * NP * ch.b + NP + p + 1)
                base = TAPPED * ch.c + TAP_END[p] - 2 * len(DVE_TAPS[p])
                for n, (dy, dx) in enumerate(DVE_TAPS[p]):
                    for j in range(2):
                        t = 2 * p + j
                        if n:
                            dve.wait_ge(tap_done, base + 2 * n - 1 + j)
                        a, e = max(0, 1 - dx), W - max(0, dx - 1)
                        out = u[:, ch.odd, t, :].rearrange("p (r w) -> p r w", w=W)[:, :, a:e]
                        dve.scalar_tensor_tensor(out, xs[:, t, dy:dy + ROWS, a + dx - 1:e + dx - 1],
                                                 k.conv_w[:, t, 3 * dy + dx:3 * dy + dx + 1], out,
                                                 ALU.mult, ALU.add).then_inc(tap_done, 1)

            def softplus(ch, p):
                n = NP * ch.c + p
                dve.wait_ge(q_ready, n + 1)
                dve.wait_ge(da_ready, n)
                dve.scalar_tensor_tensor(delta[:, :, :].rearrange("p j n -> p (j n)"), ps_d[:, :], 0.0,
                                         q[:, :, :].rearrange("p j n -> p (j n)"), ALU.max, ALU.add).then_inc(delta_ready, 1)

            def times_u(ch, p):
                n = NP * ch.c + p
                dve.wait_ge(delta_ready, n + 1)
                dve.wait_ge(dbu_ready, n)
                dve.tensor_tensor(du[:, :, :], delta[:, :, :], u[:, ch.odd, 2 * p:2 * p + 2, :], ALU.mult).then_inc(du_ready, 1)

            def first_state(ch, p):
                dve.tensor_copy(st[:, :, :, 0], carry[:, 2 * p:2 * p + 2, :])

            def inflow(ch, p):
                n = NP * ch.c + p
                dve.wait_ge(sum_done, n)
                dve.wait_ge(du_ready, n + 1)
                dve.wait_ge(bc_in[0], 16 * (ch.c + 1))
                dve.tensor_tensor(st[:, :, :, 1:T + 1], du[:, :, None, :].to_broadcast([P, 2, NS, T]),
                                  bc[:, 0:1, :, :].to_broadcast([P, 2, NS, T]), ALU.mult).then_inc(dbu_ready, 1)

            def scan(ch, p):
                n = NP * ch.c + p
                dve.wait_ge(da_ready, n + 1)
                dve.wait_ge(dbu_ready, n + 1)
                states = st[:, :, :, :].rearrange("p j n t -> p (j n t)")
                dve.tensor_tensor_scan(states, da[:, :, :, :].rearrange("p j n t -> p (j n t)"), states, 0.0,
                                       ALU.mult, ALU.add).then_inc(scan_done, 1)

            def keep_state(ch, p):
                n = NP * ch.c + p
                dve.wait_ge(scan_done, n + 1)
                dve.tensor_copy(carry[:, 2 * p:2 * p + 2, :], st[:, :, :, T]).then_inc(carry_kept, 1)

            def times_c(ch, p):
                n = NP * ch.c + p
                dve.wait_ge(bc_in[1], 16 * (ch.c + 1))
                dve.wait_ge(carry_kept, n + 1)
                v = st[:, :, :, 1:T + 1]
                dve.tensor_tensor(v, v, bc[:, 1:2, :, :].to_broadcast([P, 2, NS, T]), ALU.mult).then_inc(yc_done, 1)

            def half_sum(ch, p):
                dve.wait_ge(yc_done, NP * ch.c + p + 1)
                dve.tensor_tensor(st[:, :, 0:2, 1:T + 1], st[:, :, 0:2, 1:T + 1], st[:, :, 2:4, 1:T + 1], ALU.add).then_inc(half_done, 1)

            def state_sum(ch, p):
                n = NP * ch.c + p
                dve.wait_ge(half_done, n + 1)
                dve.wait_ge(y_used, n + 1 - RING)
                dve.tensor_tensor(y[:, p % RING, :, :], st[:, :, 0, 1:T + 1], st[:, :, 1, 1:T + 1], ALU.add).then_inc(sum_done, 1)

            def skip(ch, p):
                n = NP * ch.c + p
                dve.wait_ge(sum_done, n + 1)
                dve.wait_ge(skip_ready, n + 1)
                v = y[:, p % RING, :, :]
                dve.tensor_tensor(v, v, u[:, ch.odd, 2 * p:2 * p + 2, :], ALU.add).then_inc(y_ready, 1)

            def layer_norm(ch):
                n = 3 * ch.c
                mean, sq, var = (ln[:, m, :] for m in range(3))
                dve.wait_ge(y_used, NP * ch.c + NP)
                dve.wait_ge(rstd_ready, ch.c)
                dve.tensor_scalar(mean, ps_o[:, :, 0, CH2], 1.0 / DI, None, ALU.mult).then_inc(ln_step, 1)
                dve.wait_ge(ln_step, n + 1)
                dve.tensor_tensor(sq, mean, mean, ALU.mult).then_inc(ln_step, 1)
                dve.wait_ge(ln_step, n + 2)
                dve.scalar_tensor_tensor(var, ps_y[:, 0:TT], 1.0 / DI, sq, ALU.mult, ALU.subtract).then_inc(ln_step, 1)
                dve.wait_ge(ln_step, n + 3)
                dve.tensor_scalar(var, var, 0.0, LN_EPS, ALU.max, ALU.add).then_inc(var_ready, 1)

            def result(ch):
                dve.wait_ge(rstd_ready, ch.c + 1)
                dve.wait_ge(xb_ready, ch.c + 1)
                for tt in range(TT):
                    tile = xt[:, tt, :].rearrange("p (j c) -> p j c", j=2)
                    dve.scalar_tensor_tensor(tile, ps_o[:, tt, :, 0:CH2], ln[:, 3, tt:tt + 1], tile,
                                             ALU.mult, ALU.add).then_inc(z_ready, 1)

            def keep_sums(ch):
                dve.wait_ge(zst_done, TT * ch.c + TT)
                dve.wait_ge(zst_kept, ch.c)
                dve.tensor_tensor(k.sums[:, ch.b, :], k.sums[:, ch.b, :], ps_x[:, 0:KT], ALU.add).then_inc(zst_kept, 1)

            def body(ch):
                prev, nxt, far = ch + -1, ch + 1, ch + 2
                for p in range(NP):
                    after, q_ = (ch, p + 1) if p + 1 < NP else (nxt, 0)
                    conv, r = (nxt, p + 2) if p + 2 < NP else (far, p + 2 - NP)
                    scan(ch, p)
                    if after.there:
                        softplus(after, q_)
                    keep_state(ch, p)
                    times_c(ch, p)
                    if after.there:
                        times_u(after, q_)
                    half_sum(ch, p)
                    if p == NP - 1 and ch.last and after.there:
                        dve.wait_ge(carry_kept, NP * ch.c + NP)
                        dve.memset(carry[:, :, :], 0.0).then_inc(carry_zero, 1)
                        dve.wait_ge(carry_zero, 2 + ch.b)
                    if after.there:
                        first_state(after, q_)
                    state_sum(ch, p)
                    if after.there:
                        inflow(after, q_)
                    skip(ch, p)
                    if p == 1 and prev.there:
                        result(prev)
                    if conv.there and r < PE_PAIR:
                        convolve(conv, r)
                    if p == 0 and prev.there:
                        layer_norm(prev)
                    if p == NP - 1 and prev.there:
                        keep_sums(prev)

            one, two = Chunk(1), Chunk(2)
            dve.memset(da[:, :, :, 0], 0.0)
            dve.memset(k.sums[:, :, :], 0.0)
            dve.memset(carry[:, :, :], 0.0).then_inc(carry_zero, 1)
            dve.wait_ge(carry_zero, 1)
            for p in range(PE_PAIR):
                convolve(one, p)
            for p in range(2):
                convolve(two, p)
            softplus(one, 0)
            times_u(one, 0)
            first_state(one, 0)
            inflow(one, 0)
            chunk_loop(dve, body)
            layer_norm(END)
            result(END)
            keep_sums(END)

        @block.gpsimd
        def _(pool):
            for s, n in per_chunk:
                pool.sem_inc(s, n)

            def edge(ch):
                for p in range(NP):
                    if ch.first:
                        if p == PE_PAIR:
                            pool.wait_ge(conv_done, 2 * ch.c)
                        else:
                            pool.wait_ge(tap_done, TAPPED * (ch.c - 1) + TAP_END[p])
                        pool.memset(xs[:, 2 * p:2 * p + 2, 0, :], 0.0).then_inc(xs_zero, 1)
                    if ch.last:
                        pool.wait_ge(xs_moved, NP * ch.c + p + 1)
                        pool.memset(xs[:, 2 * p:2 * p + 2, ROWS + 1, :], 0.0).then_inc(xs_zero, 1)

            def body(ch):
                if (ch + 2).there:
                    edge(ch + 2)
                pool.wait_ge(xt_in, 16 * (ch.c + 1))
                for tt in range(TT):
                    last = pool.tensor_tensor(xt[:, tt, :], xt[:, tt, :], k.bv[:, :], ALU.add)
                last.then_inc(xb_ready, 1)

            edge(Chunk(1))
            chunk_loop(pool, body)


def mlp_stage(nc, d, k):
    with ExitStack() as ctx:
        def sb(name, shape):
            return ctx.enter_context(nc.sbuf_tensor(name, shape, F32))

        def pb(name, shape):
            return ctx.enter_context(nc.psum_tensor(name, shape, F32))

        def sem(name):
            return ctx.enter_context(nc.semaphore(name))

        PAD = 16
        NPOS = KW * H
        QC = C // 4
        UNITS = 16
        zt = sb("zt", [P, 2, KW, C + PAD])
        zt0 = sb("zt0", [P, C + PAD])
        w1 = sb("mlp_w1", [P, BP, HM * P])
        w2 = sb("mlp_w2", [P, BP, HM, 2 * PC])
        b1 = sb("mlp_b1", [P, BP, HM])
        b2 = sb("mlp_b2", [P, BP, 2 * PC])
        f_h = sb("f_h", [P, 3, 2, H])
        i_h = sb("i_h", [P, P])
        spec = sb("spec", [P, 2, NPOS])
        hid = sb("hid", [P, 2, HM, NPOS])
        val = sb("val", [P, 2, KW // 2, 2 * PC])
        clip = sb("clip", [P, 2, KW // 2, 2 * PC])
        shr = sb("shr", [P, KW // 2, 2, C])
        inv = sb("inv", [P, KW, C])
        cols = sb("cols", [P, KW, C])
        member = sb("member", [P, KT, NG])
        ones = sb("mlp_ones", [H, P])
        gm = sb("gm", [P, NB, NG])
        gv = sb("gv", [P, NB, NG])
        gt = sb("gt", [P, NB, NG])
        pick = sb("pick", [P, NB, BP])
        scale = sb("scale", [P, NB, BP])
        shift = sb("shift", [P, NB, BP])
        now = sb("now", [P, 2, BP])

        ps_f = pb("ps_f", [P, 2, 512])
        ps_h = pb("ps_h", [P, HM, 512])
        ps_v = pb("ps_v", [P, 2, 512])
        ps_c = pb("ps_c", [P, 512])

        w_in = [sem(f"mlp_w_in{quarter}") for quarter in range(4)]
        b_in, table_in, z0_in = sem("mlp_b_in"), sem("table_in"), sem("z0_in")
        z_in = [sem(f"z_in{n}") for n in range(2)]
        chain, ones_ok, zero_in, stats_ok, sign_ok, pad_ok, flipped = sem("m_chain"), sem("ones_ok"), sem("zero_in"), sem("stats_ok"), sem("sign_ok"), sem("pad_ok"), sem("flipped")
        var_ok, log_ok, root_ok = sem("m_var_ok"), sem("m_log_ok"), sem("m_root_ok")
        f_done, spec_ready, dc_done = sem("f_done"), sem("spec_ready"), sem("dc_done")
        h_done, hid_act, hid_dve = sem("h_done"), sem("hid_act"), sem("hid_dve")
        v_done, val_ready, clip_ready, shr_ready = sem("v_done"), sem("val_ready"), sem("clip_ready"), sem("shr_ready")
        inv_in = [sem(f"inv_in{quarter}") for quarter in range(4)]
        c_done, cols_ready = sem("c_done"), sem("cols_ready")
        z2_out = [sem(f"z2_out{quarter}") for quarter in range(4)]
        res_in = [sem(f"res_in{quarter}") for quarter in range(4)]
        now_ok = sem("now_ok")
        turn = sem("m_turn")
        per_step = [(f_done, BP), (spec_ready, BP), (h_done, HM * BP), (hid_act, 2 * BP), (hid_dve, BP), (v_done, BP),
                    (val_ready, BP), (clip_ready, BP), (shr_ready, BP), (c_done, UNITS),
                    (cols_ready, UNITS)] + [(s, 64) for s in inv_in] + [(s, 32) for s in z2_out] + [(s, 16) for s in res_in]
        block = ctx.enter_context(nc.Block())

        z1_tiles = d.z1.rearrange("b (t r) h c -> b t (r h) c", r=2)
        z2_cols = d.z2.rearrange("b h (t r) c -> b r h t c", r=2)
        PER = NST + 1

        def images(engine, step, end=None):
            with engine.Fori(0, NB) as b:
                for t in range(PER):
                    step(b, PER * b + t, t)
                if end:
                    end(b, PER * b + NST)

        def width_of(t):
            return KW if t < NST else 2

        def place(unit, t):
            per = width_of(t) // 2
            return unit // per, unit % per, UNITS // (4 * per)

        @block.sync
        def _(sp):
            def hold(sem_, value):
                sp.wait_ge(sem_, value)
                sp.sem_inc(turn, 1)

            for b in range(NB):
                sp.dma_start(inv[0:H, b, :], d.z1[b, 0]).then_inc(zero_in, 16)
            sp.dma_start(member[:, :, :], d.member).then_inc(table_in, 16)
            sp.dma_start(f_h[:, :, :, :], d.f_h).then_inc(table_in, 16)
            sp.dma_start(i_h[:, :], d.i_h).then_inc(table_in, 16)

            def load(b, t):
                sp.dma_start(zt[:, t % 2, :, 0:C], z1_tiles[b, t * KW:(t + 1) * KW].rearrange("t p c -> p t c")
                             ).then_inc(z_in[t % 2], 16)

            def store(b, n, t, quarter):
                part = slice(quarter * QC, (quarter + 1) * QC)
                hold(cols_ready, UNITS * (n + 2) + UNITS // 4 * (quarter + 1))
                if t < NST:
                    for r in range(2):
                        sp.dma_start(z2_cols[b, r, :, t * KW:(t + 1) * KW, part],
                                     cols[r * H:(r + 1) * H, :, part]).then_inc(z2_out[quarter], 16)
                else:
                    hold(z2_out[quarter], 32 * (n + 2))
                    sp.dma_start(d.z2[b, :, 0:2, part], cols[0:H, 0:2, part]).then_inc(z2_out[quarter], 32)

            def residual(b, n, t, quarter):
                part = slice(quarter * QC, (quarter + 1) * QC)
                hold(z2_out[quarter], 32 * (n + 2))
                if t < NST:
                    sp.dma_start(cols[:, :, part], z1_tiles[b, t * KW:(t + 1) * KW, :, part].rearrange("t p c -> p t c")
                                 ).then_inc(res_in[quarter], 16)
                else:
                    sp.dma_start(cols[0:H, 0:2, part], d.z1[b, 0:2, :, part].rearrange("q h c -> h q c")
                                 ).then_inc(res_in[quarter], 16)

            def step(b, n, t):
                m = width_of(t)
                if t == 0:
                    hold(f_done, BP * (n + 2))
                    load(b, 0)
                    sp.dma_start(zt0[:, 0:C], z1_tiles[b, 0]).then_inc(z0_in, 16)
                    for some in w_in:
                        sp.wait_ge(some, 32)
                    load(b, 1)
                for quarter in range(4):
                    if quarter:
                        residual(b, n, t, quarter - 1)
                    if t:
                        store(b, n - 1, t - 1, quarter)
                    hold(c_done, UNITS * (n + 1) + UNITS // 4 * (quarter + 1))
                    hold(shr_ready, BP * (n + 2) + 4 * quarter + 4)
                    part = slice(quarter * QC, (quarter + 1) * QC)
                    for f in range(2):
                        for r in range(2):
                            sp.dma_start(inv[r * H:(r + 1) * H, f:m:2, part],
                                         shr[f * H:(f + 1) * H, 0:m // 2, r, part]).then_inc(inv_in[quarter], 16)
                residual(b, n, t, 3)
                if t + 2 < NST:
                    hold(f_done, BP * (n + 3))
                    load(b, t + 2)

            def end(b, n):
                for quarter in range(4):
                    store(b, n, NST, quarter)

            images(sp, step, end)
            for quarter in range(4):
                sp.wait_ge(z2_out[quarter], 32 * (NB * PER + 2))

        @block.gpsimd
        def _(pool):
            for s, n in per_step:
                pool.sem_inc(s, 2 * n)
            pool.memset(zt[:, :, :, C:C + PAD], 0.0)
            pool.memset(zt0[:, C:C + PAD], 0.0).then_inc(pad_ok, 1)
            pool.wait_ge(pad_ok, 1)
            for quarter in range(4):
                some = slice(4 * quarter, 4 * quarter + 4)
                pool.wait_ge(w_in[quarter], 32)
                im_re = w1[H:P, some, :].rearrange("p a (e r m) -> p (a e) r m", e=2, r=2)[:, :, 0, :]
                parts = [im_re] + [w2[p0:p1, some, t, 0:PC] for p0, p1, t in ((96, 128, 0), (0, 64, 1), (32, 64, 2), (64, 128, 2))]
                for n, part in enumerate(parts):
                    pool.tensor_scalar(part, part, -1.0, None, ALU.mult).then_inc(flipped, 1)
                    pool.wait_ge(flipped, len(parts) * quarter + n + 1)
                pool.sem_inc(sign_ok, 1)

        @block.tensor
        def _(pe):
            pe.wait_ge(table_in, 16 * 3)
            for b in range(NB):
                for t in range(KT):
                    pe.matmul(ps_c[:, b * NG:(b + 1) * NG], k.sums[:, b, t:t + 1].to_broadcast([P, P]),
                              member[:, t, :], start=(t == 0), stop=(t == KT - 1))
            pe.wait_ge(ones_ok, 1)
            pe.wait_ge(zero_in, 16 * NB)
            for b in range(NB):
                for j in range(2):
                    last = pe.matmul((ps_h, ps_v)[b][:, j, 0:CH2], ones[:, :], inv[0:H, b, j * CH2:(j + 1) * CH2],
                                     start=True, stop=True)
            last.then_inc(stats_ok, 1)
            pe.wait_ge(pad_ok, 1)

            def transform(n, a, buf, width):
                pe.wait_ge(spec_ready, BP * (n + 2) + max(a - 1, 0))
                for j in range(width):
                    cut = slice(a * PC, a * PC + PC + PAD)
                    lhs, f = (zt0[:, cut], 1 + j) if buf is None else (zt[:, buf, j, cut], 0)
                    for r in range(2):
                        last = pe.matmul(ps_f[r * H:(r + 1) * H, a % 2, j * H:(j + 1) * H], lhs, f_h[:, f, r, :],
                                         start=True, stop=True)
                last.then_inc(f_done, 1)

            def hidden(b, n, a, buf, width):
                pe.wait_ge(spec_ready, BP * (n + 2) + a + 1)
                if buf is None:
                    pe.wait_ge(dc_done, BP * b + (a + 1))
                pe.wait_ge(hid_act, 2 * (BP * (n + 2) + a))
                pe.wait_ge(hid_dve, BP * (n + 2) + a)
                for t in range(HM):
                    pe.matmul(ps_h[:, t, 0:width * H], w1[:, a, t * P:(t + 1) * P], spec[:, a % 2, 0:width * H],
                              start=True, stop=True).then_inc(h_done, 1)

            def second(n, a, width):
                pe.wait_ge(hid_act, 2 * (BP * (n + 2) + a + 1))
                pe.wait_ge(hid_dve, BP * (n + 2) + a + 1)
                pe.wait_ge(val_ready, BP * (n + 2) + max(a - 1, 0))
                for f in range(width // 2):
                    for t in (1, 0, 2):
                        out, w = ps_v[:, a % 2, f * 2 * PC:(f + 1) * 2 * PC], w2[:, a, t, :]
                        if t != 1:
                            out, w = (v.rearrange("p (r e c) -> p e r c", r=2, e=2)[:, t // 2] for v in (out, w))
                        last = pe.matmul(out, hid[:, a % 2, t, f * P:(f + 1) * P], w,
                                         start=(t == 1), stop=(t != 1), skip_group_check=True)
                last.then_inc(v_done, 1)

            def inverse(n, unit, t):
                quarter, f, share = place(unit, t)
                pe.wait_ge(inv_in[quarter], 64 * (n + 3))
                pe.wait_ge(cols_ready, UNITS * (n + 2) + share * unit)
                pe.matmul(ps_c[:, 0:2 * QC], i_h[:, :], inv[:, 2 * f:2 * f + 2, quarter * QC:(quarter + 1) * QC],
                          start=True, stop=True).then_inc(c_done, share)

            def step(b, n, t):
                width = width_of(t)
                buf = t % 2 if t < NST else None
                if buf is None:
                    pe.wait_ge(z0_in, 16 * (b + 1))
                else:
                    pe.wait_ge(z_in[buf], 16 * (NST // 2 * b + (t // 2 + 1)))
                transform(n, 0, buf, width)
                for a in range(BP):
                    if a + 1 < BP:
                        transform(n, a + 1, buf, width)
                    if t == 0 and a % 4 == 0:
                        pe.wait_ge(sign_ok, a // 4 + 1)
                    hidden(b, n, a, buf, width)
                    if a:
                        second(n, a - 1, width)
                    if t:
                        inverse(n - 1, a, t - 1)
                second(n, BP - 1, width)

            def end(b, n):
                for unit in range(4):
                    inverse(n, unit, NST)

            images(pe, step, end)

        @block.scalar
        def _(act):
            def relu(n, a, width):
                act.wait_ge(v_done, BP * (n + 2) + max(a - 1, 0))
                for t in range(2):
                    act.wait_ge(h_done, HM * (BP * (n + 2) + a) + t + 1)
                    act.activation(hid[:, a % 2, t, 0:width * H], ps_h[:, t, 0:width * H], ACT.Relu,
                                   bias=b1[:, a, t:t + 1]).then_inc(hid_act, 1)

            def step(b, n, t):
                for a in range(BP):
                    relu(n, a, width_of(t))

            act.wait_ge(zero_in, 16 * NB)
            act.dma_start(b1[:, :, :], d.mlp_b1).then_inc(b_in, 16)
            act.dma_start(b2[:, :, :].rearrange("p a c -> p (a c)"), d.mlp_b2.to_broadcast([P, BP * 2 * PC])).then_inc(b_in, 16)
            for quarter in range(4):
                some = slice(4 * quarter, 4 * quarter + 4)
                act.dma_start(w1[:, some, :], d.mlp_w1[:, some, :]).then_inc(w_in[quarter], 16)
                act.dma_start(w2[:, some, :, :], d.mlp_w2[:, some, :, :]).then_inc(w_in[quarter], 16)
            act.wait_ge(var_ok, 1)
            act.preload_act_table_set("natural_log_exp_and_others")
            act.activation(gt[:, :, :], gt[:, :, :], ACT.Ln).then_inc(log_ok, 1)
            act.wait_ge(log_ok, 1)
            act.activation(gv[:, :, :], gt[:, :, :], ACT.Exp, scale=-0.5).then_inc(root_ok, 1)
            act.wait_ge(b_in, 16 * 2)
            images(act, step)

        @block.vector
        def _(dve):
            links = [0]

            def link(ins):
                links[0] += 1
                ins.then_inc(chain, 1)
                dve.wait_ge(chain, links[0])

            dve.memset(ones[:, :], 1.0).then_inc(ones_ok, 1)
            dve.wait_ge(stats_ok, 1)
            squares = ps_c[:, 0:NB * NG].rearrange("p (b g) -> p b g", b=NB)
            for b in range(NB):
                for j in range(2):
                    per_channel = (ps_h, ps_v)[b][:, j, 0:CH2].rearrange("p (g c) -> p g c", c=GC)
                    last = dve.tensor_reduce(gm[:, b, j * BP:(j + 1) * BP], per_channel, AX.X, ALU.add)
            link(last)
            link(dve.tensor_scalar(gm[:, :, :], gm[:, :, :], float(np.sqrt(W)) / (GC * L), None, ALU.mult))
            link(dve.tensor_tensor(gt[:, :, :], gm[:, :, :], gm[:, :, :], ALU.mult))
            for b in range(NB):
                last = dve.scalar_tensor_tensor(gv[:, b, :], squares[:, b, :], 1.0 / (GC * L), gt[:, b, :],
                                                ALU.mult, ALU.subtract)
            link(last)
            dve.tensor_scalar(gt[:, :, :], gv[:, :, :], 0.0, GN_EPS, ALU.max, ALU.add).then_inc(var_ok, 1)
            dve.wait_ge(root_ok, 1)
            for b in range(NB):
                last = dve.scalar_tensor_tensor(gm[:, b, :], gm[:, b, :], -float(H), gv[:, b, :], ALU.mult, ALU.mult)
            link(last)
            for table, out in ((gv, scale), (gm, shift)):
                pairs = table[:, :, :].rearrange("p b (a e) -> p b a e", e=2)
                link(dve.tensor_scalar(pick[:, :, :], pairs[:, :, :, 0], k.mask[:, 0:1], None, ALU.mult))
                for b in range(NB):
                    last = dve.scalar_tensor_tensor(out[:, b, :], pairs[:, b, :, 1], k.mask[:, 1:2], pick[:, b, :],
                                                    ALU.mult, ALU.add)
                link(last)
            dve.wait_ge(b_in, 16 * 2)

            def take_spec(n, a, buf, width):
                dve.wait_ge(f_done, BP * (n + 2) + a + 1)
                dve.wait_ge(h_done, HM * (BP * (n + 2) + max(a - 1, 0)))
                dve.tensor_scalar(spec[:, a % 2, 0:width * H], ps_f[:, a % 2, 0:width * H], now[:, 0, a:a + 1], None,
                                  ALU.mult).then_inc(spec_ready, 1)
                if buf is None:
                    dve.wait_ge(spec_ready, BP * (n + 2) + a + 1)
                    dve.tensor_scalar(spec[0:H, a % 2, 0:1], spec[0:H, a % 2, 0:1], now[0:H, 1, a:a + 1], None,
                                      ALU.add).then_inc(dc_done, 1)

            def relu(n, a, width):
                t = HM - 1
                dve.wait_ge(v_done, BP * (n + 2) + max(a - 1, 0))
                dve.wait_ge(h_done, HM * (BP * (n + 2) + a + 1))
                dve.tensor_scalar(hid[:, a % 2, t, 0:width * H], ps_h[:, t, 0:width * H], b1[:, a, t:t + 1], 0.0,
                                  ALU.add, ALU.max).then_inc(hid_dve, 1)

            def shrink(n, a, width):
                m = width // 2
                v, cl = val[:, a % 2, 0:m, :], clip[:, a % 2, 0:m, :]
                dve.wait_ge(v_done, BP * (n + 2) + a + 1)
                dve.wait_ge(shr_ready, BP * (n + 2) + max(a - 1, 0))
                dve.tensor_tensor(v, ps_v[:, a % 2, 0:m * 2 * PC].rearrange("p (f c) -> p f c", f=m),
                                  b2[:, a:a + 1, :].to_broadcast([P, m, 2 * PC]), ALU.add).then_inc(val_ready, 1)
                dve.wait_ge(val_ready, BP * (n + 2) + a + 1)
                dve.tensor_scalar(cl, v, -SHRINK, SHRINK, ALU.max, ALU.min).then_inc(clip_ready, 1)
                dve.wait_ge(clip_ready, BP * (n + 2) + a + 1)
                if a % 4 == 0:
                    dve.wait_ge(inv_in[a // 4], 64 * (n + 2))
                dve.tensor_tensor(shr[:, 0:m, :, a * PC:(a + 1) * PC], v.rearrange("p f (r c) -> p f r c", r=2),
                                  cl.rearrange("p f (r c) -> p f r c", r=2), ALU.subtract).then_inc(shr_ready, 1)

            def add_cols(n, unit, t):
                quarter, f, share = place(unit, t)
                rows = P if t < NST else H
                if unit % (UNITS // share // 4) == 0:
                    dve.wait_ge(res_in[quarter], 16 * (n + 3))
                dve.wait_ge(c_done, UNITS * (n + 2) + share * (unit + 1))
                v = cols[0:rows, 2 * f:2 * f + 2, quarter * QC:(quarter + 1) * QC]
                dve.tensor_tensor(v, v, ps_c[0:rows, 0:2 * QC].rearrange("p (f c) -> p f c", f=2),
                                  ALU.add).then_inc(cols_ready, share)

            def step(b, n, t):
                width = width_of(t)
                buf = t % 2 if t < NST else None
                if t == 0:
                    dve.tensor_copy(now[:, 0, :], scale[:, b, :])
                    dve.tensor_copy(now[:, 1, :], shift[:, b, :]).then_inc(now_ok, 1)
                    dve.wait_ge(now_ok, b + 1)
                take_spec(n, 0, buf, width)
                for a in range(BP):
                    if a + 1 < BP:
                        take_spec(n, a + 1, buf, width)
                    relu(n, a, width)
                    if a:
                        shrink(n, a - 1, width)
                    if t:
                        add_cols(n - 1, a, t - 1)
                shrink(n, BP - 1, width)

            def end(b, n):
                for unit in range(4):
                    add_cols(n, unit, NST)

            images(dve, step, end)


def last_stage(nc, d, k):
    with ExitStack() as ctx:
        def sb(name, shape):
            return ctx.enter_context(nc.sbuf_tensor(name, shape, F32))

        def sem(name):
            return ctx.enter_context(nc.semaphore(name))

        U = 2
        E = 4
        N = NB * L // (U * P)
        z = sb("last_z", [P, E, U, C])
        o = sb("last_o", [P, E, U, C])
        i_w = sb("i_w", [P, P])
        ps = ctx.enter_context(nc.psum_tensor("ps_last", [P, 2, U, 2, 512], F32))
        m_in = sem("i_w_in")
        z_in = [sem(f"last_z_in{e}") for e in range(E)]
        o_out = [sem(f"last_o_out{e}") for e in range(E)]
        back, taken = sem("last_back"), [sem(f"last_taken{t}") for t in range(U)]
        turn = sem("last_turn")
        block = ctx.enter_context(nc.Block())
        zs = d.z2.rearrange("b h q c -> (b h q) c").rearrange("(g t p) c -> g p t c", t=U, p=P)
        out = d.out.rearrange("(g t p) c -> g p t c", t=U, p=P)

        @block.gpsimd
        def _(pool):
            pool.sem_inc(back, U * E)
            for s in taken:
                pool.sem_inc(s, E)
            for s in o_out:
                pool.sem_inc(s, 16)

        @block.sync
        def _(sp):
            sp.dma_start(i_w[:, :], d.i_w).then_inc(m_in, 16)
            with sp.Fori(0, N // E) as i:
                for e in range(E):
                    m = E * i + e
                    sp.wait_ge(back, U * (m + 1))
                    sp.sem_inc(turn, 1)
                    sp.dma_start(z[:, e, :, :], zs[m]).then_inc(z_in[e], 16)

        @block.tensor
        def _(pe):
            pe.wait_ge(m_in, 16)
            with pe.Fori(0, N // E) as i:
                for e in range(E):
                    m = E * i + e
                    pe.wait_ge(z_in[e], 16 * (i + 1))
                    for t in range(U):
                        pe.wait_ge(taken[t], m + E - 1)
                        for j in range(2):
                            last = pe.matmul(ps[:, e % 2, t, j, 0:CH2], i_w[:, :], z[:, e, t, j * CH2:(j + 1) * CH2],
                                             start=True, stop=True)
                        last.then_inc(back, 1)

        @block.vector
        def _(dve):
            with dve.Fori(0, N // E) as i:
                for e in range(E):
                    m = E * i + e
                    dve.wait_ge(o_out[e], 16 * (i + 1))
                    dve.wait_ge(back, U * (m + E) + 1)
                    dve.tensor_copy(o[:, e, 0, :].rearrange("p (j c) -> p j c", j=2), ps[:, e % 2, 0, :, 0:CH2]).then_inc(taken[0], 1)

        @block.scalar
        def _(act):
            with act.Fori(0, N // E) as i:
                for e in range(E):
                    m = E * i + e
                    act.wait_ge(o_out[e], 16 * (i + 1))
                    act.wait_ge(back, U * (m + E) + 2)
                    act.activation(o[:, e, 1, :].rearrange("p (j c) -> p j c", j=2), ps[:, e % 2, 1, :, 0:CH2],
                                   ACT.Copy).then_inc(taken[1], 1)
                    for s in taken:
                        act.wait_ge(s, m + E + 1)
                    act.dma_start(out[m], o[:, e, :, :]).then_inc(o_out[e], 16)
            for s in o_out:
                act.wait_ge(s, 16 * (N // E + 1))


def build(nc, d):
    with ExitStack() as kept:
        k = Bufs()

        def keep(ctx, name, shape):
            return ctx.enter_context(nc.sbuf_tensor(name, shape, F32))

        k.sums = keep(kept, "sums", [P, NB, KT])
        k.mask = keep(kept, "mask", [P, 2])
        with ExitStack() as first:
            k.w_in = keep(first, "w_in", [P, KT, DI])
            k.w_out = keep(first, "w_out", [P, DT, C + 1])
            k.one = keep(first, "one", [P, 1])
            k.w_x = keep(first, "w_x", [P, DT, XR])
            k.w_dt = keep(first, "w_dt", [ONE + 1, DI])
            k.conv_w = keep(first, "conv_w", [P, DT, 9])
            k.conv_b = keep(first, "conv_b", [P, DT])
            k.conv_diag = keep(first, "conv_diag", [P, len(DIAGS), P])
            k.d_par = keep(first, "d_par", [P, DT])
            k.a_neg = keep(first, "a_neg", [P, DT * NS])
            k.gn_scale = keep(first, "gn_scale", [P, KT, NB])
            k.gn_shift = keep(first, "gn_shift", [P, KT, NB])
            k.bv = keep(first, "bv", [P, C])
            k.f_w = keep(first, "f_w", [P, P])
            k.xd = keep(first, "xd", [ONE + 1, T])
            setup_stage(nc, d, k)
            scan_stage(nc, d, k)
        mlp_stage(nc, d, k)
        last_stage(nc, d, k)


def constants():
    n = np.arange(H)
    angle = 2 * np.pi * np.outer(n, n) / H
    cos, sin = np.cos(angle), np.sin(angle)
    norm = 1 / np.sqrt(H)
    f = np.zeros((W, W))
    f[:, 0], f[:, 1] = 1, cos[:, W // 2]
    f[:, 2::2], f[:, 3::2] = cos[:, 1:W // 2], -sin[:, 1:W // 2]
    i = 2 * f.T
    i[0:2] /= 2
    two = np.eye(2)
    zero = np.zeros((H, H))
    f_h = np.stack([
        np.stack([np.vstack([cos, sin]), np.vstack([-sin, cos])], 1),
        np.stack([np.vstack([cos, zero]), np.vstack([-sin, zero])], 1),
        np.stack([np.vstack([zero, cos]), np.vstack([zero, -sin])], 1),
    ], 1)
    i_h = np.block([[cos, sin], [-sin, cos]])
    group = np.zeros((C, C))
    for g in range(NG):
        group[g * GC:(g + 1) * GC, g * GC:(g + 1) * GC] = 1 / GC
    member = np.repeat(np.eye(NG), GC, axis=0)
    first = (np.arange(P) % H < GC).astype(np.float64)
    tables = dict(
        f_w=np.kron(two, f) * norm, i_w=np.kron(two, i) * norm, f_h=f_h * norm, i_h=i_h * norm,
        group=group.reshape(KT, P, C).transpose(1, 0, 2), member=member.reshape(KT, P, NG).transpose(1, 0, 2),
        mask=np.stack([first, 1 - first], 1), ident=np.eye(P),
        zeros=np.zeros((ONE - RANK, DI)),
    )
    return {name: np.ascontiguousarray(a, dtype=np.float32) for name, a in tables.items()}


def layouts(x, L0_conv_in_proj_w, L0_conv_conv_w, L0_conv_conv_b, L0_conv_x_proj_w, L0_conv_dt_w, L0_conv_dt_b,
            L0_conv_A_log, L0_conv_D_param, L0_conv_ln_g, L0_conv_ln_b, L0_conv_out_proj_w, L1_conv_w1, L1_conv_b1,
            L1_conv_w2, L1_conv_b2):
    x = np.asarray(x)
    f32 = np.float32
    padded = np.zeros((NB, C, L + W), f32)
    padded[:, :, 0:L] = x.reshape(NB, C, L)

    def by_tile(a):
        a = np.asarray(a)
        return a.reshape(DT, P, -1).transpose(1, 0, 2)

    w1, b1 = np.asarray(L1_conv_w1), np.asarray(L1_conv_b1)
    w2, b2 = np.asarray(L1_conv_w2), np.asarray(L1_conv_b2)
    m1 = np.zeros((BP, P, 2, 2, HID), f32)
    m2 = np.zeros((BP, 2, 2, HID, 2, 2, GC), f32)
    v1 = np.zeros((BP, 2, 2, HID), f32)
    v2 = np.zeros((BP, 2, 2, GC), f32)
    for a in range(BP):
        for e in range(2):
            g = 2 * a + e
            for r in range(2):
                m1[a, e * GC:(e + 1) * GC, e, r] = w1[0, g]
                m1[a, H + e * GC:H + (e + 1) * GC, e, r] = w1[1, g]
                m2[a, e, 0, :, r, e] = w2[0, g]
                m2[a, e, 1, :, r, e] = w2[1, g]
                v1[a, e, r] = b1[r, g]
                v2[a, r, e] = b2[r, g]
    return dict(
        x=padded, x_tok=x.transpose(0, 2, 3, 1).reshape(NB * L, C),
        w_in=np.asarray(L0_conv_in_proj_w).T, w_out=np.asarray(L0_conv_out_proj_w).T,
        w_x=np.asarray(L0_conv_x_proj_w).T, w_dt=np.asarray(L0_conv_dt_w)[0].T, dt_b=np.asarray(L0_conv_dt_b),
        conv_w=by_tile(np.asarray(L0_conv_conv_w).reshape(DI, 9)), conv_b=by_tile(L0_conv_conv_b)[:, :, 0],
        d_par=by_tile(L0_conv_D_param)[:, :, 0], a_log=by_tile(L0_conv_A_log).reshape(P, DT * NS),
        ln_g=by_tile(L0_conv_ln_g)[:, :, 0], ln_b=by_tile(L0_conv_ln_b)[:, :, 0],
        mlp_w1=m1.reshape(BP, P, HM * P).transpose(1, 0, 2),
        mlp_w2=m2.reshape(BP, HM, P, 2 * PC).transpose(2, 0, 1, 3),
        mlp_b1=v1.reshape(BP, HM, P).transpose(2, 0, 1), mlp_b2=v2.reshape(1, BP * 2 * PC),
    )


def kernel(**inputs):
    import concourse.bacc as bacc
    from concourse.bass_utils import run_bass_kernel_spmd

    nc = bacc.Bacc("TRN2", target_bir_lowering=False, num_devices=1)
    d = Bufs()
    arrays = {}
    for name, a in {**layouts(**inputs), **constants()}.items():
        arrays[f"in_{name}"] = np.ascontiguousarray(a)
        ap = nc.dram_tensor(f"in_{name}", a.shape, F32, kind="ExternalInput").ap()
        d.__dict__[name] = ap
    d.bc = nc.dram_tensor("bc_rows", (1, 2 * NS * T), F32, kind="Internal").ap()
    d.z1 = nc.dram_tensor("z1", (NB, W, H, C), F32, kind="Internal").ap()
    d.z2 = nc.dram_tensor("z2", (NB, H, W, C), F32, kind="Internal").ap()
    d.out = nc.dram_tensor("out_tok", (NB * L, C), F32, kind="ExternalOutput").ap()
    build(nc, d)
    r = run_bass_kernel_spmd(nc, [arrays], core_ids=[0])
    return r.results[0]["out_tok"].reshape(NB, H, W, C).transpose(0, 3, 1, 2)
```
